# Optimizing a Trainium2 kernel written in Bass

```python
import numpy as np
import jax
import jax.numpy as jnp

def _softmax(x, axis=-1):
    return jax.nn.softmax(x, axis=axis)

def _gelu(x):
    return jax.nn.gelu(x, approximate=True)

def _silu(x):
    return jax.nn.silu(x)

def _sigmoid(x):
    return jax.nn.sigmoid(x)

def _layernorm(x, axis=-1, eps=1e-05):
    m = jnp.mean(x, axis=axis, keepdims=True)
    v = jnp.var(x, axis=axis, keepdims=True)
    return (x - m) / jnp.sqrt(v + eps)

def _scatter_add(tgt, idx, src, axis=0):
    return tgt.at[idx].add(src)

def _segment_sum(src, seg, n):
    return jax.ops.segment_sum(src, seg, n)
kernel_name = 'mk_gps_d1_gnn_r16_fffda1'

def setup_inputs(seed: int=0):
    np.random.seed(seed)
    _w = jnp.asarray

    def _rec_inputs():
        import jax
        import jax.numpy as jnp
        _gk = jax.random.key(seed)
        x = -0.0006008 + 1.001 * jax.random.normal(jax.random.fold_in(_gk, 1), (3125, 256), jnp.float32)
        _s = jax.random.randint(jax.random.fold_in(_gk, 2), (25000,), 0, 3125, jnp.int32)
        _d = jax.random.randint(jax.random.fold_in(_gk, 3), (25000,), 0, 3125, jnp.int32)
        _loop = jnp.arange(3125, dtype=jnp.int32)
        src = jnp.concatenate([_s, _d, _loop])
        dst = jnp.concatenate([_d, _s, _loop])
        _o = jnp.argsort(dst, stable=True)
        src = src[_o]
        dst = dst[_o]
        edge_type_16 = jax.random.randint(jax.random.fold_in(_gk, 12), (53125,), 0, 16, jnp.int32)
        return (x, src, dst, edge_type_16)
    x, src, dst, edge_type_16 = _rec_inputs()

    def _L0_gnn_setup():
        import jax, jax.numpy as jnp
        import numpy as np
        from jax.ops import segment_sum
        N_NODES = 625
        N_EDGES = 10000
        IN_FEAT = 256
        OUT_FEAT = 256
        NUM_RELS = 16

        def _inv_degree(idx, n):
            deg = segment_sum(jnp.ones(idx.shape[0], dtype=jnp.float32), idx, num_segments=n)
            return jnp.where(deg > 0, 1.0 / deg, 0.0)

        def _typed_pass(feat, W, bias, src_idx, dst_idx, etypes, norm_per_edge, n):
            proj = jnp.einsum('ni,rio->rno', feat, W)
            m = proj[etypes, src_idx] + bias
            m = m * norm_per_edge[:, None]
            return segment_sum(m, dst_idx, num_segments=n)
        key = jax.random.key(seed)
        ks = jax.random.split(key, 8)
        feat = jax.random.normal(ks[0], (N_NODES, IN_FEAT), dtype=jnp.float32)
        Wf = jax.random.normal(ks[1], (NUM_RELS, IN_FEAT, OUT_FEAT), dtype=jnp.float32)
        Wb = jax.random.normal(ks[2], (NUM_RELS, IN_FEAT, OUT_FEAT), dtype=jnp.float32)
        loop_weight = jax.random.normal(ks[3], (IN_FEAT, OUT_FEAT), dtype=jnp.float32)
        forward_bias = jnp.zeros((OUT_FEAT,), dtype=jnp.float32)
        backward_bias = jnp.zeros((OUT_FEAT,), dtype=jnp.float32)
        self_bias = jnp.zeros((OUT_FEAT,), dtype=jnp.float32)
        src = jax.random.randint(ks[4], (N_EDGES,), 0, N_NODES, dtype=jnp.int32)
        dst = jax.random.randint(ks[5], (N_EDGES,), 0, N_NODES, dtype=jnp.int32)
        etypes = jax.random.randint(ks[6], (N_EDGES,), 0, NUM_RELS, dtype=jnp.int32)
        return {'feat': feat, 'Wf': Wf, 'Wb': Wb, 'loop_weight': loop_weight, 'forward_bias': forward_bias, 'backward_bias': backward_bias, 'self_bias': self_bias, 'src': src, 'dst': dst, 'etypes': etypes, 'use_dis_weight': 0, 'drop_out': 0}
    _L0_gnn_all = _L0_gnn_setup()
    _L0_gnn_in = {k: v for k, v in _L0_gnn_all.items() if k in ('Wf', 'Wb', 'loop_weight', 'forward_bias', 'backward_bias', 'self_bias')}
    del _L0_gnn_all

    def _L0_mix_setup():
        import jax, jax.numpy as jnp
        import numpy as np
        B, N, C = (8, 512, 256)
        H, D, S = (8, 32, 32)
        HID = 4 * C

        def layernorm(x, w, b, eps=1e-05):
            mu = jnp.mean(x, axis=-1, keepdims=True)
            var = jnp.mean(jnp.square(x - mu), axis=-1, keepdims=True)
            return (x - mu) * jax.lax.rsqrt(var + eps) * w + b

        def linear_no_attn(x, Wx, bx, Wq, Wk, Wv, Wo, bo):
            x_mid = x @ Wx.T + bx
            x_mid = x_mid.reshape(x.shape[0], x.shape[1], H, D).transpose(0, 2, 1, 3)
            q = jax.nn.softmax(x_mid @ Wq.T, axis=-1)
            k = jax.nn.softmax(x_mid @ Wk.T, axis=-2)
            v = x_mid @ Wv.T
            kv = jnp.einsum('bhns,bhnd->bhsd', k, v)
            qkv = jnp.einsum('bhns,bhsd->bhnd', q, kv)
            qkv = qkv.transpose(0, 2, 1, 3).reshape(x.shape[0], x.shape[1], H * D)
            return qkv @ Wo.T + bo
        key = jax.random.key(seed)
        ks = jax.random.split(key, 16)
        s = lambda fan: 1.0 / np.sqrt(fan)
        return {'fx': jax.random.normal(ks[0], (B, N, C), jnp.float32), 'ln1_w': jnp.ones((C,), jnp.float32), 'ln1_b': jnp.zeros((C,), jnp.float32), 'Wx': jax.random.uniform(ks[1], (C, C), jnp.float32, -s(C), s(C)), 'bx': jax.random.uniform(ks[2], (C,), jnp.float32, -s(C), s(C)), 'Wq': jax.random.uniform(ks[3], (S, D), jnp.float32, -s(D), s(D)), 'Wk': jax.random.uniform(ks[4], (S, D), jnp.float32, -s(D), s(D)), 'Wv': jax.random.uniform(ks[5], (D, D), jnp.float32, -s(D), s(D)), 'Wo': jax.random.uniform(ks[6], (C, C), jnp.float32, -s(C), s(C)), 'bo': jax.random.uniform(ks[7], (C,), jnp.float32, -s(C), s(C)), 'ln2_w': jnp.ones((C,), jnp.float32), 'ln2_b': jnp.zeros((C,), jnp.float32), 'W1': jax.random.uniform(ks[8], (HID, C), jnp.float32, -s(C), s(C)), 'b1': jax.random.uniform(ks[9], (HID,), jnp.float32, -s(C), s(C)), 'W2': jax.random.uniform(ks[10], (C, HID), jnp.float32, -s(HID), s(HID)), 'b2': jax.random.uniform(ks[11], (C,), jnp.float32, -s(HID), s(HID))}
    _L0_mix_all = _L0_mix_setup()
    _L0_mix_in = {k: v for k, v in _L0_mix_all.items() if k in ('ln1_w', 'ln1_b', 'Wx', 'bx', 'Wq', 'Wk', 'Wv', 'Wo', 'bo', 'ln2_w', 'ln2_b', 'W1', 'b1', 'W2', 'b2')}
    del _L0_mix_all

    def _L0_ffn_setup():
        import jax, jax.numpy as jnp
        import numpy as np
        TOP_K = 2
        LN_EPS = 1e-05
        key = jax.random.key(seed)
        ks = jax.random.split(key, 8)
        B, S, D, E, H = (16, 1024, 256, 8, 1024)
        x = jax.random.normal(ks[0], (B, S, D), dtype=jnp.float32)
        Wr = jax.random.normal(ks[1], (D, E), dtype=jnp.float32) * 0.1
        br = jnp.zeros((E,), dtype=jnp.float32)
        ln_g = jnp.ones((E, D), dtype=jnp.float32)
        ln_b = jnp.zeros((E, D), dtype=jnp.float32)
        W1 = jax.random.normal(ks[2], (E, D, H), dtype=jnp.float32) * (1.0 / np.sqrt(D))
        b1 = jnp.zeros((E, H), dtype=jnp.float32)
        W2 = jax.random.normal(ks[3], (E, H, D), dtype=jnp.float32) * (1.0 / np.sqrt(H))
        b2 = jnp.zeros((E, D), dtype=jnp.float32)
        return {'x': x, 'Wr': Wr, 'br': br, 'ln_g': ln_g, 'ln_b': ln_b, 'W1': W1, 'b1': b1, 'W2': W2, 'b2': b2}
    _L0_ffn_all = _L0_ffn_setup()
    _L0_ffn_in = {k: v for k, v in _L0_ffn_all.items() if k in ('Wr', 'br', 'ln_g', 'ln_b', 'W1', 'b1', 'W2', 'b2')}
    del _L0_ffn_all
    return {'x': x, 'src': src, 'dst': dst, 'edge_type_16': edge_type_16, 'L0_gnn_Wf': _L0_gnn_in['Wf'], 'L0_gnn_Wb': _L0_gnn_in['Wb'], 'L0_gnn_loop_weight': _L0_gnn_in['loop_weight'], 'L0_gnn_forward_bias': _L0_gnn_in['forward_bias'], 'L0_gnn_backward_bias': _L0_gnn_in['backward_bias'], 'L0_gnn_self_bias': _L0_gnn_in['self_bias'], 'L0_mix_ln1_w': _L0_mix_in['ln1_w'], 'L0_mix_ln1_b': _L0_mix_in['ln1_b'], 'L0_mix_Wx': _L0_mix_in['Wx'], 'L0_mix_bx': _L0_mix_in['bx'], 'L0_mix_Wq': _L0_mix_in['Wq'], 'L0_mix_Wk': _L0_mix_in['Wk'], 'L0_mix_Wv': _L0_mix_in['Wv'], 'L0_mix_Wo': _L0_mix_in['Wo'], 'L0_mix_bo': _L0_mix_in['bo'], 'L0_mix_ln2_w': _L0_mix_in['ln2_w'], 'L0_mix_ln2_b': _L0_mix_in['ln2_b'], 'L0_mix_W1': _L0_mix_in['W1'], 'L0_mix_b1': _L0_mix_in['b1'], 'L0_mix_W2': _L0_mix_in['W2'], 'L0_mix_b2': _L0_mix_in['b2'], 'L0_ffn_Wr': _L0_ffn_in['Wr'], 'L0_ffn_br': _L0_ffn_in['br'], 'L0_ffn_ln_g': _L0_ffn_in['ln_g'], 'L0_ffn_ln_b': _L0_ffn_in['ln_b'], 'L0_ffn_W1': _L0_ffn_in['W1'], 'L0_ffn_b1': _L0_ffn_in['b1'], 'L0_ffn_W2': _L0_ffn_in['W2'], 'L0_ffn_b2': _L0_ffn_in['b2']}

def reference(x, src, dst, edge_type_16, L0_gnn_Wf, L0_gnn_Wb, L0_gnn_loop_weight, L0_gnn_forward_bias, L0_gnn_backward_bias, L0_gnn_self_bias, L0_mix_ln1_w, L0_mix_ln1_b, L0_mix_Wx, L0_mix_bx, L0_mix_Wq, L0_mix_Wk, L0_mix_Wv, L0_mix_Wo, L0_mix_bo, L0_mix_ln2_w, L0_mix_ln2_b, L0_mix_W1, L0_mix_b1, L0_mix_W2, L0_mix_b2, L0_ffn_Wr, L0_ffn_br, L0_ffn_ln_g, L0_ffn_ln_b, L0_ffn_W1, L0_ffn_b1, L0_ffn_W2, L0_ffn_b2):
    import jax
    import jax.numpy as jnp

    def _L0_gnn_ref(feat, Wf, Wb, loop_weight, forward_bias, backward_bias, self_bias, src, dst, etypes, use_dis_weight, drop_out):
        import jax, jax.numpy as jnp
        import numpy as np
        from jax.ops import segment_sum
        N_NODES = 625
        N_EDGES = 10000
        IN_FEAT = 256
        OUT_FEAT = 256
        NUM_RELS = 16

        def _inv_degree(idx, n):
            deg = segment_sum(jnp.ones(idx.shape[0], dtype=jnp.float32), idx, num_segments=n)
            return jnp.where(deg > 0, 1.0 / deg, 0.0)

        def _typed_pass(feat, W, bias, src_idx, dst_idx, etypes, norm_per_edge, n):
            proj = jnp.einsum('ni,rio->rno', feat, W)
            m = proj[etypes, src_idx] + bias
            m = m * norm_per_edge[:, None]
            return segment_sum(m, dst_idx, num_segments=n)
        n = feat.shape[0]
        norm_f = _inv_degree(dst, n)[dst]
        m_forward = _typed_pass(feat, Wf, forward_bias, src, dst, etypes, norm_f, n)
        norm_b = _inv_degree(src, n)[src]
        m_backward = _typed_pass(feat, Wb, backward_bias, dst, src, etypes, norm_b, n)
        s = feat @ loop_weight
        s = s + s + self_bias
        return s + m_forward + m_backward

    def _L0_mix_ref(fx, ln1_w, ln1_b, Wx, bx, Wq, Wk, Wv, Wo, bo, ln2_w, ln2_b, W1, b1, W2, b2):
        import jax, jax.numpy as jnp
        import numpy as np
        B, N, C = (8, 512, 256)
        H, D, S = (8, 32, 32)
        HID = 4 * C

        def layernorm(x, w, b, eps=1e-05):
            mu = jnp.mean(x, axis=-1, keepdims=True)
            var = jnp.mean(jnp.square(x - mu), axis=-1, keepdims=True)
            return (x - mu) * jax.lax.rsqrt(var + eps) * w + b

        def linear_no_attn(x, Wx, bx, Wq, Wk, Wv, Wo, bo):
            x_mid = x @ Wx.T + bx
            x_mid = x_mid.reshape(x.shape[0], x.shape[1], H, D).transpose(0, 2, 1, 3)
            q = jax.nn.softmax(x_mid @ Wq.T, axis=-1)
            k = jax.nn.softmax(x_mid @ Wk.T, axis=-2)
            v = x_mid @ Wv.T
            kv = jnp.einsum('bhns,bhnd->bhsd', k, v)
            qkv = jnp.einsum('bhns,bhsd->bhnd', q, kv)
            qkv = qkv.transpose(0, 2, 1, 3).reshape(x.shape[0], x.shape[1], H * D)
            return qkv @ Wo.T + bo
        h = linear_no_attn(layernorm(fx, ln1_w, ln1_b), Wx, bx, Wq, Wk, Wv, Wo, bo) + fx
        y = layernorm(h, ln2_w, ln2_b)
        y = jax.nn.gelu(y @ W1.T + b1, approximate=False)
        y = y @ W2.T + b2
        return y + h

    def _L0_ffn_ref(x, Wr, br, ln_g, ln_b, W1, b1, W2, b2):
        import jax, jax.numpy as jnp
        import numpy as np
        TOP_K = 2
        LN_EPS = 1e-05
        B, S, D = x.shape
        N = B * S
        xt = x.reshape(N, D)
        logits = xt @ Wr + br
        probs = jax.nn.softmax(logits, axis=-1)
        top_p, top_idx = jax.lax.top_k(probs, TOP_K)
        weights = top_p / top_p.sum(axis=-1, keepdims=True)
        mu = xt.mean(axis=-1, keepdims=True)
        var = ((xt - mu) ** 2).mean(axis=-1, keepdims=True)
        xn = (xt - mu) * jax.lax.rsqrt(var + LN_EPS)
        xe = xn[None, :, :] * ln_g[:, None, :] + ln_b[:, None, :]
        h = jax.nn.gelu(jnp.einsum('end,edh->enh', xe, W1) + b1[:, None, :], approximate=False)
        y = jnp.einsum('enh,ehd->end', h, W2) + b2[:, None, :]
        y_tok = jnp.transpose(y, (1, 0, 2))
        sel = jnp.take_along_axis(y_tok, top_idx[:, :, None], axis=1)
        out = (weights[:, :, None] * sel).sum(axis=1)
        return out.reshape(B, S, D)
    xn = _layernorm(x, axis=-1)
    x = x + _L0_gnn_ref(xn, L0_gnn_Wf, L0_gnn_Wb, L0_gnn_loop_weight, L0_gnn_forward_bias, L0_gnn_backward_bias, L0_gnn_self_bias, src, dst, edge_type_16, 0, 0) + _L0_mix_ref(xn[None], L0_mix_ln1_w, L0_mix_ln1_b, L0_mix_Wx, L0_mix_bx, L0_mix_Wq, L0_mix_Wk, L0_mix_Wv, L0_mix_Wo, L0_mix_bo, L0_mix_ln2_w, L0_mix_ln2_b, L0_mix_W1, L0_mix_b1, L0_mix_W2, L0_mix_b2)[0]
    x = x + _L0_ffn_ref(_layernorm(x, axis=-1)[None], L0_ffn_Wr, L0_ffn_br, L0_ffn_ln_g, L0_ffn_ln_b, L0_ffn_W1, L0_ffn_b1, L0_ffn_W2, L0_ffn_b2)[0]
    return x

_drawn_inputs = setup_inputs


def setup_inputs(seed=0):
    import zlib

    import numpy as np

    out = dict(_drawn_inputs(seed))
    spreads = {'L0_gnn_forward_bias': (0.0, 2.0),
     'L0_gnn_backward_bias': (0.0, 2.0),
     'L0_gnn_self_bias': (0.0, 2.0),
     'L0_mix_ln1_w': (1.0, 0.6),
     'L0_mix_ln1_b': (0.0, 0.8),
     'L0_mix_ln2_w': (1.0, 0.6),
     'L0_mix_ln2_b': (0.0, 0.8),
     'L0_ffn_br': (0.0, 2.0),
     'L0_ffn_ln_g': (1.0, 0.6),
     'L0_ffn_ln_b': (0.0, 2.0),
     'L0_ffn_b1': (0.0, 2.0),
     'L0_ffn_b2': (0.0, 2.0)}
    factors = {'L0_mix_Wx': 8.0,
     'L0_mix_bx': 8.0,
     'L0_mix_Wq': 8.0,
     'L0_mix_Wk': 8.0,
     'L0_mix_Wv': 8.0,
     'L0_mix_Wo': 8.0,
     'L0_mix_bo': 200.0,
     'L0_mix_W1': 8.0,
     'L0_mix_b1': 186.174,
     'L0_mix_W2': 8.0,
     'L0_mix_b2': 200.0,
     'L0_ffn_Wr': 3.767,
     'L0_ffn_W1': 3.782,
     'L0_ffn_W2': 3.398,
     'L0_gnn_Wf': 4.931,
     'L0_gnn_Wb': 4.936}
    for name, (base, spread) in spreads.items():
        noise = np.random.default_rng([zlib.crc32(name.encode()), seed]).standard_normal(out[name].shape)
        drawn = base * np.exp(spread * noise) if base else spread * noise
        out[name] = jnp.asarray(drawn.astype(out[name].dtype))
    for name, factor in factors.items():
        out[name] = (out[name] * factor).astype(out[name].dtype)
    return out
```

```python
import concourse.bass as bass
from concourse import mybir

N, C, E, R = 3125, 256, 53125, 16
P = 128
NT = 26
NP = NT * P
EC = 416
HEADS, HD = 8, 32
HID = 1024
NX, TOPK = 8, 2
TE = (E + (NT - 1) * (P - 1)) // P + 1
TX = (N * TOPK + NX * (P - 1)) // P
EPS = 1e-5
BIG = 1.0e6

f32, i32 = mybir.dt.float32, mybir.dt.int32
ALU, ACT, AX = mybir.AluOpType, mybir.ActivationFunctionType, mybir.AxisListType

C_ID, C_IOTA, C_TRI, C_ONE, C_VALID, C_TILE, C_PID = 0, 128, 256, 384, 512, 538, 978
C_TOK = 979
C_N = C_TOK + NT


def constants(np):
    c = np.zeros((P, C_N), np.float32)
    p = np.arange(P)
    c[:, C_ID:C_ID + P] = np.eye(P)
    c[:, C_IOTA:C_IOTA + P] = p[None, :]
    c[:, C_TRI:C_TRI + P] = p[:, None] < p[None, :]
    c[:, C_ONE:C_ONE + P] = 1.0
    rows = np.arange(NT)[None, :] * P + p[:, None]
    c[:, C_VALID:C_VALID + NT] = rows < N
    c[:, C_TILE:C_TILE + TE] = np.arange(TE)[None, :]
    c[:, C_PID] = p
    c[:, C_TOK:C_TOK + NT] = rows
    return c


class Engine:

    def __init__(self, e, ns, sem, pad):
        self.e, self.ns, self.sem, self.pad, self.n, self.reg = e, ns, sem, pad, 0, 0

    def wait(self, sem, value):
        if not (isinstance(value, int) and value <= 0):
            self.e.wait_ge(sem, value)

    def link(self, ins):
        ins.then_inc(self.sem, 1)
        self.n += 1
        self.e.wait_ge(self.sem, self.reg + self.n)

    def settle(self):
        self.e.sem_inc(self.pad, 1)

    def loop(self, n, body, last=False):
        start = self.n
        body(0)
        per = self.n - start
        end = n - 1 if last else n
        with self.e.Fori(1, end) as i:
            self.reg, self.n = i * per, start
            body(i)
        self.reg, self.n = 0, start + end * per
        if last:
            body(n - 1)


def build(nc, a, out):
    from contextlib import ExitStack
    ctx = ExitStack()
    ds = bass.ds

    def dram(name, rows, cols, dt=f32):
        return nc.dram_tensor(name, (rows, cols), dt, kind="Internal").ap()

    table = [dram("table_fwd", NP * R, C), dram("table_bwd", NP * R, C)]
    mixd = dram("mix_rows", NP, 770)
    gmapd = [dram("bin_of_tile_fwd", 1, TE, i32), dram("bin_of_tile_bwd", 1, TE, i32)]
    slotd = [dram("slots_fwd", P * TE, 2, i32), dram("slots_bwd", P * TE, 2, i32)]
    xtok = dram("ffn_tokens", NP, C)
    xslotd = dram("ffn_slots", P * TX, 1, i32)
    yslot = dram("ffn_rows", P * TX, C)

    with ctx:
        def sb(name, cols, dt=f32, rows=P):
            return ctx.enter_context(nc.sbuf_tensor(name, [rows, cols], dt))

        nsem = [0]

        def sem(name):
            nsem[0] += 1
            return ctx.enter_context(nc.semaphore(f"{name}_{nsem[0]}"))

        def sems(name, n):
            return [sem(f"{name}{i}") for i in range(n)]

        arena = sb("arena", 32768)
        X1 = sb("X1", NT * C)
        xn = sb("xn", NT * C)
        cst = sb("cst", C_N)
        work = sb("work", 3074)
        small = sb("small", 900)
        ps = [ctx.enter_context(nc.psum_tensor(f"bank{i}", [P, 512], f32)) for i in range(8)]
        ident, iota = cst[:, C_ID:C_ID + P], cst[:, C_IOTA:C_IOTA + P]
        tri, ones = cst[:, C_TRI:C_TRI + P], cst[:, C_ONE:C_ONE + P]
        one_row = cst[0:1, C_ONE:C_ONE + P]

        def ar(off, n, rows=P):
            return arena[0:rows, off:off + n]

        W_off = 0
        STG = [16384, 20480]
        W1T_off, W2T_off = 24576, 26624
        PAY = [28672, 29504]
        ADR = [30336, 30752]
        WM_off = 31168
        so = [0]

        def sm(n, rows=P):
            so[0] += n
            return small[0:rows, so[0] - n:so[0]]

        st = sm(NT * 6)
        mean, rstd, mean2, rstd2 = sm(NT), sm(NT), sm(NT), sm(NT)
        v1, v2, v3 = sm(NT), sm(NT), sm(NT)
        lncol = sm(8)
        b1col = sm(8)
        kmT = sm(2)
        bxcol = sm(2)
        cnt, tot, til, base, incl = sm(NT), sm(NT), sm(NT), sm(NT), sm(NT)
        den = sm(2)
        rmax, rsum = sm(HEADS), sm(HEADS)
        dgw = sm(2 * NT)
        brow = sb("brow", 768, f32, 1)
        lw = sb("lw", 512)
        kmax = sb("kmax", C)

        s_v, s_a, s_p, s_g, s_s = sem("dve"), sem("act"), sem("pe"), sem("pool"), sem("sp")
        s_pad = sem("pad")
        V = Engine(None, nc.vector, s_v, s_pad)
        A = Engine(None, nc.scalar, s_a, s_pad)
        T = Engine(None, nc.tensor, s_p, s_pad)
        G = Engine(None, nc.gpsimd, s_g, s_pad)
        S = Engine(None, nc.sync, s_s, s_pad)

        vec, act, pe = nc.vector, nc.scalar, nc.tensor

        def ts(out, in0, s1, op0, s2=None, op1=None):
            if op1 is None:
                return vec.tensor_scalar(out, in0, s1, None, op0)
            return vec.tensor_scalar(out, in0, s1, s2, op0, op1)

        def norm_stats(src, m, r, s_var, s_sqrt):
            def stats(t):
                V.settle()
                V.link(vec.bn_stats(st[:, ds(t * 6, 6)], src[:, ds(t * C, C)]))
            V.loop(NT, stats)
            q = st.rearrange("p (t s) -> p t s", s=6)
            me, ve, mo, vo = q[:, :, 1], q[:, :, 2], q[:, :, 4], q[:, :, 5]
            V.link(vec.tensor_tensor(m, me, mo, ALU.add))
            V.link(ts(m, m, 0.5, ALU.mult))
            V.link(vec.tensor_tensor(v1, me, mo, ALU.subtract))
            V.link(vec.tensor_tensor(v1, v1, v1, ALU.mult))
            V.link(vec.tensor_tensor(v2, ve, vo, ALU.add))
            V.link(ts(v2, v2, 1.0 / C, ALU.mult, EPS, ALU.add))
            vec.scalar_tensor_tensor(v1, v1, 0.25, v2, ALU.mult, ALU.add).then_inc(s_var, 1)
            V.e.wait_ge(s_sqrt, 1)
            V.link(vec.reciprocal(v2, v2))
            V.link(vec.tensor_tensor(v3, v2, v2, ALU.mult))
            V.link(vec.tensor_tensor(v3, v3, v1, ALU.mult))
            V.link(ts(v3, v3, -0.5, ALU.mult, 1.5, ALU.add))
            V.link(vec.tensor_tensor(r, v2, v3, ALU.mult))

        def norm_root(s_var, s_sqrt):
            A.e.wait_ge(s_var, 1)
            act.activation(v2, v1, ACT.Sqrt).then_inc(s_sqrt, 1)

        def norm_apply(dst, t, src, m, r):
            return vec.tensor_scalar(dst, src[:, ds(t * C, C)], m[:, ds(t, 1)], r[:, ds(t, 1)],
                                     ALU.subtract, ALU.mult)

        def bin_positions(key, cols, bins, pos, tmp, scan_ones, gmap, tiles, s_cnt, s_tot):
            def count(g):
                V.link(vec.tensor_scalar(tmp, key, iota[:, ds(g, 1)], None, ALU.is_equal))
                V.settle()
                V.link(vec.tensor_reduce(cnt[:, ds(g, 1)], tmp, AX.X, ALU.add))
            V.loop(bins, count)
            c_, t_, l_, b_, i_ = (x[:, 0:bins] for x in (cnt, tot, til, base, incl))
            V.e.sem_inc(s_cnt, 1)
            V.e.wait_ge(s_tot, 1)
            V.link(vec.tensor_copy(t_, ps[0][:, 64:64 + bins]))
            V.link(ts(l_, t_, float(P - 1), ALU.add))
            ti = v1[:, 0:bins].bitcast(i32)
            V.link(vec.tensor_copy(ti, l_))
            V.link(vec.tensor_single_scalar(ti, ti, 7, op=ALU.arith_shift_right))
            V.link(vec.tensor_copy(l_, ti))
            V.link(vec.tensor_tensor_scan(i_, scan_ones[:, 0:bins], l_, 0.0, ALU.mult, ALU.add))
            V.link(vec.tensor_tensor(b_, i_, l_, ALU.subtract))
            V.link(ts(b_, b_, float(P), ALU.mult, -1.0, ALU.add))
            V.link(vec.tensor_tensor(b_, b_, ps[0][:, 0:bins], ALU.add))
            V.link(vec.memset(pos, 0.0))
            V.link(vec.memset(gmap, 0.0))

            def place(g):
                V.link(vec.tensor_scalar(tmp, key, iota[:, ds(g, 1)], None, ALU.is_equal))
                V.link(vec.tensor_tensor_scan(scan_out, scan_ones, tmp, base[:, ds(g, 1)],
                                              ALU.mult, ALU.add))
                V.link(vec.tensor_tensor(tmp, tmp, scan_out, ALU.mult))
                V.link(vec.tensor_tensor(pos, pos, tmp, ALU.add))
                V.link(vec.scalar_tensor_tensor(gmap, cst[:, C_TILE:C_TILE + tiles],
                                                incl[:, ds(g, 1)], gmap, ALU.is_ge, ALU.add))
            scan_out = scan_buf[:, 0:cols]
            V.loop(bins, place)
            V.link(ts(gmap, gmap, float(bins - 1), ALU.min))

        def bin_counts(bins, s_cnt, s_tot):
            T.e.wait_ge(s_cnt, 1)
            pe.matmul(ps[0][:, 0:bins], tri, cnt[:, 0:bins], start=True, stop=True)
            pe.matmul(ps[0][:, 64:64 + bins], ones, cnt[:, 0:bins], start=True,
                      stop=True).then_inc(s_tot, 1)

        def slot_address(dst, pos, tiles, ta, tb):
            V.link(vec.tensor_copy(ta, pos))
            V.link(vec.tensor_single_scalar(tb, ta, P - 1, op=ALU.bitwise_and))
            V.link(vec.tensor_single_scalar(ta, ta, 7, op=ALU.arith_shift_right))
            V.link(vec.scalar_tensor_tensor(dst, tb, float(tiles), ta, ALU.mult, ALU.add))

        TMP = STG[0]
        ei = [ar(TMP + j * EC, EC).bitcast(i32) for j in range(3)]
        ke, tmp, scan_buf_e, posb = (ar(TMP + j * EC, EC) for j in range(3, 7))
        ones_e = ar(TMP + 7 * EC, EC)
        gmapf = ar(TMP + 8 * EC, TE)
        scan_buf = scan_buf_e
        empty = work[:, 0:2 * TE]
        gmapi = [work[0:1, 880 + d * TE:880 + (d + 1) * TE].bitcast(i32) for d in range(2)]
        s_em, s_gm, s_ed = sem("empty_slots"), sem("bin_of_tile"), sem("slots_default")
        BD = ar(TMP + 4096, P)
        BDk, BDv = ar(TMP + 4224, P), ar(TMP + 4352, P)
        WX = ar(TMP + 4480, 512)
        Pm_off = TMP + 4480 + 512
        WOT = ar(Pm_off + 512, 512)
        Pm = sb("Pm", 512)

        ld, ldx, lde, ldw, zbd = sem("ld_small"), sem("ld_x"), sem("ld_edges"), sem("ld_tables"), sem("zero")
        ldb = sem("ld_blocks")
        sv1, sq1, sv2, sq2 = sem("var"), sem("root"), sem("var"), sem("root")
        sc = [sem("counts"), sem("counts")]
        stt = [sem("totals"), sem("totals")]
        folded = sem("folded")
        foldc = sem("folded_copied")
        with nc.Block() as block:
            @block.sync
            def _(e):
                S.e = e
                n = 0
                for o, i in ((cst[:, :], a["cst"]), (lncol[:, 0:2], a["ln1w"]), (lncol[:, 2:4], a["ln1b"]),
                             (lncol[:, 4:6], a["ln2w"]), (lncol[:, 6:8], a["ln2b"]), (b1col, a["mb1"]),
                             (bxcol, a["bx"]), (brow[0:1, 512:768], a["bxrow"])):
                    e.dma_start(o, i).then_inc(ld, 16)
                    n += 16
                e.wait_ge(ld, n)
                for j, k in enumerate(("src", "dst", "et")):
                    e.dma_start(ei[j], a[k]).then_inc(lde, 16)
                for c in range(2):
                    e.dma_start(WX[:, c * C:(c + 1) * C], a["Wx"][c * P:(c + 1) * P, :]).then_inc(ld, 16)
                    e.dma_start(WOT[:, c * C:(c + 1) * C], a["WoT"][c * P:(c + 1) * P, :]).then_inc(ld, 16)
                    e.dma_start(lw[:, c * C:(c + 1) * C], a["lw"][c * P:(c + 1) * P, :]).then_inc(ld, 16)
                    e.dma_start(ar(WM_off + c * 768 + 512, C), a["WxT"][c * P:(c + 1) * P, :]).then_inc(ld, 16)
                e.wait_ge(zbd, 3)
                for j in range(4):
                    o = slice(j * HD, (j + 1) * HD)
                    for m, k in ((BD, "WqT"), (BDk, "WkT"), (BDv, "Wv")):
                        e.dma_start(m[o, o], a[k]).then_inc(ldb, 16)
                e.dma_start(X1[:, :].rearrange("p (t c) -> p t c", c=C),
                            a["x"].rearrange("(t p) c -> p t c", p=P)).then_inc(ldx, 16)
                for c in range(2):
                    for d, k in enumerate(("Wf", "Wb")):
                        e.dma_start(ar(W_off + c * 8192 + d * 4096, 4096),
                                    a[k][c * P:(c + 1) * P, :]).then_inc(ldw, 16)
                    e.dma_start(ar(W1T_off + c * HID, HID), a["mW1T"][c * P:(c + 1) * P, :]).then_inc(ldw, 16)
                for j in range(8):
                    e.dma_start(ar(W2T_off + j * C, C), a["mW2T"][j * P:(j + 1) * P, :]).then_inc(ldw, 16)
                e.wait_ge(s_em, 1)
                for d in range(2):
                    e.dma_start(slotd[d].rearrange("(p t) two -> p (t two)", p=P),
                                empty.bitcast(i32)).then_inc(s_ed, 16)
                e.wait_ge(s_gm, 2)
                for d in range(2):
                    e.dma_start(gmapd[d], gmapi[d]).then_inc(s_ed, 16)
                e.wait_ge(s_ed, 64)
                e.wait_ge(ldw, 14 * 16)
                e.wait_ge(lde, 48)
                e.wait_ge(ldx, 16)
                e.wait_ge(ld, n + 128)
                e.wait_ge(ldb, 12 * 16)

            @block.vector
            def _(e):
                V.e = e
                for m in (BD, BDk, BDv):
                    vec.memset(m, 0.0).then_inc(zbd, 1)
                e.wait_ge(ld, 8 * 16 + 128)
                e.wait_ge(lde, 48)
                V.link(vec.memset(ones_e, 1.0))
                V.link(vec.memset(empty, 0.0))
                vec.memset(empty.rearrange("p (t two) -> p t two", two=2)[:, :, 1], 999.0).then_inc(s_em, 1)
                for d in range(2):
                    key, other = (ei[1], ei[0]) if d == 0 else (ei[0], ei[1])
                    pay = ar(PAY[d], 2 * EC).bitcast(i32).rearrange("p (c two) -> p c two", two=2)
                    payf = ar(PAY[d], 2 * EC).rearrange("p (c two) -> p c two", two=2)
                    ti = tmp.bitcast(i32)
                    V.link(ts(ti, other, float(R), ALU.mult))
                    V.link(vec.tensor_tensor(pay[:, :, 0], ti, ei[2], ALU.add))
                    V.link(vec.tensor_single_scalar(ti, key, P - 1, op=ALU.bitwise_and))
                    V.link(vec.tensor_copy(payf[:, :, 1], ti))
                    V.link(vec.tensor_single_scalar(ti, key, 7, op=ALU.arith_shift_right))
                    V.link(vec.tensor_copy(ke, ti))
                    bin_positions(ke, EC, NT, posb, tmp, ones_e, gmapf, TE, sc[d], stt[d])
                    slot_address(ar(ADR[d], EC).bitcast(i32), posb, TE, ti, scan_buf.bitcast(i32))
                    ts(gmapi[d], gmapf[0:1, :], float(C + 1), ALU.mult).then_inc(s_gm, 1)
                e.wait_ge(ldx, 16)
                norm_stats(X1, mean, rstd, sv1, sq1)
                V.loop(NT, lambda t: V.link(norm_apply(xn[:, ds(t * C, C)], t, X1, mean, rstd)))
                norm_stats(xn, mean2, rstd2, sv2, sq2)
                V.link(vec.memset(kmax[:, :], -3.0e38))
                e.wait_ge(folded, 1)
                for c in range(2):
                    V.link(vec.tensor_copy(ar(WM_off + c * 768, 512), ps[1 + c][:, :]))
                V.link(vec.tensor_copy(brow[0:1, 0:512], ps[3][0:1, :]))
                V.link(vec.tensor_copy(Pm[:, :], ps[4][:, :]))

            @block.scalar
            def _(e):
                A.e = e
                norm_root(sv1, sq1)
                norm_root(sv2, sq2)

            @block.tensor
            def _(e):
                T.e = e
                e.wait_ge(ld, 8 * 16 + 128)
                for d in range(2):
                    bin_counts(NT, sc[d], stt[d])
                e.wait_ge(ldb, 12 * 16)
                for i in range(2):
                    for m, bd in enumerate((BDk, BD)):
                        for c in range(2):
                            pe.matmul(ps[1 + i][:, m * C + c * P:m * C + (c + 1) * P],
                                      WX[:, c * C + i * P:c * C + (i + 1) * P], bd, start=True, stop=True)
                for m, bd in enumerate((BDk, BD)):
                    for c in range(2):
                        pe.matmul(ps[3][0:1, m * C + c * P:m * C + (c + 1) * P], bxcol[:, c:c + 1], bd,
                                  start=True, stop=True)
                for c in range(2):
                    last = pe.matmul(ps[4][:, c * C:(c + 1) * C], BDv, WOT[:, c * C:(c + 1) * C],
                                     start=True, stop=True)
                last.then_inc(folded, 1)

        w = [0]

        def wk(n):
            w[0] += n
            return work[:, w[0] - n:w[0]]

        xs, zs, xT, zT = ([wk(C) for _ in range(2)] for _ in range(4))
        mst = wk(770)
        qx = wk(C)
        ist = [sb(f"ist{h}", 4, i32) for h in range(2)]
        pst = [sb(f"pst{h}", 8, i32) for h in range(2)]
        s_xs, s_tp, s_xT, s_mm, s_loop = sem("tile_ready"), sem("transposed"), sem("transposes_out"), sem("mix_mm"), sem("loop_mm")
        s_ev, s_mrow, s_mdma, s_x1 = sem("mix_evacuated"), sem("mix_row"), sem("mix_dma"), sem("x1_added")
        s_pj, s_pe_, s_q, s_qe = sem("proj_mm"), sem("proj_out"), sem("q_minus_max"), sem("q_exp")
        s_td = [sem("table_dma"), sem("table_dma")]
        s_sc = sems("scatter", 8)
        s_cp = sem("copied")
        s_ms = sem("ones_set")
        s_xm = sem("xm_out")

        def bin_edges(e, count, table_dram, adr, pay, width, base_, bound=None):
            def body(i):
                for h in range(2):
                    for u in range(4):
                        G.wait(s_sc[4 * h + u], sc_base[0] + 16 * i)
                    G.settle()
                    c0 = i * 8 + 4 * h
                    nc.gpsimd.tensor_copy(ist[h][:, :], adr[:, ds(c0, 4)]).then_inc(s_cp, 1)
                    nc.gpsimd.tensor_copy(pst[h][:, 0:4 * width],
                                          pay[:, ds(c0 * width, 4 * width)]).then_inc(s_cp, 1)
                    e.wait_ge(s_cp, base_ + 4 * i + 2 * h + 2)
                    G.settle()
                    for u in range(4):
                        kw = {} if bound is None else dict(bounds_check=bound, oob_is_err=False)
                        e.indirect_dma_start(table_dram, bass.IndirectOffsetOnAxis(ap=ist[h][:, u:u + 1], axis=0),
                                             pst[h][:, u * width:(u + 1) * width], None,
                                             **kw).then_inc(s_sc[4 * h + u], 16)
            G.loop(count // 8, body)
            sc_base[0] += 16 * (count // 8)
            for u in range(8):
                e.wait_ge(s_sc[u], sc_base[0])
            return base_ + 4 * (count // 8)

        sc_base = [0]
        with nc.Block() as block:
            @block.gpsimd
            def _(e):
                G.e = e
                n = 0
                for d in range(2):
                    n = bin_edges(e, EC, slotd[d], ar(ADR[d], EC).bitcast(i32), ar(PAY[d], 2 * EC).bitcast(i32), 2, n)

            @block.vector
            def _(e):
                V.e = e
                V.link(vec.memset(mst[:, 512 + P:512 + P + 1], 1.0))
                V.link(vec.memset(mst[:, 769:770], 1.0))

                def body(i):
                    for u in range(2):
                        t = i * 2 + u
                        V.wait(s_tp, t - 1)
                        V.link(norm_apply(zs[u], t, xn, mean2, rstd2))
                        ts(xs[u], xn[:, ds(t * C, C)], 1.0, ALU.mult).then_inc(s_xs, 1)
                        e.wait_ge(s_tp, t + 1)
                        V.wait(s_loop, t - 1)
                        V.link(vec.tensor_copy(xT[u], ps[0][:, 0:C]))
                        for k in range(2):
                            V.link(ts(zT[u][:, k * P:(k + 1) * P], ps[0][:, C + k * P:C + (k + 1) * P],
                                      lncol[:, k:k + 1], ALU.mult, lncol[:, 2 + k:3 + k], ALU.add))
                        e.sem_inc(s_xT, 1)
                        e.wait_ge(s_mm, t + 1)
                        V.link(vec.scalar_tensor_tensor(X1[:, ds(t * C, C)], ps[3][:, 0:C], 2.0,
                                                        X1[:, ds(t * C, C)], ALU.mult, ALU.add))
                        V.wait(s_mdma, 16 * t)
                        V.link(vec.tensor_tensor(kmax[:, :], kmax[:, :], ps[1][:, 0:C], ALU.max))
                        V.link(vec.tensor_copy(mst[:, 0:C], ps[1][:, 0:C]))
                        V.link(vec.tensor_copy(mst[:, 512:770].rearrange("p (k c) -> p k c", k=2)[:, :, 0:P],
                                               ps[2][:, 0:C].rearrange("p (k c) -> p k c", k=2)))
                        qv = ps[1][:, C:2 * C].rearrange("p (h s) -> p h s", s=HD)
                        qxv = qx.rearrange("p (h s) -> p h s", s=HD)
                        V.link(vec.tensor_reduce(rmax, qv, AX.X, ALU.max))
                        vec.tensor_tensor(qxv, qv, rmax.unsqueeze(2).broadcast_to([P, HEADS, HD]),
                                          ALU.subtract).then_inc(s_q, 1)
                        e.wait_ge(s_qe, t + 1)
                        V.link(vec.tensor_reduce(rsum, qxv, AX.X, ALU.add))
                        V.link(vec.reciprocal(rsum, rsum))
                        vec.tensor_tensor(mst[:, C:2 * C].rearrange("p (h s) -> p h s", s=HD), qxv,
                                          rsum.unsqueeze(2).broadcast_to([P, HEADS, HD]),
                                          ALU.mult).then_inc(s_mrow, 1)
                V.loop(NT // 2, body)

            @block.scalar
            def _(e):
                A.e = e

                def body(i):
                    for u in range(2):
                        t = i * 2 + u
                        for d in range(2):
                            A.wait(s_td[d], 16 * t)
                            for c in range(8):
                                n = d * 8 + c
                                e.wait_ge(s_pj, t * 16 + n + 1)
                                act.activation(ar(STG[d] + c * 512, 512), ps[4 + n % 4][:, :],
                                               ACT.Copy).then_inc(s_pe_, 1)
                                if n == 3:
                                    e.wait_ge(s_q, t + 1)
                                    act.activation(qx, qx, ACT.Exp).then_inc(s_qe, 1)
                A.loop(NT // 2, body)

            @block.tensor
            def _(e):
                T.e = e

                def body(i):
                    for u in range(2):
                        t = i * 2 + u
                        e.wait_ge(s_xs, t + 1)
                        T.wait(s_xT, t)
                        for k in range(2):
                            pe.transpose(ps[0][:, k * P:(k + 1) * P], xs[u][:, k * P:(k + 1) * P], ident)
                        for k in range(2):
                            last = pe.transpose(ps[0][:, C + k * P:C + (k + 1) * P],
                                                zs[u][:, k * P:(k + 1) * P], ident)
                        last.then_inc(s_tp, 1)
                        e.wait_ge(s_xT, t + 1)
                        T.wait(s_mrow, t)
                        for k in range(2):
                            lz = zT[u][:, k * P:(k + 1) * P]
                            wm = WM_off + k * 768
                            pe.matmul(ps[1][:, :], lz, ar(wm, 512), start=(k == 0), stop=False)
                            pe.matmul(ps[2][:, 0:C], lz, ar(wm + 512, C), start=(k == 0), stop=False)
                            pe.matmul(ps[3][:, 0:C], xT[u][:, k * P:(k + 1) * P], lw[:, k * C:(k + 1) * C],
                                      start=(k == 0), stop=(k == 1))
                        pe.matmul(ps[1][:, :], one_row, brow[0:1, 0:512], start=False, stop=True)
                        pe.matmul(ps[2][:, 0:C], one_row, brow[0:1, 512:768], start=False,
                                  stop=True).then_inc(s_mm, 1)
                        for d in range(2):
                            for c in range(8):
                                n = d * 8 + c
                                T.wait(s_pe_, t * 16 + n - 3)
                                for k in range(2):
                                    last = pe.matmul(ps[4 + n % 4][:, :], xT[u][:, k * P:(k + 1) * P],
                                                     ar(W_off + k * 8192 + d * 4096 + c * 512, 512),
                                                     start=(k == 0), stop=(k == 1))
                                last.then_inc(s_pj, 1)
                        e.sem_inc(s_loop, 1)
                T.loop(NT // 2, body)

            @block.sync
            def _(e):
                S.e = e
                tv = [tb.rearrange("(n r) c -> n (r c)", r=R) for tb in table]

                def body(i):
                    for u in range(2):
                        t = i * 2 + u
                        e.wait_ge(s_mrow, t + 1)
                        e.dma_start(mixd[ds(t * P, P), :], mst).then_inc(s_mdma, 16)
                        for d in range(2):
                            e.wait_ge(s_pe_, t * 16 + d * 8 + 8)
                            e.dma_start(tv[d][ds(t * P, P), :], ar(STG[d], 4096)).then_inc(s_td[d], 16)
                S.loop(NT // 2, body)
                e.wait_ge(s_mdma, 16 * NT)
                for d in range(2):
                    e.wait_ge(s_td[d], 16 * NT)

        kx = [work[:, j * 512:j * 512 + 258] for j in range(2)]
        km = [ar(512 * j, C) for j in range(2)]
        kin = [ar(1024 + 770 * j, 770) for j in range(2)]
        kmb = ar(3072, C)
        dg = ar(3328, P)
        KX = ar(3584, C)
        KXT = ar(3840, C)
        M = ar(5120, 512)
        s_k1, s_k2, s_k3, s_k4, s_k5 = (sem("kmax_step") for _ in range(5))
        s_ki = sems("mix_in", 2)
        s_ks, s_ke, s_kv, s_km, s_kd = sem("k_minus_max"), sem("k_exp"), sem("xm_masked"), sem("kv_mm"), sem("kv_steps")
        with nc.Block() as block:
            @block.sync
            def _(e):
                S.e = e

                def body(i):
                    for u in range(2):
                        t = i * 2 + u
                        S.wait(s_kv, t - 1)
                        e.dma_start(kin[u], mixd[ds(t * P, P), :]).then_inc(s_ki[u], 16)
                S.loop(NT // 2, body)
                for u in range(2):
                    e.wait_ge(s_ki[u], 16 * NT // 2)

            @block.vector
            def _(e):
                V.e = e
                e.wait_ge(s_k1, 1)
                V.link(vec.tensor_reduce(kmT, ps[0][:, 0:C].rearrange("p (c n) -> p c n", c=2), AX.X, ALU.max))
                for c in range(2):
                    ts(dg, ident, kmT[:, c:c + 1], ALU.mult).then_inc(s_k2, 1)
                    e.wait_ge(s_k3, c + 1)
                V.link(vec.tensor_copy(kmb, ps[1][:, 0:C]))

                def body(i):
                    for u in range(2):
                        t = i * 2 + u
                        V.wait(s_km, t - 1)
                        e.wait_ge(s_ki[u], 16 * (i + 1))
                        vec.tensor_tensor(km[u], kin[u][:, 0:C], kmb, ALU.subtract).then_inc(s_ks, 1)
                        ts(kx[u], kin[u][:, 512:770], cst[:, ds(C_VALID + t, 1)], ALU.mult).then_inc(s_kv, 1)
                V.loop(NT // 2, body)
                e.wait_ge(s_km, NT)
                V.link(vec.memset(KX, 0.0))
                for c in range(2):
                    V.link(vec.reciprocal(den[:, c:c + 1], ps[2 + c][:, P:P + 1]))
                    for j in range(4):
                        o = slice(j * HD, (j + 1) * HD)
                        V.link(vec.tensor_scalar(KX[o, c * P + j * HD:c * P + (j + 1) * HD], ps[2 + c][o, o],
                                                 den[o, c:c + 1], None, ALU.mult))
                e.sem_inc(s_kd, 1)
                e.wait_ge(s_k4, 1)
                vec.tensor_copy(KXT, ps[4][:, 0:C]).then_inc(s_kd, 1)
                e.wait_ge(s_k4, 2)
                V.link(vec.tensor_copy(M, ps[5][:, :]))

            @block.scalar
            def _(e):
                A.e = e

                def body(i):
                    for u in range(2):
                        e.wait_ge(s_ks, i * 2 + u + 1)
                        act.activation(km[u], km[u], ACT.Exp).then_inc(s_ke, 1)
                A.loop(NT // 2, body)

            @block.tensor
            def _(e):
                T.e = e
                for c in range(2):
                    last = pe.transpose(ps[0][:, c * P:(c + 1) * P], kmax[:, c * P:(c + 1) * P], ident)
                last.then_inc(s_k1, 1)
                for c in range(2):
                    e.wait_ge(s_k2, c + 1)
                    pe.matmul(ps[1][:, c * P:(c + 1) * P], ones, dg, start=True, stop=True).then_inc(s_k3, 1)

                def body(i):
                    for u in range(2):
                        t = i * 2 + u
                        first = isinstance(i, int) and i == 0 and u == 0
                        final = isinstance(i, int) and i == NT // 2 - 1 and u == 1
                        e.wait_ge(s_ke, t + 1)
                        e.wait_ge(s_kv, t + 1)
                        for c in range(2):
                            last = pe.matmul(ps[2 + c][:, 0:P + 1], km[u][:, c * P:(c + 1) * P],
                                             kx[u][:, c * 129:(c + 1) * 129], start=first, stop=final)
                        last.then_inc(s_km, 1)
                T.loop(NT // 2, body, last=True)
                e.wait_ge(s_kd, 1)
                for c in range(2):
                    last = pe.transpose(ps[4][:, c * P:(c + 1) * P], KX[:, c * P:(c + 1) * P], ident)
                last.then_inc(s_k4, 1)
                e.wait_ge(s_kd, 2)
                for c in range(2):
                    last = pe.matmul(ps[5][:, c * C:(c + 1) * C], KXT[:, c * P:(c + 1) * P],
                                     Pm[:, c * C:(c + 1) * C], start=True, stop=True)
                last.then_inc(s_k4, 1)

        H_off = 16384
        hall = ar(H_off, NT * C)
        qin = [ar(C * j, C) for j in range(2)]
        qT = [ar(512 + C * j, C) for j in range(2)]
        z2 = [ar(1024 + C * j, C) for j in range(2)]
        z2T = ar(1536, 512)
        hT = ar(2048, 8 * C)
        rows1 = ar(4608, C, 1)
        rows2 = ar(4864, C, 1)
        s_rw = sem("rows")
        s_qi = sems("q_in", 2)
        s_qt, s_qc, s_at, s_h = sem("q_transposed"), sem("qT"), sem("attn_mm"), sem("h_out")
        sv3, sq3 = sem("var"), sem("root")
        s_z, s_zt, s_zc, s_m1, s_ge, s_m2, s_ad = (sem(n) for n in
            ("z2", "z2_transposed", "z2T", "mlp1", "gelu", "mlp2", "mlp_added"))
        with nc.Block() as block:
            @block.sync
            def _(e):
                S.e = e
                e.dma_start(rows1, a["bo"]).then_inc(s_rw, 16)
                e.dma_start(rows2, a["mb2"]).then_inc(s_rw, 16)

                def body(i):
                    for u in range(2):
                        t = i * 2 + u
                        S.wait(s_qt, t - 1)
                        e.dma_start(qin[u], mixd[ds(t * P, P), C:2 * C]).then_inc(s_qi[u], 16)
                S.loop(NT // 2, body)
                for u in range(2):
                    e.wait_ge(s_qi[u], 16 * NT // 2)

            @block.vector
            def _(e):
                V.e = e

                def attn(i):
                    for u in range(2):
                        t = i * 2 + u
                        e.wait_ge(s_at, t + 1)
                        vec.tensor_tensor(hall[:, ds(t * C, C)], ps[2 + u][:, 0:C], xn[:, ds(t * C, C)],
                                          ALU.add).then_inc(s_h, 1)
                V.loop(NT // 2, attn)
                e.wait_ge(s_h, NT)
                norm_stats(hall, mean, rstd, sv3, sq3)

                def mlp(i):
                    V.wait(s_zt, i)
                    for u in range(2):
                        t = i * 2 + u
                        norm_apply(z2[u], t, hall, mean, rstd).then_inc(s_z, 1)
                    e.wait_ge(s_zt, i + 1)
                    V.wait(s_m1, 8 * i)
                    for k in range(2):
                        V.link(ts(z2T[:, k * C:(k + 1) * C], ps[0][:, k * C:(k + 1) * C],
                                  lncol[:, 4 + k:5 + k], ALU.mult, lncol[:, 6 + k:7 + k], ALU.add))
                    e.sem_inc(s_zc, 1)
                    for u in range(2):
                        t = i * 2 + u
                        e.wait_ge(s_m2, t + 1)
                        V.link(vec.tensor_tensor(X1[:, ds(t * C, C)], X1[:, ds(t * C, C)],
                                                 ps[6 + u][:, 0:C], ALU.add))
                        vec.tensor_tensor(X1[:, ds(t * C, C)], X1[:, ds(t * C, C)], hall[:, ds(t * C, C)],
                                          ALU.add).then_inc(s_ad, 1)
                V.loop(NT // 2, mlp)

            @block.scalar
            def _(e):
                A.e = e

                def attn(i):
                    for u in range(2):
                        t = i * 2 + u
                        e.wait_ge(s_qt, t + 1)
                        A.wait(s_at, t - 1)
                        act.activation(qT[u], ps[u][:, 0:C], ACT.Copy).then_inc(s_qc, 1)
                A.loop(NT // 2, attn)
                norm_root(sv3, sq3)

                def mlp(i):
                    A.wait(s_m2, 2 * i)
                    for j in range(8):
                        e.wait_ge(s_m1, 8 * i + j + 1)
                        act.activation(hT[:, j * C:(j + 1) * C], ps[1 + j % 4][:, 0:C], ACT.Gelu,
                                       bias=b1col[:, j:j + 1]).then_inc(s_ge, 1)
                A.loop(NT // 2, mlp)

            @block.tensor
            def _(e):
                T.e = e
                e.wait_ge(s_rw, 32)

                def attn(i):
                    for u in range(2):
                        t = i * 2 + u
                        e.wait_ge(s_qi[u], 16 * (i + 1))
                        T.wait(s_qc, t - 1)
                        for c in range(2):
                            last = pe.transpose(ps[u][:, c * P:(c + 1) * P], qin[u][:, c * P:(c + 1) * P], ident)
                        last.then_inc(s_qt, 1)
                        e.wait_ge(s_qc, t + 1)
                        T.wait(s_h, t - 1)
                        for c in range(2):
                            pe.matmul(ps[2 + u][:, 0:C], qT[u][:, c * P:(c + 1) * P], M[:, c * C:(c + 1) * C],
                                      start=(c == 0), stop=False)
                        pe.matmul(ps[2 + u][:, 0:C], one_row, rows1, start=False, stop=True).then_inc(s_at, 1)
                T.loop(NT // 2, attn)

                def mlp(i):
                    e.wait_ge(s_z, 2 * i + 2)
                    T.wait(s_zc, i)
                    for k in range(2):
                        for u in range(2):
                            last = pe.transpose(ps[0][:, k * C + u * P:k * C + (u + 1) * P],
                                                z2[u][:, k * P:(k + 1) * P], ident)
                    last.then_inc(s_zt, 1)
                    e.wait_ge(s_zc, i + 1)
                    for j in range(8):
                        T.wait(s_ge, 8 * i + j - 3)
                        for k in range(2):
                            w1 = ar(W1T_off + k * HID + j * P, P)
                            last = pe.matmul(ps[1 + j % 4][:, 0:C], w1, z2T[:, k * C:(k + 1) * C],
                                             start=(k == 0), stop=(k == 1))
                        last.then_inc(s_m1, 1)
                    e.wait_ge(s_ge, 8 * i + 8)
                    T.wait(s_ad, 2 * i)
                    for u in range(2):
                        for j in range(8):
                            pe.matmul(ps[6 + u][:, 0:C], hT[:, j * C + u * P:j * C + (u + 1) * P],
                                      ar(W2T_off + j * C, C), start=(j == 0), stop=False)
                        pe.matmul(ps[6 + u][:, 0:C], one_row, rows2, start=False, stop=True).then_inc(s_m2, 1)
                T.loop(NT // 2, mlp)

        W = C + 1
        ACC = [0, 6784]
        U = 8
        msg = [ar(16384 + j * 260, W) for j in range(U)]
        oh = [ar(18688 + j * P, P) for j in range(U)]
        rb = [ar(20000 + j * C, C) for j in range(3)]
        slots = [ar(20800 + d * 2 * TE, 2 * TE) for d in range(2)]
        gmapi = [ar(22560 + d * TE, TE, 1).bitcast(i32) for d in range(2)]
        scr = ar(24576, NT * C)
        s_ga = sems("gather", U)
        s_pm, s_oh, s_sm, s_ac, s_bi, s_st, s_sl = (sem(n) for n in
            ("pool_copies", "onehot", "segment_mm", "accumulated", "bias_in", "acc_zero", "slots_in"))
        with nc.Block() as block:
            @block.gpsimd
            def _(e):
                G.e = e
                e.wait_ge(s_st, 1)
                e.wait_ge(s_sl, 64)
                for d in range(2):
                    def body(i, d=d):
                        for h in range(2):
                            g0 = d * TE
                            G.wait(s_sm, g0 + i * U + 4 * h - 4)
                            G.settle()
                            nc.gpsimd.tensor_copy(ist[h][:, :], slots[d][:, ds(i * 2 * U + 8 * h, 8)].bitcast(i32).rearrange(
                                "p (t two) -> p t two", two=2)[:, :, 0]).then_inc(s_pm, 1)
                            e.wait_ge(s_pm, d * (TE // 4) + 2 * i + h + 1)
                            G.settle()
                            for u in range(4):
                                e.indirect_dma_start(msg[4 * h + u][:, 0:C], None, table[d],
                                                     bass.IndirectOffsetOnAxis(ap=ist[h][:, u:u + 1], axis=0)
                                                     ).then_inc(s_ga[4 * h + u], 16)
                    G.loop(TE // U, body)

            @block.sync
            def _(e):
                for d in range(2):
                    e.dma_start(slots[d].bitcast(i32),
                                slotd[d].rearrange("(p t) two -> p (t two)", p=P)).then_inc(s_sl, 16)
                    e.dma_start(gmapi[d], gmapd[d]).then_inc(s_sl, 16)
                e.wait_ge(s_sl, 64)
                for j, k in enumerate(("self_b", "fwd_b", "bwd_b")):
                    e.dma_start(rb[j], a[k].broadcast_to([P, C])).then_inc(s_bi, 16)
                e.wait_ge(s_bi, 48)

            @block.vector
            def _(e):
                V.e = e
                for d in range(2):
                    V.link(vec.memset(ar(ACC[d], NT * W), 0.0))
                for u in range(U):
                    V.link(vec.memset(msg[u][:, C:W], 1.0))
                e.sem_inc(s_st, 1)
                e.wait_ge(s_sl, 64)
                V.settle()
                for d in range(2):
                    acc = ar(ACC[d], NT * W)
                    lo = slots[d]

                    def body(i, d=d, acc=acc, lo=lo):
                        n0 = d * TE + i * U
                        for u in range(U):
                            V.wait(s_sm, n0 + u - U + 1)
                            ts(oh[u], iota, lo[:, ds((i * U + u) * 2 + 1, 1)], ALU.is_equal).then_inc(s_oh, 1)
                        for u in range(U):
                            g = e.value_load(gmapi[d][0:1, ds(i * U + u, 1)], min_val=0, max_val=(NT - 1) * W)
                            e.wait_ge(s_sm, n0 + u + 1)
                            V.wait(s_ac, n0 + u)
                            vec.tensor_tensor(acc[:, ds(g, W)], acc[:, ds(g, W)], ps[u][:, 0:W],
                                              ALU.add).then_inc(s_ac, 1)
                    V.loop(TE // U, body)
                e.wait_ge(s_ac, 2 * TE)
                e.wait_ge(s_bi, 48)
                x3 = X1[:, :].rearrange("p (t c) -> p t c", c=C)
                s3 = scr.rearrange("p (t c) -> p t c", c=C)

                def spread(v):
                    return v.unsqueeze(2).broadcast_to([P, NT, C])

                def rows(v):
                    return v.unsqueeze(1).broadcast_to([P, NT, C])

                for d in range(2):
                    a3 = ar(ACC[d], NT * W).rearrange("p (t c) -> p t c", c=W)
                    V.link(ts(v1, a3[:, :, C], 1.0, ALU.max))
                    V.link(vec.reciprocal(v1, v1))
                    V.link(ts(v2, a3[:, :, C], 1.0, ALU.min))
                    V.link(vec.tensor_tensor(s3, a3[:, :, 0:C], spread(v1), ALU.mult))
                    V.link(vec.tensor_tensor(x3, x3, s3, ALU.add))
                    V.link(vec.tensor_tensor(s3, rows(rb[1 + d]), spread(v2), ALU.mult))
                    V.link(vec.tensor_tensor(x3, x3, s3, ALU.add))
                V.link(vec.tensor_tensor(x3, x3, rows(rb[0]), ALU.add))

            @block.tensor
            def _(e):
                T.e = e
                for d in range(2):
                    def body(i, d=d):
                        n0 = d * TE + i * U
                        for u in range(U):
                            e.wait_ge(s_ga[u], 16 * (d * (TE // U) + i + 1))
                            e.wait_ge(s_oh, n0 + u + 1)
                            T.wait(s_ac, n0 + u - U + 1)
                            pe.matmul(ps[u][:, 0:W], oh[u], msg[u], start=True, stop=True).then_inc(s_sm, 1)
                    T.loop(TE // U, body)

        WE1, WE2 = 0, 16384
        lgt = work[:, 2640:2640 + NT * NX]
        xk = [work[:, j * 768:j * 768 + C] for j in range(2)]
        xkT = [work[:, j * 768 + C:j * 768 + 2 * C] for j in range(2)]
        xg = [work[:, j * 768 + 2 * C:(j + 1) * 768] for j in range(2)]
        so[0] = 0
        st, mean, rstd, mean2, rstd2, v1, v2, v3 = (sm(n) for n in (NT * 6,) + (NT,) * 7)
        cnt, tot, til, base, incl = (sm(NT) for _ in range(5))
        wgt = sm(2 * NT)
        gsel = sm(2 * NX * 2)
        key52, tmp52, scan52, pos52, posf = (sm(2 * NT) for _ in range(5))
        wr = sm(2 * NX)
        br = sm(NX, 1)
        L = NT * NX
        lg2, eq, oh1 = work[:, 1536:1536 + L], work[:, 1744:1744 + L], work[:, 1952:1952 + L]
        gx, gxi = work[:, 2160:2160 + TX], sm(TX, 1).bitcast(i32)
        adr52, tok52 = work[:, 2220:2272].bitcast(i32), work[:, 2272:2324].bitcast(i32)
        tA, tB = work[:, 2324:2376].bitcast(i32), work[:, 2376:2428].bitcast(i32)
        pos_i = work[:, 2428:2480].bitcast(i32)
        xsl = work[:, 2480:2480 + TX].bitcast(i32)
        sv4, sq4, sv5, sq5 = sem("var"), sem("root"), sem("var"), sem("root")
        s_w, s_wx, s_xk, s_xt, s_xc, s_lg, s_le = (sem(n) for n in
            ("small_in", "experts_in", "token_tile", "token_T", "token_T_out", "logits", "logits_out"))
        s_xo = sems("token_rows", 2)
        s_c5, s_t5, s_d, s_dw = sem("counts"), sem("totals"), sem("difference"), sem("ratio")
        s_gf, s_xd = sem("slots_ready"), sem("slot_dma")
        scan_buf = scan52
        with nc.Block() as block:
            @block.sync
            def _(e):
                S.e = e
                for c in range(2):
                    e.dma_start(wr[:, c * NX:(c + 1) * NX], a["Wr"][c * P:(c + 1) * P, :]).then_inc(s_w, 16)
                e.dma_start(br, a["br"]).then_inc(s_w, 16)
                e.dma_start(gsel[:, 0:2 * NX], a["lng"]).then_inc(s_w, 16)
                e.dma_start(gsel[:, 2 * NX:4 * NX], a["lnb"]).then_inc(s_w, 16)
                for x in range(NX):
                    for k in range(2):
                        e.dma_start(ar(WE1 + k * 8192 + x * HID, HID),
                                    a["W1"][x * C + k * P:x * C + (k + 1) * P, :]).then_inc(s_wx, 16)
                    e.dma_start(ar(WE2 + x * 2048, 2048).rearrange("p (j c) -> p j c", c=C),
                                a["W2"][x * HID:(x + 1) * HID, :].rearrange("(j p) c -> p j c", p=P)
                                ).then_inc(s_wx, 16)

                def body(i):
                    for u in range(2):
                        t = i * 2 + u
                        e.wait_ge(s_xk, t * 2 + 2)
                        e.dma_start(xtok[ds(t * P, P), :], xg[u]).then_inc(s_xo[u], 16)
                S.loop(NT // 2, body)
                for u in range(2):
                    e.wait_ge(s_xo[u], 16 * NT // 2)
                e.wait_ge(s_w, 5 * 16)
                e.wait_ge(s_wx, 24 * 16)

            @block.vector
            def _(e):
                V.e = e
                norm_stats(X1, mean, rstd, sv4, sq4)
                V.loop(NT, lambda t: V.link(norm_apply(xn[:, ds(t * C, C)], t, X1, mean, rstd)))
                norm_stats(xn, mean2, rstd2, sv5, sq5)

                def body(i):
                    for u in range(2):
                        t = i * 2 + u
                        V.wait(s_xt, t - 1)
                        ts(xk[u], xn[:, ds(t * C, C)], 1.0, ALU.mult).then_inc(s_xk, 1)
                        V.wait(s_xo[u], 16 * i)
                        norm_apply(xg[u], t, xn, mean2, rstd2).then_inc(s_xk, 1)
                        e.wait_ge(s_xt, t + 1)
                        V.wait(s_lg, t - 1)
                        vec.tensor_copy(xkT[u], ps[u][:, 0:C]).then_inc(s_xc, 1)
                        e.wait_ge(s_lg, t + 1)
                        ts(lgt[:, ds(t * NX, NX)], ps[2 + u][:, 0:NX], 1.0, ALU.mult).then_inc(s_le, 1)
                V.loop(NT // 2, body)
                e.wait_ge(s_le, NT)
                lg3 = lgt.rearrange("p (t e) -> p t e", e=NX)
                l23, e3, o3 = (x.rearrange("p (t e) -> p t e", e=NX) for x in (lg2, eq, oh1))
                io = iota[:, 0:NX].unsqueeze(1).broadcast_to([P, NT, NX])

                def spread(v):
                    return v.unsqueeze(2).broadcast_to([P, NT, NX])

                def first_max(src, top, idx):
                    V.link(vec.tensor_reduce(top, src, AX.X, ALU.max))
                    V.link(vec.tensor_tensor(e3, src, spread(top), ALU.not_equal))
                    V.link(vec.scalar_tensor_tensor(e3, e3, 100.0, io, ALU.mult, ALU.add))
                    V.link(vec.tensor_reduce(idx, e3, AX.X, ALU.min))
                first_max(lg3, v1, key52[:, 0:NT])
                V.link(vec.tensor_tensor(o3, io, spread(key52[:, 0:NT]), ALU.is_equal))
                V.link(vec.scalar_tensor_tensor(l23, o3, -1.0e30, lg3, ALU.mult, ALU.add))
                first_max(l23, v2, key52[:, NT:2 * NT])
                vec.tensor_tensor(v2, v2, v1, ALU.subtract).then_inc(s_d, 1)
                e.wait_ge(s_dw, 1)
                V.link(ts(v1, v3, 1.0, ALU.add))
                V.link(vec.reciprocal(wgt[:, 0:NT], v1))
                V.link(vec.tensor_tensor(wgt[:, NT:2 * NT], wgt[:, 0:NT], v3, ALU.mult))
                vd = cst[:, C_VALID:C_VALID + NT]
                for j in range(2):
                    k_ = key52[:, j * NT:(j + 1) * NT]
                    V.link(ts(k_, k_, -float(NX), ALU.add))
                    V.link(vec.tensor_tensor(k_, k_, vd, ALU.mult))
                    V.link(ts(k_, k_, float(NX), ALU.add))
                    V.link(vec.tensor_copy(tok52[:, j * NT:(j + 1) * NT], cst[:, C_TOK:C_TOK + NT]))
                bin_positions(key52, 2 * NT, NX, pos52, tmp52, ones[:, 0:2 * NT], gx, TX, s_c5, s_t5)
                V.link(vec.tensor_copy(pos_i, pos52))
                slot_address(adr52, pos52, TX, tA, tB)
                V.link(vec.tensor_copy(posf, adr52))
                for j in range(2):
                    V.link(ts(tmp52[:, 0:NT], vd, -BIG, ALU.mult, BIG, ALU.add))
                    V.link(vec.tensor_tensor(posf[:, j * NT:(j + 1) * NT], posf[:, j * NT:(j + 1) * NT],
                                             tmp52[:, 0:NT], ALU.add))
                V.link(vec.tensor_copy(adr52, posf))
                V.link(vec.tensor_copy(gxi[0:1, :], gx[0:1, :]))
                V.link(vec.memset(xsl, 0))

            @block.scalar
            def _(e):
                A.e = e
                norm_root(sv4, sq4)
                norm_root(sv5, sq5)
                e.wait_ge(s_d, 1)
                act.activation(v3, v2, ACT.Exp).then_inc(s_dw, 1)

            @block.tensor
            def _(e):
                T.e = e
                e.wait_ge(s_w, 5 * 16)

                def body(i):
                    for u in range(2):
                        t = i * 2 + u
                        e.wait_ge(s_xk, t * 2 + 1)
                        T.wait(s_xc, t - 1)
                        for k in range(2):
                            last = pe.transpose(ps[u][:, k * P:(k + 1) * P], xk[u][:, k * P:(k + 1) * P], ident)
                        last.then_inc(s_xt, 1)
                        e.wait_ge(s_xc, t + 1)
                        T.wait(s_le, t - 1)
                        for k in range(2):
                            pe.matmul(ps[2 + u][:, 0:NX], xkT[u][:, k * P:(k + 1) * P],
                                      wr[:, k * NX:(k + 1) * NX], start=(k == 0), stop=False)
                        pe.matmul(ps[2 + u][:, 0:NX], one_row, br, start=False, stop=True).then_inc(s_lg, 1)
                T.loop(NT // 2, body)
                bin_counts(NX, s_c5, s_t5)

        s_y = sem("slot_default")
        s_l4 = sems("last_scatter", 4)
        b1e, b2e = xn[0:NX, 4608:4608 + HID], xn[0:NX, 5632:5632 + C]
        s_be = sem("expert_biases")
        with nc.Block() as block:
            @block.sync
            def _(e):
                e.dma_start(b1e, a["b1"]).then_inc(s_be, 16)
                e.dma_start(b2e, a["b2"]).then_inc(s_be, 16)
                e.wait_ge(s_be, 32)

            @block.gpsimd
            def _(e):
                G.e = e
                xv = xslotd.rearrange("(p t) o -> p (t o)", p=P)
                e.dma_start(xv, xsl).then_inc(s_y, 16)
                e.wait_ge(s_y, 16)
                n = bin_edges(e, 48, xslotd, adr52, tok52, 1, 4 * 2 * (EC // 8), bound=P * TX - 1)
                for u in range(4):
                    e.indirect_dma_start(xslotd, bass.IndirectOffsetOnAxis(ap=adr52[:, 48 + u:49 + u], axis=0),
                                         tok52[:, 48 + u:49 + u], None, bounds_check=P * TX - 1,
                                         oob_is_err=False).then_inc(s_l4[u], 16)
                for u in range(4):
                    e.wait_ge(s_l4[u], 16)
                e.dma_start(xsl, xv).then_inc(s_y, 16)
                e.wait_ge(s_y, 32)

        xT7 = xk
        sel = [xkT[u][0:NX, 0:P] for u in range(2)]
        XB = xn[:, 0:4608]
        hb = [XB[:, j * HID:(j + 1) * HID] for j in range(2)]
        hTb = [XB[:, 2048 + j * HID:2048 + (j + 1) * HID] for j in range(2)]
        yb = [XB[:, 4096 + j * C:4096 + (j + 1) * C] for j in range(2)]
        ist7 = [sb(f"ist7{u}", 1, i32) for u in range(2)]
        s_g7 = sems("token_gather", 2)
        s_i7, s_t7, s_x7, s_s7, s_h7, s_e7, s_r7, s_c7, s_y7, s_o7 = (sem(n) for n in
            ("index", "x_T", "x_T_out", "selector", "layer1", "gelu", "hidden_T", "hidden_T_out", "layer2", "y_out"))
        s_yd = sems("y_dma", 2)
        with nc.Block() as block:
            @block.gpsimd
            def _(e):
                G.e = e

                def body(i):
                    for u in range(2):
                        t = i * 2 + u
                        G.wait(s_t7, t - 1)
                        G.settle()
                        nc.gpsimd.tensor_copy(ist7[u][:, :], xsl[:, ds(t, 1)]).then_inc(s_i7, 1)
                        e.wait_ge(s_i7, t + 1)
                        G.settle()
                        e.indirect_dma_start(xg[u], None, xtok, bass.IndirectOffsetOnAxis(
                            ap=ist7[u][:, 0:1], axis=0)).then_inc(s_g7[u], 16)
                G.loop(TX // 2, body)

            @block.vector
            def _(e):
                V.e = e

                def body(i):
                    for u in range(2):
                        t = i * 2 + u
                        V.settle()
                        x = e.value_load(gxi[0:1, ds(t, 1)], min_val=0, max_val=NX - 1)
                        e.wait_ge(s_t7, t + 1)
                        V.wait(s_h7, t - 1)
                        for k in range(2):
                            V.link(ts(xT7[u][:, k * P:(k + 1) * P], ps[0][:, k * P:(k + 1) * P],
                                      gsel[:, ds(x + k * NX, 1)], ALU.mult,
                                      gsel[:, ds(x + (2 + k) * NX, 1)], ALU.add))
                        V.wait(s_y7, t - 1)
                        ts(sel[u], gx[0:NX, ds(t, 1)].broadcast_to([NX, P]), cst[0:NX, C_PID:C_PID + 1],
                           ALU.is_equal).then_inc(s_x7, 1)
                        e.wait_ge(s_r7, t + 1)
                        V.wait(s_y7, t - 1)
                        for k in range(2):
                            vec.tensor_copy(hTb[u][:, k * 512:(k + 1) * 512], ps[3 + k][:, :]).then_inc(s_c7, 1)
                        e.wait_ge(s_y7, t + 1)
                        V.wait(s_yd[u], 16 * i)
                        vec.tensor_copy(yb[u], ps[5][:, 0:C]).then_inc(s_o7, 1)
                V.loop(TX // 2, body)

            @block.scalar
            def _(e):
                A.e = e

                def body(i):
                    for u in range(2):
                        t = i * 2 + u
                        for c in range(2):
                            e.wait_ge(s_h7, t + 1)
                            A.wait(s_r7, t - 1)
                            act.activation(hb[u][:, c * 512:(c + 1) * 512], ps[1 + c][:, :],
                                           ACT.Gelu).then_inc(s_e7, 1)
                A.loop(TX // 2, body)

            @block.tensor
            def _(e):
                T.e = e

                def body(i):
                    for u in range(2):
                        t = i * 2 + u
                        T.wait(s_x7, t)
                        e.wait_ge(s_g7[u], 16 * (i + 1))
                        for k in range(2):
                            last = pe.transpose(ps[0][:, k * P:(k + 1) * P], xg[u][:, k * P:(k + 1) * P], ident)
                        last.then_inc(s_t7, 1)
                        e.wait_ge(s_x7, t + 1)
                        x = e.value_load(gxi[0:1, ds(t, 1)], min_val=0, max_val=NX - 1)
                        T.wait(s_e7, 2 * t)
                        for c in range(2):
                            for k in range(2):
                                pe.matmul(ps[1 + c][:, :], xT7[u][:, k * P:(k + 1) * P],
                                          arena[:, ds(x * HID + (WE1 + k * 8192 + c * 512), 512)],
                                          start=(k == 0), stop=False)
                            last = pe.matmul(ps[1 + c][:, :], sel[u], b1e[:, c * 512:(c + 1) * 512],
                                             start=False, stop=True)
                        last.then_inc(s_h7, 1)
                        e.wait_ge(s_e7, 2 * t + 2)
                        T.wait(s_c7, 2 * t)
                        for j in range(8):
                            last = pe.transpose(ps[3 + j // 4][:, (j % 4) * P:(j % 4 + 1) * P],
                                                hb[u][:, j * P:(j + 1) * P], ident)
                        last.then_inc(s_r7, 1)
                        e.wait_ge(s_c7, 2 * t + 2)
                        T.wait(s_o7, t)
                        for j in range(8):
                            pe.matmul(ps[5][:, 0:C], hTb[u][:, j * P:(j + 1) * P],
                                      arena[:, ds(x * 2048 + (WE2 + j * C), C)], start=(j == 0), stop=False)
                        pe.matmul(ps[5][:, 0:C], sel[u], b2e, start=False, stop=True).then_inc(s_y7, 1)
                T.loop(TX // 2, body)

            @block.sync
            def _(e):
                S.e = e

                def body(i):
                    for u in range(2):
                        t = i * 2 + u
                        e.wait_ge(s_o7, t + 1)
                        e.dma_start(yslot[ds(t * P, P), :], yb[u]).then_inc(s_yd[u], 16)
                S.loop(TX // 2, body)
                for u in range(2):
                    e.wait_ge(s_yd[u], 16 * TX // 2)

        pk = [[XB[:, (2 * j + u) * C:(2 * j + u + 1) * C] for j in range(2)] for u in range(2)]
        s_i8, s_u8, s_w8 = sem("index"), sem("first_added"), sem("second_added")
        s_g8 = [sems(f"pick{u}", 2) for u in range(2)]
        ist8 = [sb(f"ist8{u}", 2, i32) for u in range(2)]
        s_od = sems("out", 2)
        with nc.Block() as block:
            @block.gpsimd
            def _(e):
                G.e = e

                def body(i):
                    for u in range(2):
                        t = i * 2 + u
                        G.wait(s_w8, t - 1)
                        G.settle()
                        for j in range(2):
                            nc.gpsimd.tensor_copy(ist8[u][:, j:j + 1], pos_i[:, ds(t + j * NT, 1)]).then_inc(s_i8, 1)
                        e.wait_ge(s_i8, 2 * t + 2)
                        G.settle()
                        for j in range(2):
                            e.indirect_dma_start(pk[u][j], None, yslot, bass.IndirectOffsetOnAxis(
                                ap=ist8[u][:, j:j + 1], axis=0)).then_inc(s_g8[u][j], 16)
                G.loop(NT // 2, body)

            @block.vector
            def _(e):
                V.e = e

                def body(i):
                    for u in range(2):
                        t = i * 2 + u
                        xt_ = X1[:, ds(t * C, C)]
                        for j in range(2):
                            e.wait_ge(s_g8[u][j], 16 * (i + 1))
                            vec.scalar_tensor_tensor(xt_, pk[u][j], wgt[:, ds(t + j * NT, 1)], xt_, ALU.mult,
                                                     ALU.add).then_inc((s_u8, s_w8)[j], 1)
                            if j == 0:
                                e.wait_ge(s_u8, t + 1)
                V.loop(NT // 2, body)

            @block.sync
            def _(e):
                S.e = e

                def body(i):
                    for u in range(2):
                        t = i * 2 + u
                        e.wait_ge(s_w8, t + 1)
                        e.dma_start(out[ds(t * P, P), :], X1[:, ds(t * C, C)]).then_inc(s_od[u], 16)
                S.loop(NT // 2, body)
                for u in range(2):
                    e.wait_ge(s_od[u], 16 * NT // 2)


def kernel(**inputs):
    import numpy as np
    import concourse.bacc as bacc
    from concourse.bass_utils import run_bass_kernel_spmd as run

    g = {k: np.asarray(v) for k, v in inputs.items()}
    cols = lambda v: np.ascontiguousarray(v.reshape(-1, P).T)
    row = lambda v: v.reshape(1, -1)
    edge = lambda v, fill: np.concatenate([v, np.full(P * EC - E, fill, v.dtype)]).reshape(P, EC)
    x = g["x"]
    arrays = {
        "cst": constants(np),
        "x": np.concatenate([x, x[:NP - N]]),
        "src": edge(g["src"], N + P - 1), "dst": edge(g["dst"], N + P - 1), "et": edge(g["edge_type_16"], 0),
        "Wf": g["L0_gnn_Wf"].transpose(1, 0, 2).reshape(C, R * C),
        "Wb": g["L0_gnn_Wb"].transpose(1, 0, 2).reshape(C, R * C),
        "lw": g["L0_gnn_loop_weight"], "fwd_b": row(g["L0_gnn_forward_bias"]),
        "bwd_b": row(g["L0_gnn_backward_bias"]), "self_b": row(g["L0_gnn_self_bias"]),
        "ln1w": cols(g["L0_mix_ln1_w"]), "ln1b": cols(g["L0_mix_ln1_b"]),
        "ln2w": cols(g["L0_mix_ln2_w"]), "ln2b": cols(g["L0_mix_ln2_b"]),
        "Wx": g["L0_mix_Wx"], "WxT": g["L0_mix_Wx"].T, "bx": cols(g["L0_mix_bx"]), "bxrow": row(g["L0_mix_bx"]),
        "WqT": g["L0_mix_Wq"].T, "WkT": g["L0_mix_Wk"].T, "Wv": g["L0_mix_Wv"], "WoT": g["L0_mix_Wo"].T,
        "bo": row(g["L0_mix_bo"]), "mW1T": g["L0_mix_W1"].T, "mb1": cols(g["L0_mix_b1"]),
        "mW2T": g["L0_mix_W2"].T, "mb2": row(g["L0_mix_b2"]),
        "Wr": g["L0_ffn_Wr"], "br": row(g["L0_ffn_br"]),
        "lng": g["L0_ffn_ln_g"].reshape(NX, 2, P).transpose(2, 1, 0).reshape(P, 2 * NX),
        "lnb": g["L0_ffn_ln_b"].reshape(NX, 2, P).transpose(2, 1, 0).reshape(P, 2 * NX),
        "W1": g["L0_ffn_W1"].reshape(NX * C, HID), "b1": g["L0_ffn_b1"],
        "W2": g["L0_ffn_W2"].reshape(NX * HID, C), "b2": g["L0_ffn_b2"],
    }
    arrays = {f"in_{k}": np.ascontiguousarray(v) for k, v in arrays.items()}
    nc = bacc.Bacc("TRN2", target_bir_lowering=False, num_devices=1)
    a = {k[3:]: nc.dram_tensor(k, v.shape, mybir.dt.from_np(v.dtype), kind="ExternalInput").ap()
         for k, v in arrays.items()}
    out = nc.dram_tensor("out", (NP, C), f32, kind="ExternalOutput").ap()
    build(nc, a, out)
    return run(nc, [arrays], core_ids=[0]).results[0]["out"][:N]
```

```python
import concourse.bass as bass
from concourse import mybir

N, C, E, R = 3125, 256, 53125, 16
P = 128
NT = 26
NP = NT * P
EC = 416
HEADS, HD = 8, 32
HID = 1024
NX, TOPK = 8, 2
TE = (E + (NT - 1) * (P - 1)) // P + 1
TX = (N * TOPK + NX * (P - 1)) // P
EPS = 1e-5
BIG = 1.0e6

f32, i32, bf16 = mybir.dt.float32, mybir.dt.int32, mybir.dt.bfloat16
ALU, ACT, AX = mybir.AluOpType, mybir.ActivationFunctionType, mybir.AxisListType

C_ID, C_IOTA, C_TRI, C_ONE, C_VALID, C_TILE, C_PID = 0, 128, 256, 384, 512, 538, 978
C_TOK, C_ROW = 979, 979 + NT
C_N = C_ROW + 1


def constants(np):
    c = np.zeros((P, C_N), np.float32)
    p = np.arange(P)
    c[:, C_ID:C_ID + P] = np.eye(P)
    c[:, C_IOTA:C_IOTA + P] = p[None, :]
    c[:, C_TRI:C_TRI + P] = p[:, None] < p[None, :]
    c[:, C_ONE:C_ONE + P] = 1.0
    rows = np.arange(NT)[None, :] * P + p[:, None]
    c[:, C_VALID:C_VALID + NT] = rows < N
    c[:, C_TILE:C_TILE + TE] = np.arange(TE)[None, :]
    c[:, C_PID] = np.where((p < 96) & (p % 32 < NX), p % 32, -1)
    c[:, C_ROW] = (p < 96) & (p % 32 == 0)
    c[:, C_TOK:C_TOK + NT] = rows
    return c


class Engine:

    def __init__(self, e, ns, sem, pad):
        self.e, self.ns, self.sem, self.pad, self.n, self.reg = e, ns, sem, pad, 0, 0

    def wait(self, sem, value):
        if not (isinstance(value, int) and value <= 0):
            self.e.wait_ge(sem, value)

    def link(self, ins):
        ins.then_inc(self.sem, 1)
        self.n += 1
        self.e.wait_ge(self.sem, self.reg + self.n)

    def settle(self):
        self.e.sem_inc(self.pad, 1)

    def barrier(self, sem, n, parties=4):
        self.e.drain().then_inc(sem, 1)
        self.e.wait_ge(sem, parties * n)

    def loop(self, n, body, last=False, start=0):
        before = self.n
        body(start)
        per = self.n - before
        end = n - 1 if last else n
        with self.e.Fori(start + 1, end) as i:
            self.reg, self.n = (i - start) * per if per else 0, before
            body(i)
        self.reg, self.n = 0, before + (end - start) * per
        if last:
            body(n - 1)


def build(nc, a, out):
    from contextlib import ExitStack
    ctx = ExitStack()
    ds = bass.ds

    def dram(name, rows, cols, dt=f32):
        return nc.dram_tensor(name, (rows, cols), dt, kind="Internal").ap()

    table = [dram("table_fwd", NP * R, C), dram("table_bwd", NP * R, C)]
    mixd = dram("mix_rows", NP, 770)
    gmapd = [dram("bin_of_tile_fwd", 1, TE, i32), dram("bin_of_tile_bwd", 1, TE, i32)]
    slotd = [dram("slots_fwd", P * TE, 2, i32), dram("slots_bwd", P * TE, 2, i32)]
    xtok = dram("ffn_tokens", NP, C)
    xslotd = dram("ffn_slots", P * TX, 1, i32)
    yslot = dram("ffn_rows", P * TX, C)

    with ctx:
        def sb(name, cols, dt=f32, rows=P):
            return ctx.enter_context(nc.sbuf_tensor(name, [rows, cols], dt))

        nsem = [0]

        scope = []

        def sem(name, whole=False):
            nsem[0] += 1
            s_ = nc.alloc_semaphore(f"{name}_{nsem[0]}")
            if not whole:
                scope.append(s_)
            return s_

        def sems(name, n, whole=False):
            return [sem(f"{name}{i}", whole) for i in range(n)]

        def end_of_block():
            nc.clear_and_free_semaphores(list(scope))
            scope.clear()
            nc.all_engine_barrier()

        arena = sb("arena", 32768)
        X1 = sb("X1", NT * C)
        xn = sb("xn", NT * C)
        cst = sb("cst", C_N)
        work = sb("work", 3074)
        small = sb("small", 900)
        ps = [ctx.enter_context(nc.psum_tensor(f"bank{i}", [P, 512], f32)) for i in range(8)]
        ident, iota = cst[:, C_ID:C_ID + P], cst[:, C_IOTA:C_IOTA + P]
        tri, ones = cst[:, C_TRI:C_TRI + P], cst[:, C_ONE:C_ONE + P]

        def ar(off, n, rows=P):
            return arena[0:rows, off:off + n]

        W_off = 0
        STG = [16384, 20480]
        W1T_off, W2T_off = 24576, 26624
        PAY = [28672, 29504]
        ADR = [30336, 30752]
        WM_off = 31168
        so = [0]

        def sm(n, rows=P):
            so[0] += n
            return small[0:rows, so[0] - n:so[0]]

        st = sm(NT * 6)
        mean, rstd, mean2, rstd2 = sm(NT), sm(NT), sm(NT), sm(NT)
        v1, v2, v3 = sm(NT), sm(NT), sm(NT)
        lncol = sm(8)
        b1col = sm(8)
        kmT = sm(2)
        bxcol = sm(2)
        cnt, tot, til, base, incl, ends = (sm(NT) for _ in range(6))
        den = sm(2)
        rmax, rsum = sm(HEADS), sm(HEADS)
        dgw = sm(2 * NT)
        brow = sb("brow", 768, bf16, 96)
        rows_o = sb("rows_o", C, bf16, 96)
        rows_2 = sb("rows_2", C, bf16, 96)
        row_sel = sb("row_sel", P, bf16, 96)
        lw = sb("lw", 512)
        kmax = sb("kmax", C)

        s_v, s_a, s_p, s_g, s_s, s_pad = (sem(n, True) for n in ("dve", "act", "pe", "pool", "sp", "pad"))
        V = Engine(None, nc.vector, s_v, s_pad)
        A = Engine(None, nc.scalar, s_a, s_pad)
        T = Engine(None, nc.tensor, s_p, s_pad)
        G = Engine(None, nc.gpsimd, s_g, s_pad)
        S = Engine(None, nc.sync, s_s, s_pad)

        vec, act, pe = nc.vector, nc.scalar, nc.tensor

        def ts(out, in0, s1, op0, s2=None, op1=None):
            if op1 is None:
                return vec.tensor_scalar(out, in0, s1, None, op0)
            return vec.tensor_scalar(out, in0, s1, s2, op0, op1)

        def norm_stats(src, m, r, s_var, s_sqrt):
            def stats(t):
                V.settle()
                V.link(vec.bn_stats(st[:, ds(t * 6, 6)], src[:, ds(t * C, C)]))
            V.loop(NT, stats)
            q = st.rearrange("p (t s) -> p t s", s=6)
            me, ve, mo, vo = q[:, :, 1], q[:, :, 2], q[:, :, 4], q[:, :, 5]
            V.link(vec.tensor_tensor(m, me, mo, ALU.add))
            V.link(ts(m, m, 0.5, ALU.mult))
            V.link(vec.tensor_tensor(v1, me, mo, ALU.subtract))
            V.link(vec.tensor_tensor(v1, v1, v1, ALU.mult))
            V.link(vec.tensor_tensor(v2, ve, vo, ALU.add))
            V.link(ts(v2, v2, 1.0 / C, ALU.mult, EPS, ALU.add))
            vec.scalar_tensor_tensor(v1, v1, 0.25, v2, ALU.mult, ALU.add).then_inc(s_var, 1)
            V.e.wait_ge(s_sqrt, 1)
            V.link(vec.reciprocal(v2, v2))
            V.link(vec.tensor_tensor(v3, v2, v2, ALU.mult))
            V.link(vec.tensor_tensor(v3, v3, v1, ALU.mult))
            V.link(ts(v3, v3, -0.5, ALU.mult, 1.5, ALU.add))
            V.link(vec.tensor_tensor(r, v2, v3, ALU.mult))

        def norm_root(s_var, s_sqrt):
            A.e.wait_ge(s_var, 1)
            act.activation(v2, v1, ACT.Sqrt).then_inc(s_sqrt, 1)

        def norm_apply(dst, t, src, m, r):
            return vec.tensor_scalar(dst, src[:, ds(t * C, C)], m[:, ds(t, 1)], r[:, ds(t, 1)],
                                     ALU.subtract, ALU.mult)

        def bin_positions(key, cols, bins, pos, sets, s_cnt, s_tot, bank):
            c_, t_, l_, b_, i_, end = (x[:, 0:bins] for x in (cnt, tot, til, base, incl, ends))
            views = []
            for g0, g1, hit, run in sets:
                n = (g1 - g0) * cols
                h3, r3 = (x[:, 0:n].rearrange("p (g c) -> p g c", c=cols) for x in (hit, run))
                views.append((g0, g1, h3, r3))
                shape = [P, g1 - g0, cols]
                V.link(vec.tensor_tensor(h3, key.unsqueeze(1).broadcast_to(shape),
                                         iota[:, g0:g1].unsqueeze(2).broadcast_to(shape), ALU.is_equal))
                V.link(vec.tensor_tensor_scan(run[:, 0:n], hit[:, 0:n], hit[:, 0:n], 0.0, ALU.add, ALU.max))
                V.link(vec.tensor_copy(end[:, g0:g1], r3[:, :, cols - 1]))
                V.link(vec.tensor_copy(c_[:, g0:g1], end[:, g0:g1]))
                V.link(vec.tensor_tensor(c_[:, g0 + 1:g1], end[:, g0 + 1:g1], end[:, g0:g1 - 1], ALU.subtract))
            V.e.sem_inc(s_cnt, 1)
            V.e.wait_ge(s_tot, 1)
            V.link(vec.tensor_copy(t_, bank[:, 64:64 + bins]))
            V.link(ts(l_, t_, float(P - 1), ALU.add))
            ti = v1[:, 0:bins].bitcast(i32)
            V.link(vec.tensor_copy(ti, l_))
            V.link(vec.tensor_single_scalar(ti, ti, 7, op=ALU.arith_shift_right))
            V.link(vec.tensor_copy(l_, ti))
            V.link(vec.tensor_tensor_scan(i_, l_, l_, 0.0, ALU.add, ALU.max))
            V.link(vec.tensor_tensor(b_, i_, l_, ALU.subtract))
            V.link(ts(b_, b_, float(P), ALU.mult, -1.0, ALU.add))
            V.link(vec.tensor_tensor(b_, b_, bank[:, 0:bins], ALU.add))
            for n, (g0, g1, h3, r3) in enumerate(views):
                V.link(vec.tensor_tensor(b_[:, g0 + 1:g1], b_[:, g0 + 1:g1], end[:, g0:g1 - 1], ALU.subtract))
                V.link(vec.tensor_tensor(r3, r3, b_[:, g0:g1].unsqueeze(2).broadcast_to([P, g1 - g0, cols]),
                                         ALU.add))
                V.link(vec.tensor_tensor(r3, r3, h3, ALU.mult))
                part = views[0][3][:, 0, :] if n else pos
                V.link(vec.tensor_reduce(part, r3.rearrange("p g c -> p c g"), AX.X, ALU.add))
                if n:
                    V.link(vec.tensor_tensor(pos, pos, part, ALU.add))

        def bins_of_tiles(gmap, bins, tiles, rows):
            V.link(vec.memset(gmap, 0.0))

            def passed(g):
                V.link(vec.scalar_tensor_tensor(gmap, cst[0:rows, C_TILE:C_TILE + tiles],
                                                incl[0:rows, ds(g, 1)], gmap, ALU.is_ge, ALU.add))
            V.loop(bins, passed)
            V.link(ts(gmap, gmap, float(bins - 1), ALU.min))

        def three_parts(rows, raw, part):
            for j in range(3):
                o = slice(32 * j, 32 * j + 32)
                V.link(vec.tensor_copy(part, raw))
                for dst, c0, n in rows:
                    V.link(vec.tensor_copy(dst[o, :], part[o, c0:c0 + n]))
                if j < 2:
                    V.link(vec.tensor_tensor(raw, raw, part, ALU.subtract))

        def bin_counts(bins, s_cnt, s_tot, bank):
            T.e.wait_ge(s_cnt, 1)
            pe.matmul(bank[:, 0:bins], tri, cnt[:, 0:bins], start=True, stop=True)
            pe.matmul(bank[:, 64:64 + bins], ones, cnt[:, 0:bins], start=True,
                      stop=True).then_inc(s_tot, 1)

        def slot_address(dst, pos, tiles, ta, tb):
            V.link(vec.tensor_copy(ta, pos))
            V.link(vec.tensor_single_scalar(tb, ta, P - 1, op=ALU.bitwise_and))
            V.link(vec.tensor_single_scalar(ta, ta, 7, op=ALU.arith_shift_right))
            V.link(vec.scalar_tensor_tensor(dst, tb, float(tiles), ta, ALU.mult, ALU.add))

        HB = NT // 2
        bin_sets = [(0, HB, ar(25888, 2704).bitcast(bf16), ar(20480, HB * EC)),
                    (HB, NT, ar(8192, 2704).bitcast(bf16), ar(10896, HB * EC))]
        ei = [work[:, 1024 + j * EC:1024 + (j + 1) * EC].bitcast(i32) for j in range(3)]
        tmp_i = work[:, 1024 + 3 * EC:1024 + 4 * EC].bitcast(i32)
        gmap_s = work[0:1, 0:TE]
        gmap_row = work[0:1, 1024 + 3 * EC:1024 + 3 * EC + TE]
        BD, BDk, BDv = ar(0, P), ar(128, P), ar(256, P)
        WX, WOT = ar(384, 512), ar(896, 512)
        empty = ar(1408, 2 * TE)
        Pm = sb("Pm", 512)
        raw_rows = ar(2304, 1280, 96)
        part_rows = ar(3584, 640, 96).bitcast(bf16)

        ld, lde, ldf, ldb, ldx, ldw, zbd = (sem(n) for n in
            ("ld_small", "ld_edges", "ld_fold", "ld_blocks", "ld_x", "ld_tables", "zero"))
        s_em, s_ed = sem("empty_slots"), sem("slots_default")
        sc, stt = sems("counts", 2, True), sems("totals", 2, True)
        folded, fold_out = sem("folded"), sem("fold_out")

        def bin_edges_of(d):
            key, other = (ei[1], ei[0]) if d == 0 else (ei[0], ei[1])
            pay = ar(PAY[d], 2 * EC).bitcast(i32).rearrange("p (c two) -> p c two", two=2)
            payf = ar(PAY[d], 2 * EC).rearrange("p (c two) -> p c two", two=2)
            V.link(ts(tmp_i, other, float(R), ALU.mult))
            V.link(vec.tensor_tensor(pay[:, :, 0], tmp_i, ei[2], ALU.add))
            V.link(vec.tensor_single_scalar(tmp_i, key, P - 1, op=ALU.bitwise_and))
            V.link(vec.tensor_copy(payf[:, :, 1], tmp_i))
            V.link(vec.tensor_single_scalar(tmp_i, key, 7, op=ALU.arith_shift_right))
            bin_positions(tmp_i, EC, NT, ar(ADR[d], EC), bin_sets, sc[d], stt[d], ps[3 * d])
            slot_address(ar(ADR[d], EC).bitcast(i32), ar(ADR[d], EC), TE, tmp_i,
                         ar(20480, EC).bitcast(i32))

        def fwd_gmap(gm):
            bins_of_tiles(gm, NT, TE, 1)
            return ts(gm.bitcast(i32), gm, float(C + 1), ALU.mult)

        s_gm, s_gd = sem("bin_of_tile"), sem("bin_of_tile_dma", True)
        with nc.Block() as block:
            @block.sync
            def _(e):
                S.e = e
                for j, k in enumerate(("src", "dst", "et")):
                    e.dma_start(ei[j], a[k]).then_inc(lde, 16)
                small_loads = ((cst[:, :], a["cst"]), (lncol[:, 0:2], a["ln1w"]), (lncol[:, 2:4], a["ln1b"]),
                               (lncol[:, 4:6], a["ln2w"]), (lncol[:, 6:8], a["ln2b"]), (b1col, a["mb1"]),
                               (bxcol, a["bx"]))
                for o, i in small_loads:
                    e.dma_start(o, i).then_inc(ld, 16)
                for c in range(2):
                    cs = slice(c * P, (c + 1) * P)
                    e.dma_start(WX[:, c * C:(c + 1) * C], a["Wx"][cs, :]).then_inc(ldf, 16)
                    e.dma_start(WOT[:, c * C:(c + 1) * C], a["WoT"][cs, :]).then_inc(ldf, 16)
                    e.dma_start(lw[:, c * C:(c + 1) * C], a["lw"][cs, :]).then_inc(ldf, 16)
                    e.dma_start(ar(WM_off + c * 768 + 512, C), a["WxT"][cs, :]).then_inc(ldf, 16)
                for j, k in enumerate(("bxrow", "bo", "mb2")):
                    e.dma_start(raw_rows[:, 512 + j * C:512 + (j + 1) * C],
                                a[k].broadcast_to([96, C])).then_inc(ldf, 16)
                e.wait_ge(zbd, 3)
                for j in range(4):
                    o = slice(j * HD, (j + 1) * HD)
                    for m, k in ((BD, "WqT"), (BDk, "WkT"), (BDv, "Wv")):
                        e.dma_start(m[o, o], a[k]).then_inc(ldb, 16)
                e.wait_ge(s_em, 1)
                for d in range(2):
                    e.dma_start(slotd[d].rearrange("(p t) two -> p (t two)", p=P),
                                empty.bitcast(i32)).then_inc(s_ed, 16)
                e.dma_start(X1[:, :].rearrange("p (t c) -> p t c", c=C),
                            a["x"].rearrange("(t p) c -> p t c", p=P)).then_inc(ldx, 16)
                e.wait_ge(s_ed, 32)
                e.wait_ge(fold_out, 1)
                for c in range(2):
                    e.dma_start(ar(W_off + c * 4096, 4096), a["Wf"][c * P:(c + 1) * P, :]).then_inc(ldw, 16)
                e.wait_ge(s_gm, 1)
                e.dma_start(gmapd[0], gmap_s.bitcast(i32)).then_inc(s_gd, 16)
                e.wait_ge(s_gd, 16)
                e.wait_ge(ldw, 32)
                e.wait_ge(ldx, 16)

            @block.vector
            def _(e):
                V.e = e
                for m in (BD, BDk, BDv):
                    vec.memset(m, 0.0).then_inc(zbd, 1)
                V.link(vec.memset(empty, 0.0))
                vec.memset(empty.rearrange("p (t two) -> p t two", two=2)[:, :, 1], 999.0).then_inc(s_em, 1)
                e.wait_ge(ld, 7 * 16)
                V.link(vec.tensor_copy(row_sel[:, :], cst[0:96, C_ROW:C_ROW + 1].broadcast_to([96, P])))
                e.wait_ge(ldf, 11 * 16)
                e.wait_ge(folded, 1)
                for c in range(2):
                    V.link(vec.tensor_copy(ar(WM_off + c * 768, 512), ps[1 + c][:, :]))
                V.link(vec.tensor_copy(raw_rows[:, 0:512], ps[3][0:96, :]))
                V.link(vec.tensor_copy(Pm[:, :], ps[4][:, :]))
                three_parts([(brow, 0, 768), (rows_o, 768, C), (rows_2, 1024, C)], raw_rows, part_rows)
                e.sem_inc(fold_out, 1)
                e.wait_ge(lde, 48)
                bin_edges_of(0)
                fwd_gmap(gmap_s).then_inc(s_gm, 1)

            @block.tensor
            def _(e):
                T.e = e
                e.wait_ge(ld, 7 * 16)
                e.wait_ge(ldf, 11 * 16)
                e.wait_ge(ldb, 12 * 16)
                for i in range(2):
                    for m, bd in enumerate((BDk, BD)):
                        for c in range(2):
                            pe.matmul(ps[1 + i][:, m * C + c * P:m * C + (c + 1) * P],
                                      WX[:, c * C + i * P:c * C + (i + 1) * P], bd, start=True, stop=True)
                for m, bd in enumerate((BDk, BD)):
                    for c in range(2):
                        pe.matmul(ps[3][0:96, m * C + c * P:m * C + (c + 1) * P],
                                  bxcol[:, c:c + 1].broadcast_to([P, 96]), bd, start=True, stop=True)
                for c in range(2):
                    last = pe.matmul(ps[4][:, c * C:(c + 1) * C], BDv, WOT[:, c * C:(c + 1) * C],
                                     start=True, stop=True)
                last.then_inc(folded, 1)
                bin_counts(NT, sc[0], stt[0], ps[0])

        end_of_block()
        w = [0]

        def wk(n):
            w[0] += n
            return work[:, w[0] - n:w[0]]

        xs, xT, zs, zT = ([wk(C) for _ in range(2)] for _ in range(4))
        mst = wk(770)
        qx = wk(C)
        ist = [sb(f"ist{h}", 8, i32) for h in range(2)]
        pst = [sb(f"pst{h}", 16, i32) for h in range(2)]
        s_sc = sems("scatter", 8, True)
        s_cp = sem("copied", True)
        sc_base = [0]

        def bin_edges(e, count, table_dram, adr, pay, width, base_, bound=None):
            def body(i):
                for h in range(2):
                    for u in range(4):
                        G.wait(s_sc[4 * h + u], sc_base[0] + 16 * i)
                    G.settle()
                    c0 = i * 8 + 4 * h
                    nc.gpsimd.tensor_copy(ist[h][:, 0:4], adr[:, ds(c0, 4)]).then_inc(s_cp, 1)
                    nc.gpsimd.tensor_copy(pst[h][:, 0:4 * width],
                                          pay[:, ds(c0 * width, 4 * width)]).then_inc(s_cp, 1)
                    e.wait_ge(s_cp, base_ + 4 * i + 2 * h + 2)
                    G.settle()
                    for u in range(4):
                        kw = {} if bound is None else dict(bounds_check=bound, oob_is_err=False)
                        e.indirect_dma_start(table_dram, bass.IndirectOffsetOnAxis(ap=ist[h][:, u:u + 1], axis=0),
                                             pst[h][:, u * width:(u + 1) * width], None,
                                             **kw).then_inc(s_sc[4 * h + u], 16)
            G.loop(count // 8, body)
            sc_base[0] += 16 * (count // 8)
            for u in range(8):
                e.wait_ge(s_sc[u], sc_base[0])
            return base_ + 4 * (count // 8)

        def tiles(eng, step, after=None, job=None):
            def body(i):
                for u in range(2):
                    step(2 * i + u, i, u)
            if job is not None:
                eng.loop(after, body)
                job()
            eng.loop(NT // 2 - 1, body, start=after or 0)
            for u in range(2):
                step(NT - 2 + u, NT // 2 - 1, u)

        def has(t, n):
            return not (isinstance(t, int) and t + n >= NT)

        s_bar = sem("phase")
        sv1, sq1, sv2, sq2 = sem("var"), sem("root"), sem("var"), sem("root")
        s_xn, s_ixb, s_wb = sem("xn_ready"), sem("backward_addresses"), sem("backward_weights")
        pass_sems = [[sem(n) for n in ("tile_ready", "transposed", "transposes_out", "proj_mm", "proj_out",
                                       "tile_done")] for _ in range(2)]
        s_td = [sems("table_dma", 2) for _ in range(2)]
        s_mm, s_mrow, s_mdma, s_q, s_qe = (sem(n) for n in
            ("mix_mm", "mix_row", "mix_dma", "q_minus_max", "q_exp"))

        def evacuate(d, t, c):
            s_pj, s_po = pass_sems[d][3:5]
            if c % 4 == 0:
                A.wait(s_td[d][c // 4], 16 * t)
            A.e.wait_ge(s_pj, 8 * t + c + 1)
            act.activation(ar(STG[d] + c * 512, 512), ps[4 + c % 4][:, :], ACT.Copy).then_inc(s_po, 1)

        def project(d, t, u):
            s_pj, s_po, s_done = pass_sems[d][3:6]
            for c in range(8):
                T.wait(s_po, 8 * t + c - 3)
                for k in range(2):
                    last = pe.matmul(ps[4 + c % 4][:, :], xT[u][:, k * P:(k + 1) * P],
                                     ar(W_off + d * 8192 + k * 4096 + c * 512, 512),
                                     start=(k == 0), stop=(k == 1))
                last.then_inc(s_pj, 1)
            T.e.sem_inc(s_done, 1)

        tv = [tb.rearrange("(n r) c -> n (r c)", r=R) for tb in table]

        def store_rows(d, t):
            s_po = pass_sems[d][4]
            for h in range(2):
                S.e.wait_ge(s_po, 8 * t + 4 * h + 4)
                S.e.dma_start(tv[d][ds(t * P, P), h * 2048:(h + 1) * 2048],
                              ar(STG[d] + h * 2048, 2048)).then_inc(s_td[d][h], 16)

        kx = [work[:, j * 512:j * 512 + 258] for j in range(2)]
        km = [ar(512 * j, C) for j in range(2)]
        kin = [ar(1024 + 770 * j, 770) for j in range(2)]
        kmb = ar(3072, C)
        dg = ar(3328, P)
        KX, KXT = ar(3584, C), ar(3840, C)
        M = ar(5120, 512)
        s_k1, s_k2, s_k3, s_k4 = (sem("kmax_step") for _ in range(4))
        s_ki = sems("mix_in", 2)
        s_ks, s_ke, s_kv, s_km, s_kd = (sem(n) for n in
            ("k_minus_max", "k_exp", "xm_masked", "kv_mm", "kv_steps"))
        hall = ar(16384, NT * C)
        qin = [ar(C * j, C) for j in range(2)]
        qT = [ar(512 + C * j, C) for j in range(2)]
        s_qi = sems("q_in", 2)
        s_qt, s_qc, s_at, s_h = sem("q_transposed"), sem("qT"), sem("attn_mm"), sem("h_out")
        sv3, sq3 = sem("var"), sem("root")
        z2 = [Pm[:, j * C:(j + 1) * C] for j in range(2)]
        z2T = ar(13568, 512)
        hT = ar(14080, 8 * C)
        s_z, s_zt, s_zc, s_m1, s_ge, s_m2, s_ad = (sem(n) for n in
            ("z2", "z2_transposed", "z2T", "mlp1", "gelu", "mlp2", "mlp_added"))
        W = C + 1
        ACC = [0, 6784]
        U = 8
        NG = TE // U
        QUARTERS = 4
        msg = [ar(28672 + j * W, W) for j in range(15)] + [lw[:, 0:W]]
        oh = [work[:, j * P:(j + 1) * P] for j in range(16)]
        slots = [work[:, 2048:2048 + 2 * TE], ar(23040, 2 * TE)]
        gmapi = [xn[0:1, 1024 + d * TE:1024 + (d + 1) * TE].bitcast(i32) for d in range(2)]
        rb = [xn[:, j * C:(j + 1) * C] for j in range(3)]
        scr = hall
        s_ga = sems("gather", 2 * U)
        s_pm, s_oh, s_sm, s_ac, s_bi, s_st, s_sl, s_scd = (sem(n) for n in
            ("pool_copies", "onehot", "segment_mm", "accumulated", "bias_in", "acc_zero", "slots_in",
             "scattered"))

        class Group:
            def __init__(self, d, i, per, off):
                self.d, self.i, self.per, self.off = d, i, per, off
                self.n = i * per + off
                self.half = off % 2
                self.before = i * (per // 2) + off // 2
                self.tile = (self.n - NG * d) * U

            def next(self, d=None):
                return Group(self.d if d is None else d, self.i, self.per, self.off + 1)

        def gather_group(e, g):
            G.wait(s_sm, (g.n - 1) * U)
            G.settle()
            nc.gpsimd.tensor_copy(ist[g.half][:, :], slots[g.d][:, ds(g.tile * 2, 2 * U)].bitcast(i32).rearrange(
                "p (t two) -> p t two", two=2)[:, :, 0]).then_inc(s_pm, 1)
            e.wait_ge(s_pm, g.n + 1)
            G.settle()
            for u in range(U):
                b = U * g.half + u
                e.indirect_dma_start(msg[b][:, 0:C], None, table[g.d], bass.IndirectOffsetOnAxis(
                    ap=ist[g.half][:, u:u + 1], axis=0)).then_inc(s_ga[b], 16)

        def onehots(g):
            V.wait(s_sm, (g.n - 1) * U)
            for u in range(U):
                ts(oh[U * g.half + u], iota, slots[g.d][:, ds((g.tile + u) * 2 + 1, 1)],
                   ALU.is_equal).then_inc(s_oh, 1)

        def add_sums(e, g):
            acc = ar(ACC[g.d], NT * W)
            for u in range(U):
                n = g.n * U + u
                at = e.value_load(gmapi[g.d][0:1, ds(g.tile + u, 1)], min_val=0, max_val=(NT - 1) * W)
                e.wait_ge(s_sm, n + 1)
                V.wait(s_ac, n)
                vec.tensor_tensor(acc[:, ds(at, W)], acc[:, ds(at, W)], ps[4 + u % 4][:, 0:W],
                                  ALU.add).then_inc(s_ac, 1)

        def sum_tile(e, g, u):
            n, b = g.n * U + u, U * g.half + u
            e.wait_ge(s_ga[b], 16 * (g.before + 1))
            e.wait_ge(s_oh, n + 1)
            T.wait(s_ac, n - 3)
            pe.matmul(ps[4 + u % 4][:, 0:W], oh[b], msg[b], start=True, stop=True).then_inc(s_sm, 1)

        def sum_group(e, g):
            for u in range(U):
                sum_tile(e, g, u)

        def messages(eng, turn, group):
            eng.loop(NT // 2, lambda i: turn(i, [Group(0, i, QUARTERS, o) for o in range(QUARTERS)]))
            for o in range(NT // 2 * QUARTERS, NG):
                g = Group(0, 0, 2, o)
                group(g, g.next(1 if o == NG - 1 else 0))
            eng.loop(NG // 2, lambda i: [group(g, g.next()) for g in (Group(1, i, 2, NG), Group(1, i, 2, NG + 1))])
            group(Group(1, 0, 2, 2 * NG - 1), None)

        with nc.Block() as block:
            @block.gpsimd
            def _(e):
                G.e = e
                n = bin_edges(e, EC, slotd[0], ar(ADR[0], EC).bitcast(i32), ar(PAY[0], 2 * EC).bitcast(i32), 2, 0)
                e.wait_ge(s_ixb, 1)
                bin_edges(e, EC, slotd[1], ar(ADR[1], EC).bitcast(i32), ar(PAY[1], 2 * EC).bitcast(i32), 2, n)
                e.sem_inc(s_scd, 1)
                e.wait_ge(s_st, 1)
                e.wait_ge(s_sl, 80)
                messages(G, lambda i, gs: [gather_group(e, g) for g in gs], lambda g, nxt: gather_group(e, g))

            @block.sync
            def _(e):
                S.e = e
                pair = lambda i: [store_rows(0, i * 2 + u) for u in range(2)]
                S.loop(7, pair)
                e.wait_ge(s_ixb, 2)
                e.dma_start(gmapd[1], gmap_row.bitcast(i32)).then_inc(s_gd, 16)
                for c in range(2):
                    e.dma_start(ar(W_off + 8192 + c * 4096, 4096), a["Wb"][c * P:(c + 1) * P, :]).then_inc(s_wb, 16)
                    e.dma_start(ar(W1T_off + c * HID, HID), a["mW1T"][c * P:(c + 1) * P, :]).then_inc(s_wb, 16)
                for j in range(8):
                    e.dma_start(ar(W2T_off + j * C, C), a["mW2T"][j * P:(j + 1) * P, :]).then_inc(s_wb, 16)
                S.loop(NT // 2, pair, start=7)

                def second(i):
                    for u in range(2):
                        t = i * 2 + u
                        store_rows(1, t)
                        e.wait_ge(s_mrow, t + 1)
                        e.dma_start(mixd[ds(t * P, P), :], mst).then_inc(s_mdma, 16)
                S.loop(NT // 2, second)
                e.wait_ge(s_mdma, 16 * NT)
                for d in range(2):
                    for h in range(2):
                        e.wait_ge(s_td[d][h], 16 * NT)
                e.wait_ge(s_gd, 32)
                S.barrier(s_bar, 1)

                def mix_in(i):
                    for u in range(2):
                        t = i * 2 + u
                        S.wait(s_kv, t - 1)
                        S.wait(s_ks, t - 1)
                        e.dma_start(kin[u], mixd[ds(t * P, P), :]).then_inc(s_ki[u], 16)
                S.loop(NT // 2, mix_in)
                S.barrier(s_bar, 2)

                def q_in(i):
                    for u in range(2):
                        t = i * 2 + u
                        S.wait(s_qt, t - 1)
                        e.dma_start(qin[u], mixd[ds(t * P, P), C:2 * C]).then_inc(s_qi[u], 16)
                S.loop(NT // 2, q_in)
                S.barrier(s_bar, 3)
                for j, k in enumerate(("self_b", "fwd_b", "bwd_b")):
                    e.dma_start(rb[j], a[k].broadcast_to([P, C])).then_inc(s_bi, 16)
                e.wait_ge(s_scd, 1)
                for d in range(2):
                    e.dma_start(slots[d].bitcast(i32),
                                slotd[d].rearrange("(p t) two -> p (t two)", p=P)).then_inc(s_sl, 16)
                    e.dma_start(gmapi[d], gmapd[d]).then_inc(s_sl, 16)
                e.wait_ge(s_sl, 64)
                e.sem_inc(s_sl, 16)
                e.wait_ge(s_bi, 48)

            @block.vector
            def _(e):
                V.e = e
                norm_stats(X1, mean, rstd, sv1, sq1)
                V.loop(NT, lambda t: V.link(norm_apply(xn[:, ds(t * C, C)], t, X1, mean, rstd)))
                e.sem_inc(s_xn, 1)
                bin_edges_of(1)
                e.sem_inc(s_ixb, 1)
                V.link(fwd_gmap(gmap_row))
                e.sem_inc(s_ixb, 1)
                norm_stats(xn, mean2, rstd2, sv2, sq2)
                V.link(vec.memset(kmax[:, :], -3.0e38))
                V.link(vec.memset(mst[:, 512 + P:512 + P + 1], 1.0))
                V.link(vec.memset(mst[:, 769:770], 1.0))
                s_xs, s_tp, s_xT, _, _, s_done = pass_sems[1]

                def load_tile(t, u):
                    V.wait(s_tp, t - 1)
                    V.link(norm_apply(zs[u], t, xn, mean2, rstd2))
                    ts(xs[u], xn[:, ds(t * C, C)], 1.0, ALU.mult).then_inc(s_xs, 1)

                def transposes_out(t, u):
                    e.wait_ge(s_tp, t + 1)
                    V.wait(s_done, t - 1)
                    V.link(vec.tensor_copy(xT[u], ps[0][:, 0:C]))
                    for k in range(2):
                        V.link(ts(zT[u][:, k * P:(k + 1) * P], ps[0][:, C + k * P:C + (k + 1) * P],
                                  lncol[:, k:k + 1], ALU.mult, lncol[:, 2 + k:3 + k], ALU.add))
                    e.sem_inc(s_xT, 1)

                def mix_rows(t):
                    e.wait_ge(s_mm, t + 1)
                    V.link(vec.scalar_tensor_tensor(X1[:, ds(t * C, C)], ps[3][:, 0:C], 2.0,
                                                    X1[:, ds(t * C, C)], ALU.mult, ALU.add))
                    V.wait(s_mdma, 16 * t)
                    V.link(vec.tensor_tensor(kmax[:, :], kmax[:, :], ps[1][:, 0:C], ALU.max))
                    V.link(vec.tensor_copy(mst[:, 0:C], ps[1][:, 0:C]))
                    V.link(vec.tensor_copy(mst[:, 512:770].rearrange("p (k c) -> p k c", k=2)[:, :, 0:P],
                                           ps[2][:, 0:C].rearrange("p (k c) -> p k c", k=2)))
                    qv = ps[1][:, C:2 * C].rearrange("p (h s) -> p h s", s=HD)
                    qxv = qx.rearrange("p (h s) -> p h s", s=HD)
                    V.link(vec.tensor_reduce(rmax, qv, AX.X, ALU.max))
                    vec.tensor_tensor(qxv, qv, rmax.unsqueeze(2).broadcast_to([P, HEADS, HD]),
                                      ALU.subtract).then_inc(s_q, 1)
                    e.wait_ge(s_qe, t + 1)
                    V.link(vec.tensor_reduce(rsum, qxv, AX.X, ALU.add))
                    V.link(vec.reciprocal(rsum, rsum))
                    vec.tensor_tensor(mst[:, C:2 * C].rearrange("p (h s) -> p h s", s=HD), qxv,
                                      rsum.unsqueeze(2).broadcast_to([P, HEADS, HD]),
                                      ALU.mult).then_inc(s_mrow, 1)

                e.wait_ge(pass_sems[0][5], NT)
                load_tile(0, 0)
                load_tile(1, 1)
                transposes_out(0, 0)

                def second(t, i, u):
                    if has(t, 1):
                        transposes_out(t + 1, 1 - u)
                    if has(t, 2):
                        load_tile(t + 2, u)
                    mix_rows(t)
                tiles(V, second)
                V.barrier(s_bar, 1)

                e.wait_ge(s_k1, 1)
                V.link(vec.tensor_reduce(kmT, ps[0][:, 0:C].rearrange("p (c n) -> p c n", c=2), AX.X, ALU.max))
                for c in range(2):
                    ts(dg, ident, kmT[:, c:c + 1], ALU.mult).then_inc(s_k2, 1)
                    e.wait_ge(s_k3, c + 1)
                V.link(vec.tensor_copy(kmb, ps[1][:, 0:C]))

                def keys(i):
                    for u in range(2):
                        t = i * 2 + u
                        V.wait(s_km, t - 1)
                        e.wait_ge(s_ki[u], 16 * (i + 1))
                        vec.tensor_tensor(km[u], kin[u][:, 0:C], kmb, ALU.subtract).then_inc(s_ks, 1)
                        ts(kx[u], kin[u][:, 512:770], cst[:, ds(C_VALID + t, 1)], ALU.mult).then_inc(s_kv, 1)
                V.loop(NT // 2, keys)
                e.wait_ge(s_km, NT)
                V.link(vec.memset(KX, 0.0))
                for c in range(2):
                    V.link(vec.reciprocal(den[:, c:c + 1], ps[2 + c][:, P:P + 1]))
                    for j in range(4):
                        o = slice(j * HD, (j + 1) * HD)
                        V.link(vec.tensor_scalar(KX[o, c * P + j * HD:c * P + (j + 1) * HD], ps[2 + c][o, o],
                                                 den[o, c:c + 1], None, ALU.mult))
                e.sem_inc(s_kd, 1)
                e.wait_ge(s_k4, 1)
                vec.tensor_copy(KXT, ps[4][:, 0:C]).then_inc(s_kd, 1)
                e.wait_ge(s_k4, 2)
                V.link(vec.tensor_copy(M, ps[5][:, :]))
                V.barrier(s_bar, 2)

                def attn(i):
                    for u in range(2):
                        t = i * 2 + u
                        e.wait_ge(s_at, t + 1)
                        vec.tensor_tensor(hall[:, ds(t * C, C)], ps[2 + u][:, 0:C], xn[:, ds(t * C, C)],
                                          ALU.add).then_inc(s_h, 1)
                V.loop(NT // 2, attn)
                e.wait_ge(s_h, NT)
                V.barrier(s_bar, 3)

                for d in range(2):
                    V.link(vec.memset(ar(ACC[d], NT * W), 0.0))
                norm_stats(hall, mean, rstd, sv3, sq3)
                e.wait_ge(s_scd, 1)
                for m in msg:
                    V.link(vec.memset(m[:, C:W], 1.0))
                e.sem_inc(s_st, 1)
                e.wait_ge(s_sl, 80)
                onehots(Group(0, 0, QUARTERS, 0))

                def turn(i, gs):
                    V.wait(s_zt, i)
                    for u in range(2):
                        norm_apply(z2[u], i * 2 + u, hall, mean, rstd).then_inc(s_z, 1)
                    onehots(gs[1])
                    e.wait_ge(s_zt, i + 1)
                    V.wait(s_m1, 8 * i)
                    for k in range(2):
                        ts(z2T[:, k * C:(k + 1) * C], ps[0][:, k * C:(k + 1) * C], lncol[:, 4 + k:5 + k],
                           ALU.mult, lncol[:, 6 + k:7 + k], ALU.add).then_inc(s_zc, 1)
                    add_sums(e, gs[0])
                    for g in gs[1:]:
                        onehots(g.next())
                        add_sums(e, g)
                    for u in range(2):
                        xt = X1[:, ds((i * 2 + u) * C, C)]
                        e.wait_ge(s_m2, i * 2 + u + 1)
                        V.link(vec.tensor_tensor(xt, xt, ps[3][:, u * C:(u + 1) * C], ALU.add))
                        vec.tensor_tensor(xt, xt, hall[:, ds((i * 2 + u) * C, C)], ALU.add).then_inc(s_ad, 1)

                def group(g, nxt):
                    if nxt is not None:
                        onehots(nxt)
                    add_sums(e, g)
                messages(V, turn, group)
                e.wait_ge(s_ac, 2 * TE)
                e.wait_ge(s_ad, NT)
                e.wait_ge(s_bi, 48)
                x3 = X1[:, :].rearrange("p (t c) -> p t c", c=C)
                s3 = scr.rearrange("p (t c) -> p t c", c=C)

                def spread(v):
                    return v.unsqueeze(2).broadcast_to([P, NT, C])

                def rows(v):
                    return v.unsqueeze(1).broadcast_to([P, NT, C])

                for d in range(2):
                    a3 = ar(ACC[d], NT * W).rearrange("p (t c) -> p t c", c=W)
                    V.link(ts(v1, a3[:, :, C], 1.0, ALU.max))
                    V.link(vec.reciprocal(v1, v1))
                    V.link(ts(v2, a3[:, :, C], 1.0, ALU.min))
                    V.link(vec.tensor_tensor(s3, a3[:, :, 0:C], spread(v1), ALU.mult))
                    V.link(vec.tensor_tensor(x3, x3, s3, ALU.add))
                    V.link(vec.tensor_tensor(s3, rows(rb[1 + d]), spread(v2), ALU.mult))
                    V.link(vec.tensor_tensor(x3, x3, s3, ALU.add))
                V.link(vec.tensor_tensor(x3, x3, rows(rb[0]), ALU.add))

            @block.scalar
            def _(e):
                A.e = e
                norm_root(sv1, sq1)
                s_xs, s_tp, s_xT, _, _, s_done = pass_sems[0]

                def load_tile(t, u):
                    A.wait(s_tp, t - 1)
                    A.settle()
                    act.activation(xs[u], xn[:, ds(t * C, C)], ACT.Copy).then_inc(s_xs, 1)

                def transposes_out(t, u):
                    e.wait_ge(s_tp, t + 1)
                    A.wait(s_done, t - 1)
                    act.activation(xT[u], ps[0][:, 0:C], ACT.Copy).then_inc(s_xT, 1)

                e.wait_ge(s_xn, 1)
                load_tile(0, 0)
                load_tile(1, 1)
                transposes_out(0, 0)

                def first(t, i, u):
                    for c in range(8):
                        evacuate(0, t, c)
                        if c == 3:
                            if has(t, 1):
                                transposes_out(t + 1, 1 - u)
                            if has(t, 2):
                                load_tile(t + 2, u)
                tiles(A, first)
                norm_root(sv2, sq2)

                def second(t, i, u):
                    for c in range(8):
                        evacuate(1, t, c)
                        if c == 3:
                            e.wait_ge(s_q, t + 1)
                            act.activation(qx, qx, ACT.Exp).then_inc(s_qe, 1)
                tiles(A, second)
                A.barrier(s_bar, 1)

                def keys(i):
                    for u in range(2):
                        e.wait_ge(s_ks, i * 2 + u + 1)
                        act.activation(km[u], km[u], ACT.Exp).then_inc(s_ke, 1)
                A.loop(NT // 2, keys)
                A.barrier(s_bar, 2)

                def attn(i):
                    for u in range(2):
                        t = i * 2 + u
                        e.wait_ge(s_qt, t + 1)
                        A.wait(s_at, t - 1)
                        act.activation(qT[u], ps[u][:, 0:C], ACT.Copy).then_inc(s_qc, 1)
                A.loop(NT // 2, attn)
                A.barrier(s_bar, 3)
                norm_root(sv3, sq3)

                def mlp(i):
                    A.wait(s_m2, 2 * i)
                    for j in range(8):
                        e.wait_ge(s_m1, 8 * i + j + 1)
                        act.activation(hT[:, j * C:(j + 1) * C], ps[1 + j % 2][:, 0:C], ACT.Gelu,
                                       bias=b1col[:, j:j + 1]).then_inc(s_ge, 1)
                A.loop(NT // 2, mlp)

            @block.tensor
            def _(e):
                T.e = e

                def transpose_tile(d, t, u):
                    s_xs, s_tp, s_xT = pass_sems[d][0:3]
                    e.wait_ge(s_xs, t + 1)
                    T.wait(s_xT, t)
                    for k in range(2):
                        last = pe.transpose(ps[0][:, k * P:(k + 1) * P], xs[u][:, k * P:(k + 1) * P], ident)
                    if d == 1:
                        for k in range(2):
                            last = pe.transpose(ps[0][:, C + k * P:C + (k + 1) * P],
                                                zs[u][:, k * P:(k + 1) * P], ident)
                    last.then_inc(s_tp, 1)

                def first(t, i, u):
                    if has(t, 1):
                        transpose_tile(0, t + 1, 1 - u)
                    e.wait_ge(pass_sems[0][2], t + 1)
                    project(0, t, u)

                transpose_tile(0, 0, 0)
                tiles(T, first, 2, lambda: bin_counts(NT, sc[1], stt[1], ps[3]))
                e.wait_ge(s_wb, 12 * 16)
                transpose_tile(1, 0, 0)

                def second(t, i, u):
                    e.wait_ge(pass_sems[1][2], t + 1)
                    T.wait(s_mrow, t)
                    for k in range(2):
                        lz = zT[u][:, k * P:(k + 1) * P]
                        wm = WM_off + k * 768
                        pe.matmul(ps[1][:, :], lz, ar(wm, 512), start=(k == 0), stop=False)
                        pe.matmul(ps[2][:, 0:C], lz, ar(wm + 512, C), start=(k == 0), stop=False)
                        pe.matmul(ps[3][:, 0:C], xT[u][:, k * P:(k + 1) * P], lw[:, k * C:(k + 1) * C],
                                  start=(k == 0), stop=(k == 1))
                    pe.matmul(ps[1][:, :], row_sel[:, :], brow[:, 0:512], start=False, stop=True)
                    pe.matmul(ps[2][:, 0:C], row_sel[:, :], brow[:, 512:768], start=False,
                              stop=True).then_inc(s_mm, 1)
                    if has(t, 1):
                        transpose_tile(1, t + 1, 1 - u)
                    project(1, t, u)
                tiles(T, second)
                T.barrier(s_bar, 1)

                for c in range(2):
                    last = pe.transpose(ps[0][:, c * P:(c + 1) * P], kmax[:, c * P:(c + 1) * P], ident)
                last.then_inc(s_k1, 1)
                for c in range(2):
                    e.wait_ge(s_k2, c + 1)
                    pe.matmul(ps[1][:, c * P:(c + 1) * P], ones, dg, start=True, stop=True).then_inc(s_k3, 1)

                def keys(i):
                    for u in range(2):
                        t = i * 2 + u
                        first = isinstance(i, int) and i == 0 and u == 0
                        final = isinstance(i, int) and i == NT // 2 - 1 and u == 1
                        e.wait_ge(s_ke, t + 1)
                        e.wait_ge(s_kv, t + 1)
                        for c in range(2):
                            last = pe.matmul(ps[2 + c][:, 0:P + 1], km[u][:, c * P:(c + 1) * P],
                                             kx[u][:, c * 129:(c + 1) * 129], start=first, stop=final)
                        last.then_inc(s_km, 1)
                T.loop(NT // 2, keys, last=True)
                e.wait_ge(s_kd, 1)
                for c in range(2):
                    last = pe.transpose(ps[4][:, c * P:(c + 1) * P], KX[:, c * P:(c + 1) * P], ident)
                last.then_inc(s_k4, 1)
                e.wait_ge(s_kd, 2)
                for c in range(2):
                    last = pe.matmul(ps[5][:, c * C:(c + 1) * C], KXT[:, c * P:(c + 1) * P],
                                     Pm[:, c * C:(c + 1) * C], start=True, stop=True)
                last.then_inc(s_k4, 1)
                T.barrier(s_bar, 2)

                def attn(i):
                    for u in range(2):
                        t = i * 2 + u
                        e.wait_ge(s_qi[u], 16 * (i + 1))
                        T.wait(s_qc, t - 1)
                        for c in range(2):
                            last = pe.transpose(ps[u][:, c * P:(c + 1) * P], qin[u][:, c * P:(c + 1) * P], ident)
                        last.then_inc(s_qt, 1)
                        e.wait_ge(s_qc, t + 1)
                        T.wait(s_h, t - 1)
                        for c in range(2):
                            pe.matmul(ps[2 + u][:, 0:C], qT[u][:, c * P:(c + 1) * P], M[:, c * C:(c + 1) * C],
                                      start=(c == 0), stop=False)
                        pe.matmul(ps[2 + u][:, 0:C], row_sel[:, :], rows_o[:, :], start=False,
                                  stop=True).then_inc(s_at, 1)
                T.loop(NT // 2, attn)
                T.barrier(s_bar, 3)

                def turn(i, gs):
                    e.wait_ge(s_z, 2 * i + 2)
                    T.wait(s_zc, 2 * i)
                    for k in range(2):
                        for u in range(2):
                            last = pe.transpose(ps[0][:, k * C + u * P:k * C + (u + 1) * P],
                                                z2[u][:, k * P:(k + 1) * P], ident)
                    last.then_inc(s_zt, 1)
                    sum_group(e, gs[0])
                    e.wait_ge(s_zc, 2 * i + 2)
                    for j in range(8):
                        T.wait(s_ge, 8 * i + j - 1)
                        for k in range(2):
                            w1 = ar(W1T_off + k * HID + j * P, P)
                            last = pe.matmul(ps[1 + j % 2][:, 0:C], w1, z2T[:, k * C:(k + 1) * C],
                                             start=(k == 0), stop=(k == 1))
                        last.then_inc(s_m1, 1)
                        sum_tile(e, gs[1], j)
                    sum_group(e, gs[2])
                    e.wait_ge(s_ge, 8 * i + 8)
                    T.wait(s_ad, 2 * i)
                    for u in range(2):
                        for j in range(8):
                            pe.matmul(ps[3][:, u * C:(u + 1) * C], hT[:, j * C + u * P:j * C + (u + 1) * P],
                                      ar(W2T_off + j * C, C), start=(j == 0), stop=False)
                        pe.matmul(ps[3][:, u * C:(u + 1) * C], row_sel[:, :], rows_2[:, :], start=False,
                                  stop=True).then_inc(s_m2, 1)
                    sum_group(e, gs[3])
                messages(T, turn, lambda g, nxt: sum_group(e, g))

        end_of_block()
        WE1, WE2 = 0, 16384
        lgt = work[:, 2640:2640 + NT * NX]
        xk = [work[:, j * 768:j * 768 + C] for j in range(2)]
        xkT = [work[:, j * 768 + C:j * 768 + 2 * C] for j in range(2)]
        xg = [work[:, j * 768 + 2 * C:(j + 1) * 768] for j in range(2)]
        so[0] = 0
        st, mean, rstd, mean2, rstd2, v1, v2, v3 = (sm(n) for n in (NT * 6,) + (NT,) * 7)
        cnt, tot, til, base, incl, ends = (sm(NT) for _ in range(6))
        wgt = sm(2 * NT)
        gsel = sm(2 * NX * 2)
        key52, tmp52, pos52, posf = (sm(2 * NT) for _ in range(4))
        wr = sm(2 * NX)
        br = sm(NX, 1)
        L = NT * NX
        lg2, eq, oh1 = work[:, 1536:1536 + L], work[:, 1744:1744 + L], work[:, 1952:1952 + L]
        gx, gxi = work[:, 2160:2160 + TX], sm(TX, 1).bitcast(i32)
        adr52, tok52 = work[:, 2220:2272].bitcast(i32), work[:, 2272:2324].bitcast(i32)
        tA, tB = work[:, 2324:2376].bitcast(i32), work[:, 2376:2428].bitcast(i32)
        pos_i = work[:, 2428:2480].bitcast(i32)
        xsl = work[:, 2480:2480 + TX].bitcast(i32)
        sv4, sq4, sv5, sq5 = sem("var"), sem("root"), sem("var"), sem("root")
        s_w, s_wx, s_xk, s_xt, s_xc, s_lg, s_le = (sem(n) for n in
            ("small_in", "experts_in", "token_tile", "token_T", "token_T_out", "logits", "logits_out"))
        s_xo = sems("token_rows", 2)
        s_c5, s_t5, s_d, s_dw = sem("counts"), sem("totals"), sem("difference"), sem("ratio")
        s_gf, s_xd = sem("slots_ready"), sem("slot_dma")
        hit5, run5 = xk[0].bitcast(bf16), work[:, 768:768 + 2 * NT * NX]
        with nc.Block() as block:
            @block.sync
            def _(e):
                S.e = e
                for c in range(2):
                    e.dma_start(wr[:, c * NX:(c + 1) * NX], a["Wr"][c * P:(c + 1) * P, :]).then_inc(s_w, 16)
                e.dma_start(br, a["br"]).then_inc(s_w, 16)
                e.dma_start(gsel[:, 0:2 * NX], a["lng"]).then_inc(s_w, 16)
                e.dma_start(gsel[:, 2 * NX:4 * NX], a["lnb"]).then_inc(s_w, 16)
                for x in range(NX):
                    for k in range(2):
                        e.dma_start(ar(WE1 + k * 8192 + x * HID, HID),
                                    a["W1"][x * C + k * P:x * C + (k + 1) * P, :]).then_inc(s_wx, 16)
                    e.dma_start(ar(WE2 + x * 2048, 2048).rearrange("p (j c) -> p j c", c=C),
                                a["W2"][x * HID:(x + 1) * HID, :].rearrange("(j p) c -> p j c", p=P)
                                ).then_inc(s_wx, 16)

                def body(i):
                    for u in range(2):
                        t = i * 2 + u
                        e.wait_ge(s_xk, t * 2 + 2)
                        e.dma_start(xtok[ds(t * P, P), :], xg[u]).then_inc(s_xo[u], 16)
                S.loop(NT // 2, body)
                for u in range(2):
                    e.wait_ge(s_xo[u], 16 * NT // 2)
                e.wait_ge(s_w, 5 * 16)
                e.wait_ge(s_wx, 24 * 16)

            @block.vector
            def _(e):
                V.e = e
                norm_stats(X1, mean, rstd, sv4, sq4)
                V.loop(NT, lambda t: V.link(norm_apply(xn[:, ds(t * C, C)], t, X1, mean, rstd)))
                norm_stats(xn, mean2, rstd2, sv5, sq5)

                def body(i):
                    for u in range(2):
                        t = i * 2 + u
                        V.wait(s_xt, t - 1)
                        ts(xk[u], xn[:, ds(t * C, C)], 1.0, ALU.mult).then_inc(s_xk, 1)
                        V.wait(s_xo[u], 16 * i)
                        norm_apply(xg[u], t, xn, mean2, rstd2).then_inc(s_xk, 1)
                        e.wait_ge(s_xt, t + 1)
                        V.wait(s_lg, t - 1)
                        vec.tensor_copy(xkT[u], ps[u][:, 0:C]).then_inc(s_xc, 1)
                        e.wait_ge(s_lg, t + 1)
                        ts(lgt[:, ds(t * NX, NX)], ps[2 + u][:, 0:NX], 1.0, ALU.mult).then_inc(s_le, 1)
                V.loop(NT // 2, body)
                e.wait_ge(s_le, NT)
                lg3 = lgt.rearrange("p (t e) -> p t e", e=NX)
                l23, e3, o3 = (x.rearrange("p (t e) -> p t e", e=NX) for x in (lg2, eq, oh1))
                io = iota[:, 0:NX].unsqueeze(1).broadcast_to([P, NT, NX])

                def spread(v):
                    return v.unsqueeze(2).broadcast_to([P, NT, NX])

                def first_max(src, top, idx):
                    V.link(vec.tensor_reduce(top, src, AX.X, ALU.max))
                    V.link(vec.tensor_tensor(e3, src, spread(top), ALU.not_equal))
                    V.link(vec.scalar_tensor_tensor(e3, e3, 100.0, io, ALU.mult, ALU.add))
                    V.link(vec.tensor_reduce(idx, e3, AX.X, ALU.min))
                first_max(lg3, v1, key52[:, 0:NT])
                V.link(vec.tensor_tensor(o3, io, spread(key52[:, 0:NT]), ALU.is_equal))
                V.link(vec.scalar_tensor_tensor(l23, o3, -1.0e30, lg3, ALU.mult, ALU.add))
                first_max(l23, v2, key52[:, NT:2 * NT])
                vec.tensor_tensor(v2, v2, v1, ALU.subtract).then_inc(s_d, 1)
                e.wait_ge(s_dw, 1)
                V.link(ts(v1, v3, 1.0, ALU.add))
                V.link(vec.reciprocal(wgt[:, 0:NT], v1))
                V.link(vec.tensor_tensor(wgt[:, NT:2 * NT], wgt[:, 0:NT], v3, ALU.mult))
                vd = cst[:, C_VALID:C_VALID + NT]
                for j in range(2):
                    k_ = key52[:, j * NT:(j + 1) * NT]
                    V.link(ts(k_, k_, -float(NX), ALU.add))
                    V.link(vec.tensor_tensor(k_, k_, vd, ALU.mult))
                    V.link(ts(k_, k_, float(NX), ALU.add))
                    V.link(vec.tensor_copy(tok52[:, j * NT:(j + 1) * NT], cst[:, C_TOK:C_TOK + NT]))
                bin_positions(key52, 2 * NT, NX, pos52, [(0, NX, hit5, run5)], s_c5, s_t5, ps[0])
                bins_of_tiles(gx, NX, TX, P)
                V.link(vec.tensor_copy(pos_i, pos52))
                slot_address(adr52, pos52, TX, tA, tB)
                V.link(vec.tensor_copy(posf, adr52))
                for j in range(2):
                    V.link(ts(tmp52[:, 0:NT], vd, -BIG, ALU.mult, BIG, ALU.add))
                    V.link(vec.tensor_tensor(posf[:, j * NT:(j + 1) * NT], posf[:, j * NT:(j + 1) * NT],
                                             tmp52[:, 0:NT], ALU.add))
                V.link(vec.tensor_copy(adr52, posf))
                V.link(vec.tensor_copy(gxi[0:1, :], gx[0:1, :]))
                V.link(vec.memset(xsl, 0))

            @block.scalar
            def _(e):
                A.e = e
                norm_root(sv4, sq4)
                norm_root(sv5, sq5)
                e.wait_ge(s_d, 1)
                act.activation(v3, v2, ACT.Exp).then_inc(s_dw, 1)

            @block.tensor
            def _(e):
                T.e = e
                e.wait_ge(s_w, 5 * 16)

                def body(i):
                    for u in range(2):
                        t = i * 2 + u
                        e.wait_ge(s_xk, t * 2 + 1)
                        T.wait(s_xc, t - 1)
                        for k in range(2):
                            last = pe.transpose(ps[u][:, k * P:(k + 1) * P], xk[u][:, k * P:(k + 1) * P], ident)
                        last.then_inc(s_xt, 1)
                        e.wait_ge(s_xc, t + 1)
                        T.wait(s_le, t - 1)
                        for k in range(2):
                            pe.matmul(ps[2 + u][:, 0:NX], xkT[u][:, k * P:(k + 1) * P],
                                      wr[:, k * NX:(k + 1) * NX], start=(k == 0), stop=False)
                        pe.matmul(ps[2 + u][:, 0:NX], cst[0:1, C_ONE:C_ONE + P], br, start=False, stop=True).then_inc(s_lg, 1)
                T.loop(NT // 2, body)
                bin_counts(NX, s_c5, s_t5, ps[0])

        end_of_block()
        s_y = sem("slot_default")
        s_l4 = sems("last_scatter", 4)
        b1e, b2e = xn[0:96, 4608:5120].bitcast(bf16), xn[0:96, 5120:5248].bitcast(bf16)
        braw, bpart = xn[0:96, 0:1280], xn[0:96, 1280:1920].bitcast(bf16)
        s_be, s_bz = sem("expert_biases"), sem("zeroed")
        with nc.Block() as block:
            @block.sync
            def _(e):
                e.wait_ge(s_bz, 1)
                for j in range(3):
                    o = slice(32 * j, 32 * j + NX)
                    e.dma_start(xn[o, 0:HID], a["b1"]).then_inc(s_be, 16)
                    e.dma_start(xn[o, HID:HID + C], a["b2"]).then_inc(s_be, 16)
                e.wait_ge(s_be, 96)

            @block.vector
            def _(e):
                V.e = e
                vec.memset(braw, 0.0).then_inc(s_bz, 1)
                e.wait_ge(s_be, 96)
                three_parts([(xn[0:96, 4608:5248].bitcast(bf16), 0, HID + C)], braw, bpart)

            @block.gpsimd
            def _(e):
                G.e = e
                xv = xslotd.rearrange("(p t) o -> p (t o)", p=P)
                e.dma_start(xv, xsl).then_inc(s_y, 16)
                e.wait_ge(s_y, 16)
                n = bin_edges(e, 48, xslotd, adr52, tok52, 1, 4 * 2 * (EC // 8), bound=P * TX - 1)
                for u in range(4):
                    e.indirect_dma_start(xslotd, bass.IndirectOffsetOnAxis(ap=adr52[:, 48 + u:49 + u], axis=0),
                                         tok52[:, 48 + u:49 + u], None, bounds_check=P * TX - 1,
                                         oob_is_err=False).then_inc(s_l4[u], 16)
                for u in range(4):
                    e.wait_ge(s_l4[u], 16)
                e.dma_start(xsl, xv).then_inc(s_y, 16)
                e.wait_ge(s_y, 32)

        end_of_block()
        xT7 = xk
        sel1 = [xkT[u][0:96, 0:64].bitcast(bf16) for u in range(2)]
        sel2 = [xkT[u][0:96, 64:128].bitcast(bf16) for u in range(2)]
        XB = xn[:, 0:4608]
        hb = [XB[:, j * HID:(j + 1) * HID] for j in range(2)]
        hTb = [XB[:, 2048 + j * HID:2048 + (j + 1) * HID] for j in range(2)]
        yb = [XB[:, 4096 + j * C:4096 + (j + 1) * C] for j in range(2)]
        ist7 = [sb(f"ist7{u}", 1, i32) for u in range(2)]
        s_g7 = sems("token_gather", 2)
        s_i7, s_t7, s_x7, s_h7, s_e7, s_r7, s_c7, s_y7, s_o7 = (sem(n) for n in
            ("index", "x_T", "x_T_out", "layer1", "gelu", "hidden_T", "hidden_T_out", "layer2", "y_out"))
        s_yd = sems("y_dma", 2)

        def in_pairs(eng, step):
            def body(i):
                for c in (1, 2):
                    step(2 * i + c, i, c)
            eng.loop(TX // 2 - 1, body)
            step(TX - 1, TX // 2 - 1, 1)

        with nc.Block() as block:
            @block.gpsimd
            def _(e):
                G.e = e

                def body(i):
                    for u in range(2):
                        t = i * 2 + u
                        G.wait(s_t7, t - 1)
                        G.settle()
                        nc.gpsimd.tensor_copy(ist7[u][:, :], xsl[:, ds(t, 1)]).then_inc(s_i7, 1)
                        e.wait_ge(s_i7, t + 1)
                        G.settle()
                        e.indirect_dma_start(xg[u], None, xtok, bass.IndirectOffsetOnAxis(
                            ap=ist7[u][:, 0:1], axis=0)).then_inc(s_g7[u], 16)
                G.loop(TX // 2, body)

            @block.vector
            def _(e):
                V.e = e

                def pick(dst, t):
                    return ts(dst, gx[0:96, ds(t, 1)].broadcast_to([96, P]), cst[0:96, C_PID:C_PID + 1],
                              ALU.is_equal)

                def x_out(t, u):
                    V.settle()
                    x = e.value_load(gxi[0:1, ds(t, 1)], min_val=0, max_val=NX - 1)
                    V.wait(s_h7, 2 * t - 2)
                    V.link(pick(sel1[u], t))
                    e.wait_ge(s_t7, t + 1)
                    for k in range(2):
                        last = ts(xT7[u][:, k * P:(k + 1) * P], ps[0][:, k * P:(k + 1) * P],
                                  gsel[:, ds(x + k * NX, 1)], ALU.mult, gsel[:, ds(x + (2 + k) * NX, 1)], ALU.add)
                        if k == 0:
                            V.link(last)
                    last.then_inc(s_x7, 1)

                def h_out(t, u):
                    V.wait(s_y7, t - 1)
                    V.link(pick(sel2[u], t))
                    e.wait_ge(s_r7, t + 1)
                    for k in range(2):
                        vec.tensor_copy(hTb[u][:, k * 512:(k + 1) * 512], ps[3 + k][:, :]).then_inc(s_c7, 1)

                def y_out(t, i, u):
                    e.wait_ge(s_y7, t + 1)
                    V.wait(s_yd[u], 16 * i)
                    vec.tensor_copy(yb[u], ps[5 + u][:, 0:C]).then_inc(s_o7, 1)

                x_out(0, 0)
                x_out(1, 1)

                def step(t, i, c):
                    h_out(t - 1, (c - 1) % 2)
                    if not (isinstance(t, int) and t == TX - 1):
                        x_out(t + 1, (c + 1) % 2)
                    y_out(t - 1, i, (c - 1) % 2)
                in_pairs(V, step)
                h_out(TX - 1, 1)
                y_out(TX - 1, TX // 2 - 1, 1)

            @block.scalar
            def _(e):
                A.e = e

                def body(i):
                    for u in range(2):
                        t = i * 2 + u
                        A.wait(s_r7, t - 1)
                        for c in range(2):
                            e.wait_ge(s_h7, 2 * t + c + 1)
                            act.activation(hb[u][:, c * 512:(c + 1) * 512], ps[1 + c][:, :],
                                           ACT.Gelu).then_inc(s_e7, 1)
                A.loop(TX // 2, body)

            @block.tensor
            def _(e):
                T.e = e

                def expert(t):
                    T.settle()
                    return e.value_load(gxi[0:1, ds(t, 1)], min_val=0, max_val=NX - 1)

                def x_transpose(t, i, u):
                    T.wait(s_x7, t)
                    e.wait_ge(s_g7[u], 16 * (i + 1))
                    for k in range(2):
                        last = pe.transpose(ps[0][:, k * P:(k + 1) * P], xg[u][:, k * P:(k + 1) * P], ident)
                    last.then_inc(s_t7, 1)

                def layer1(t, u):
                    x = expert(t)
                    e.wait_ge(s_x7, t + 1)
                    T.wait(s_e7, 2 * t)
                    for c in range(2):
                        for k in range(2):
                            pe.matmul(ps[1 + c][:, :], xT7[u][:, k * P:(k + 1) * P],
                                      arena[:, ds(x * HID + (WE1 + k * 8192 + c * 512), 512)],
                                      start=(k == 0), stop=False)
                        pe.matmul(ps[1 + c][:, :], sel1[u], b1e[:, c * 512:(c + 1) * 512],
                                  start=False, stop=True).then_inc(s_h7, 1)

                def h_transpose(t, u):
                    e.wait_ge(s_e7, 2 * t + 2)
                    T.wait(s_c7, 2 * t)
                    for j in range(8):
                        last = pe.transpose(ps[3 + j // 4][:, (j % 4) * P:(j % 4 + 1) * P],
                                            hb[u][:, j * P:(j + 1) * P], ident)
                    last.then_inc(s_r7, 1)

                def layer2(t, u):
                    x = expert(t)
                    e.wait_ge(s_c7, 2 * t + 2)
                    T.wait(s_o7, t - 1)
                    for j in range(8):
                        pe.matmul(ps[5 + u][:, 0:C], hTb[u][:, j * P:(j + 1) * P],
                                  arena[:, ds(x * 2048 + (WE2 + j * C), C)], start=(j == 0), stop=False)
                    pe.matmul(ps[5 + u][:, 0:C], sel2[u], b2e, start=False, stop=True).then_inc(s_y7, 1)

                x_transpose(0, 0, 0)
                x_transpose(1, 0, 1)
                layer1(0, 0)

                def step(t, i, c):
                    h_transpose(t - 1, (c - 1) % 2)
                    if not (isinstance(t, int) and t == TX - 1):
                        x_transpose(t + 1, i + (c + 1) // 2, (c + 1) % 2)
                    layer1(t, c % 2)
                    layer2(t - 1, (c - 1) % 2)
                in_pairs(T, step)
                h_transpose(TX - 1, 1)
                layer2(TX - 1, 1)

            @block.sync
            def _(e):
                S.e = e

                def body(i):
                    for u in range(2):
                        t = i * 2 + u
                        e.wait_ge(s_o7, t + 1)
                        e.dma_start(yslot[ds(t * P, P), :], yb[u]).then_inc(s_yd[u], 16)
                S.loop(TX // 2, body)
                for u in range(2):
                    e.wait_ge(s_yd[u], 16 * TX // 2)

        end_of_block()
        pk = [[XB[:, (2 * j + u) * C:(2 * j + u + 1) * C] for j in range(2)] for u in range(2)]
        s_i8, s_u8, s_w8 = sem("index"), sem("first_added"), sem("second_added")
        s_g8 = [sems(f"pick{u}", 2) for u in range(2)]
        ist8 = [sb(f"ist8{u}", 2, i32) for u in range(2)]
        s_od = sems("out", 2)
        with nc.Block() as block:
            @block.gpsimd
            def _(e):
                G.e = e

                def body(i):
                    for u in range(2):
                        t = i * 2 + u
                        G.wait(s_w8, t - 1)
                        G.settle()
                        for j in range(2):
                            nc.gpsimd.tensor_copy(ist8[u][:, j:j + 1], pos_i[:, ds(t + j * NT, 1)]).then_inc(s_i8, 1)
                        e.wait_ge(s_i8, 2 * t + 2)
                        G.settle()
                        for j in range(2):
                            e.indirect_dma_start(pk[u][j], None, yslot, bass.IndirectOffsetOnAxis(
                                ap=ist8[u][:, j:j + 1], axis=0)).then_inc(s_g8[u][j], 16)
                G.loop(NT // 2, body)

            @block.vector
            def _(e):
                V.e = e

                def body(i):
                    for u in range(2):
                        t = i * 2 + u
                        xt_ = X1[:, ds(t * C, C)]
                        for j in range(2):
                            e.wait_ge(s_g8[u][j], 16 * (i + 1))
                            vec.scalar_tensor_tensor(xt_, pk[u][j], wgt[:, ds(t + j * NT, 1)], xt_, ALU.mult,
                                                     ALU.add).then_inc((s_u8, s_w8)[j], 1)
                            if j == 0:
                                e.wait_ge(s_u8, t + 1)
                V.loop(NT // 2, body)

            @block.sync
            def _(e):
                S.e = e

                def body(i):
                    for u in range(2):
                        t = i * 2 + u
                        e.wait_ge(s_w8, t + 1)
                        e.dma_start(out[ds(t * P, P), :], X1[:, ds(t * C, C)]).then_inc(s_od[u], 16)
                S.loop(NT // 2, body)
                for u in range(2):
                    e.wait_ge(s_od[u], 16 * NT // 2)


def kernel(**inputs):
    import numpy as np
    import concourse.bacc as bacc
    from concourse.bass_utils import run_bass_kernel_spmd as run

    g = {k: np.asarray(v) for k, v in inputs.items()}
    cols = lambda v: np.ascontiguousarray(v.reshape(-1, P).T)
    row = lambda v: v.reshape(1, -1)
    edge = lambda v, fill: np.concatenate([v, np.full(P * EC - E, fill, v.dtype)]).reshape(P, EC)
    x = g["x"]
    arrays = {
        "cst": constants(np),
        "x": np.concatenate([x, x[:NP - N]]),
        "src": edge(g["src"], N + P - 1), "dst": edge(g["dst"], N + P - 1), "et": edge(g["edge_type_16"], 0),
        "Wf": g["L0_gnn_Wf"].transpose(1, 0, 2).reshape(C, R * C),
        "Wb": g["L0_gnn_Wb"].transpose(1, 0, 2).reshape(C, R * C),
        "lw": g["L0_gnn_loop_weight"], "fwd_b": row(g["L0_gnn_forward_bias"]),
        "bwd_b": row(g["L0_gnn_backward_bias"]), "self_b": row(g["L0_gnn_self_bias"]),
        "ln1w": cols(g["L0_mix_ln1_w"]), "ln1b": cols(g["L0_mix_ln1_b"]),
        "ln2w": cols(g["L0_mix_ln2_w"]), "ln2b": cols(g["L0_mix_ln2_b"]),
        "Wx": g["L0_mix_Wx"], "WxT": g["L0_mix_Wx"].T, "bx": cols(g["L0_mix_bx"]), "bxrow": row(g["L0_mix_bx"]),
        "WqT": g["L0_mix_Wq"].T, "WkT": g["L0_mix_Wk"].T, "Wv": g["L0_mix_Wv"], "WoT": g["L0_mix_Wo"].T,
        "bo": row(g["L0_mix_bo"]), "mW1T": g["L0_mix_W1"].T, "mb1": cols(g["L0_mix_b1"]),
        "mW2T": g["L0_mix_W2"].T, "mb2": row(g["L0_mix_b2"]),
        "Wr": g["L0_ffn_Wr"], "br": row(g["L0_ffn_br"]),
        "lng": g["L0_ffn_ln_g"].reshape(NX, 2, P).transpose(2, 1, 0).reshape(P, 2 * NX),
        "lnb": g["L0_ffn_ln_b"].reshape(NX, 2, P).transpose(2, 1, 0).reshape(P, 2 * NX),
        "W1": g["L0_ffn_W1"].reshape(NX * C, HID), "b1": g["L0_ffn_b1"],
        "W2": g["L0_ffn_W2"].reshape(NX * HID, C), "b2": g["L0_ffn_b2"],
    }
    arrays = {f"in_{k}": np.ascontiguousarray(v) for k, v in arrays.items()}
    nc = bacc.Bacc("TRN2", target_bir_lowering=False, num_devices=1)
    a = {k[3:]: nc.dram_tensor(k, v.shape, mybir.dt.from_np(v.dtype), kind="ExternalInput").ap()
         for k, v in arrays.items()}
    out = nc.dram_tensor("out", (NP, C), f32, kind="ExternalOutput").ap()
    build(nc, a, out)
    return run(nc, [arrays], core_ids=[0]).results[0]["out"][:N]
```

```python
import concourse.bass as bass
from concourse import mybir

N, C, E, R = 3125, 256, 53125, 16
P = 128
NT = 26
NP = NT * P
EC = 416
HEADS, HD = 8, 32
HID = 1024
NX, TOPK = 8, 2
TE = (E + (NT - 1) * (P - 1)) // P + 1
TX = (N * TOPK + NX * (P - 1)) // P
EPS = 1e-5

f32, i32, bf16 = mybir.dt.float32, mybir.dt.int32, mybir.dt.bfloat16
ALU, ACT, AX = mybir.AluOpType, mybir.ActivationFunctionType, mybir.AxisListType

C_ID, C_IOTA, C_TRI, C_ONE, C_VALID, C_TILE, C_PID = 0, 128, 256, 384, 512, 538, 978
C_TOK, C_ROW = 979, 979 + NT
C_N = C_ROW + 1


def constants(np):
    c = np.zeros((P, C_N), np.float32)
    p = np.arange(P)
    c[:, C_ID:C_ID + P] = np.eye(P)
    c[:, C_IOTA:C_IOTA + P] = p[None, :]
    c[:, C_TRI:C_TRI + P] = p[:, None] < p[None, :]
    c[:, C_ONE:C_ONE + P] = 1.0
    rows = np.arange(NT)[None, :] * P + p[:, None]
    c[:, C_VALID:C_VALID + NT] = rows < N
    c[:, C_TILE:C_TILE + TE] = np.arange(TE)[None, :]
    c[:, C_PID] = np.where((p < 96) & (p % 32 < NX), p % 32, -1)
    c[:, C_ROW] = (p < 96) & (p % 32 == 0)
    c[:, C_TOK:C_TOK + NT] = rows
    return c


class Engine:

    def __init__(self, e, ns, sem, pad):
        self.e, self.ns, self.sem, self.pad, self.n, self.reg = e, ns, sem, pad, 0, 0

    def wait(self, sem, value):
        if not (isinstance(value, int) and value <= 0):
            self.e.wait_ge(sem, value)

    def link(self, ins):
        ins.then_inc(self.sem, 1)
        self.n += 1
        self.e.wait_ge(self.sem, self.reg + self.n)

    def mark(self, ins):
        ins.then_inc(self.sem, 1)
        self.n += 1

    def join(self):
        self.e.wait_ge(self.sem, self.reg + self.n)

    def settle(self):
        self.e.sem_inc(self.pad, 1)

    def barrier(self, sem, n, parties=4):
        self.e.drain().then_inc(sem, 1)
        self.e.wait_ge(sem, parties * n)

    def loop(self, n, body, last=False, start=0):
        before = self.n
        body(start)
        per = self.n - before
        end = n - 1 if last else n
        with self.e.Fori(start + 1, end) as i:
            self.reg, self.n = (i - start) * per if per else 0, before
            body(i)
        self.reg, self.n = 0, before + (end - start) * per
        if last:
            body(n - 1)


def build(nc, a, out):
    from contextlib import ExitStack
    ctx = ExitStack()
    ds = bass.ds

    def dram(name, rows, cols, dt=f32):
        return nc.dram_tensor(name, (rows, cols), dt, kind="Internal").ap()

    table = [dram("table_fwd", NP * R, C), dram("table_bwd", NP * R, C)]
    mixd = dram("mix_rows", NP, 770)
    gmapd = [dram("bin_of_tile_fwd", 1, TE, i32), dram("bin_of_tile_bwd", 1, TE, i32)]
    slotd = [dram("slots_fwd", P * TE, 2, i32), dram("slots_bwd", P * TE, 2, i32)]
    xtok = dram("ffn_tokens", NP, C)
    yslot = dram("ffn_rows", P * TX, C)

    with ctx:
        def sb(name, cols, dt=f32, rows=P):
            return ctx.enter_context(nc.sbuf_tensor(name, [rows, cols], dt))

        nsem = [0]

        scope = []

        def sem(name, whole=False):
            nsem[0] += 1
            s_ = nc.alloc_semaphore(f"{name}_{nsem[0]}")
            if not whole:
                scope.append(s_)
            return s_

        def sems(name, n, whole=False):
            return [sem(f"{name}{i}", whole) for i in range(n)]

        def end_of_block():
            nc.clear_and_free_semaphores(list(scope))
            scope.clear()
            nc.all_engine_barrier()

        arena = sb("arena", 32768)
        X1 = sb("X1", NT * C)
        xn = sb("xn", NT * C)
        cst = sb("cst", C_N)
        work = sb("work", 3074)
        small = sb("small", 900)
        ps = [ctx.enter_context(nc.psum_tensor(f"bank{i}", [P, 512], f32)) for i in range(8)]
        ident, iota = cst[:, C_ID:C_ID + P], cst[:, C_IOTA:C_IOTA + P]
        tri, ones = cst[:, C_TRI:C_TRI + P], cst[:, C_ONE:C_ONE + P]

        def ar(off, n, rows=P):
            return arena[0:rows, off:off + n]

        W_off = 0
        STG = [16384, 20480]
        W1T_off, W2T_off = 24576, 26624
        PAY = [28672, 29504]
        ADR = [30336, 30752]
        WM_off = 31168
        so = [0]

        def sm(n, rows=P):
            so[0] += n
            return small[0:rows, so[0] - n:so[0]]

        st = sm(NT * 6)
        mean, rstd, mean2, rstd2 = sm(NT), sm(NT), sm(NT), sm(NT)
        v1, v2, v3 = sm(NT), sm(NT), sm(NT)
        winv, whas = sm(NT), sm(NT)
        lncol = sm(8)
        b1col = sm(8)
        kmT = sm(2)
        bxcol = sm(2)
        cnt, tot, til, base, incl, ends = (sm(NT) for _ in range(6))
        den = sm(2)
        rmax, rsum = sm(HEADS), sm(HEADS)
        brow = sb("brow", 768, bf16, 96)
        rows_o = sb("rows_o", C, bf16, 96)
        rows_2 = sb("rows_2", C, bf16, 96)
        row_sel = sb("row_sel", P, bf16, 96)
        lw = sb("lw", 512)
        kmax = sb("kmax", C)

        s_v, s_a, s_p, s_g, s_s, s_pad = (sem(n, True) for n in ("dve", "act", "pe", "pool", "sp", "pad"))
        V = Engine(None, nc.vector, s_v, s_pad)
        A = Engine(None, nc.scalar, s_a, s_pad)
        T = Engine(None, nc.tensor, s_p, s_pad)
        G = Engine(None, nc.gpsimd, s_g, s_pad)
        S = Engine(None, nc.sync, s_s, s_pad)

        vec, act, pe = nc.vector, nc.scalar, nc.tensor

        def ts(out, in0, s1, op0, s2=None, op1=None):
            if op1 is None:
                return vec.tensor_scalar(out, in0, s1, None, op0)
            return vec.tensor_scalar(out, in0, s1, s2, op0, op1)

        def tile_stats(src, t):
            V.mark(vec.bn_stats(st[:, ds(t * 6, 6)], src[:, ds(t * C, C)]))

        def norm_stats(src, m, r, s_var, s_sqrt, before=None):
            def stats(ts_):
                if before is not None:
                    before(ts_)
                for t in ts_:
                    if before is not None:
                        V.settle()
                    tile_stats(src, t)
            if src is not None:
                V.loop(NT // 4, lambda i: stats([4 * i + u for u in range(4)]))
                stats(range(NT // 4 * 4, NT))
            V.join()
            q = st.rearrange("p (t s) -> p t s", s=6)
            me, ve, mo, vo = q[:, :, 1], q[:, :, 2], q[:, :, 4], q[:, :, 5]
            V.link(vec.tensor_tensor(m, me, mo, ALU.add))
            V.link(ts(m, m, 0.5, ALU.mult))
            V.link(vec.tensor_tensor(v1, me, mo, ALU.subtract))
            V.link(vec.tensor_tensor(v1, v1, v1, ALU.mult))
            V.link(vec.tensor_tensor(v2, ve, vo, ALU.add))
            V.link(ts(v2, v2, 1.0 / C, ALU.mult, EPS, ALU.add))
            vec.scalar_tensor_tensor(v1, v1, 0.25, v2, ALU.mult, ALU.add).then_inc(s_var, 1)
            V.e.wait_ge(s_sqrt, 1)
            V.link(vec.reciprocal(v2, v2))
            V.link(vec.tensor_tensor(v3, v2, v2, ALU.mult))
            V.link(vec.tensor_tensor(v3, v3, v1, ALU.mult))
            V.link(ts(v3, v3, -0.5, ALU.mult, 1.5, ALU.add))
            V.link(vec.tensor_tensor(r, v2, v3, ALU.mult))

        def norm_root(s_var, s_sqrt):
            A.e.wait_ge(s_var, 1)
            act.activation(v2, v1, ACT.Sqrt).then_inc(s_sqrt, 1)

        def norm_apply(dst, t, src, m, r):
            return vec.tensor_scalar(dst, src[:, ds(t * C, C)], m[:, ds(t, 1)], r[:, ds(t, 1)],
                                     ALU.subtract, ALU.mult)

        def bin_positions(key, cols, bins, pos, sets, s_cnt, s_tot, bank):
            c_, t_, l_, b_, i_, end = (x[:, 0:bins] for x in (cnt, tot, til, base, incl, ends))
            views = []
            for g0, g1, hit, run in sets:
                n = (g1 - g0) * cols
                h3, r3 = (x[:, 0:n].rearrange("p (g c) -> p g c", c=cols) for x in (hit, run))
                views.append((g0, g1, h3, r3))
                shape = [P, g1 - g0, cols]
                V.link(vec.tensor_tensor(h3, key.unsqueeze(1).broadcast_to(shape),
                                         iota[:, g0:g1].unsqueeze(2).broadcast_to(shape), ALU.is_equal))
                V.link(vec.tensor_tensor_scan(run[:, 0:n], hit[:, 0:n], hit[:, 0:n], 0.0, ALU.add, ALU.max))
                V.link(vec.tensor_copy(end[:, g0:g1], r3[:, :, cols - 1]))
                V.link(vec.tensor_copy(c_[:, g0:g1], end[:, g0:g1]))
                V.link(vec.tensor_tensor(c_[:, g0 + 1:g1], end[:, g0 + 1:g1], end[:, g0:g1 - 1], ALU.subtract))
            V.e.sem_inc(s_cnt, 1)
            V.e.wait_ge(s_tot, 1)
            V.link(vec.tensor_copy(t_, bank[:, 64:64 + bins]))
            V.link(ts(l_, t_, float(P - 1), ALU.add))
            ti = v1[:, 0:bins].bitcast(i32)
            V.link(vec.tensor_copy(ti, l_))
            V.link(vec.tensor_single_scalar(ti, ti, 7, op=ALU.arith_shift_right))
            V.link(vec.tensor_copy(l_, ti))
            V.link(vec.tensor_tensor_scan(i_, l_, l_, 0.0, ALU.add, ALU.max))
            V.link(vec.tensor_tensor(b_, i_, l_, ALU.subtract))
            V.link(ts(b_, b_, float(P), ALU.mult, -1.0, ALU.add))
            V.link(vec.tensor_tensor(b_, b_, bank[:, 0:bins], ALU.add))
            for n, (g0, g1, h3, r3) in enumerate(views):
                V.link(vec.tensor_tensor(b_[:, g0 + 1:g1], b_[:, g0 + 1:g1], end[:, g0:g1 - 1], ALU.subtract))
                V.link(vec.tensor_tensor(r3, r3, b_[:, g0:g1].unsqueeze(2).broadcast_to([P, g1 - g0, cols]),
                                         ALU.add))
                V.link(vec.tensor_tensor(r3, r3, h3, ALU.mult))
                part = views[0][3][:, 0, :] if n else pos
                V.link(vec.tensor_reduce(part, r3.rearrange("p g c -> p c g"), AX.X, ALU.add))
                if n:
                    V.link(vec.tensor_tensor(pos, pos, part, ALU.add))

        def bins_of_tiles(gmap, bins, tiles, rows):
            V.link(vec.memset(gmap, 0.0))

            def passed(g):
                V.link(vec.scalar_tensor_tensor(gmap, cst[0:rows, C_TILE:C_TILE + tiles],
                                                incl[0:rows, ds(g, 1)], gmap, ALU.is_ge, ALU.add))
            V.loop(bins, passed)
            V.link(ts(gmap, gmap, float(bins - 1), ALU.min))

        def three_parts(rows, raw, part):
            for j in range(3):
                o = slice(32 * j, 32 * j + 32)
                V.link(vec.tensor_copy(part, raw))
                for dst, c0, n in rows:
                    V.link(vec.tensor_copy(dst[o, :], part[o, c0:c0 + n]))
                if j < 2:
                    V.link(vec.tensor_tensor(raw, raw, part, ALU.subtract))

        def bin_counts(bins, s_cnt, s_tot, bank):
            T.e.wait_ge(s_cnt, 1)
            pe.matmul(bank[:, 0:bins], tri, cnt[:, 0:bins], start=True, stop=True)
            pe.matmul(bank[:, 64:64 + bins], ones, cnt[:, 0:bins], start=True,
                      stop=True).then_inc(s_tot, 1)

        def slot_address(dst, pos, tiles, ta, tb):
            V.link(vec.tensor_copy(ta, pos))
            V.link(vec.tensor_single_scalar(tb, ta, P - 1, op=ALU.bitwise_and))
            V.link(vec.tensor_single_scalar(ta, ta, 7, op=ALU.arith_shift_right))
            V.link(vec.scalar_tensor_tensor(dst, tb, float(tiles), ta, ALU.mult, ALU.add))

        HB = NT // 2
        bin_sets = [(0, HB, ar(25888, 2704).bitcast(bf16), ar(20480, HB * EC)),
                    (HB, NT, ar(8192, 2704).bitcast(bf16), ar(10896, HB * EC))]
        ei = [work[:, 1024 + j * EC:1024 + (j + 1) * EC].bitcast(i32) for j in range(3)]
        tmp_i = work[:, 1024 + 3 * EC:1024 + 4 * EC].bitcast(i32)
        gmap_s = lw[0:1, 0:TE]
        gmap_row = work[0:1, 1024 + 3 * EC:1024 + 3 * EC + TE]
        BD, BDk, BDv = (ar(STG[0] + j * P, P) for j in range(3))
        WX, WOT = ar(STG[0] + 384, 512), ar(STG[0] + 896, 512)
        empty = work[:, 0:2 * TE]
        Pm = sb("Pm", 512)
        raw_rows = ar(8192, 1280, 96)
        part_rows = ar(9472, 640, 96).bitcast(bf16)

        ld, lde, ldf, ldb, ldx, ldw, zbd = (sem(n) for n in
            ("ld_small", "ld_edges", "ld_fold", "ld_blocks", "ld_x", "ld_tables", "zero"))
        s_ixf = sem("forward_addresses")
        s_em, s_ed = sem("empty_slots"), sem("slots_default")
        sc, stt = sems("counts", 2, True), sems("totals", 2, True)
        folded, s_pmo, ldr = sem("folded"), sem("Wv_Wo_out"), sem("ld_rows")

        def bin_edges_of(d):
            key, other = (ei[1], ei[0]) if d == 0 else (ei[0], ei[1])
            pay = ar(PAY[d], 2 * EC).bitcast(i32).rearrange("p (c two) -> p c two", two=2)
            payf = ar(PAY[d], 2 * EC).rearrange("p (c two) -> p c two", two=2)
            V.link(ts(tmp_i, other, float(R), ALU.mult))
            V.link(vec.tensor_tensor(pay[:, :, 0], tmp_i, ei[2], ALU.add))
            V.link(vec.tensor_single_scalar(tmp_i, key, P - 1, op=ALU.bitwise_and))
            V.link(vec.tensor_copy(payf[:, :, 1], tmp_i))
            V.link(vec.tensor_single_scalar(tmp_i, key, 7, op=ALU.arith_shift_right))
            bin_positions(tmp_i, EC, NT, ar(ADR[d], EC), bin_sets, sc[d], stt[d], ps[3 * d])
            slot_address(ar(ADR[d], EC).bitcast(i32), ar(ADR[d], EC), TE, tmp_i,
                         ar(20480, EC).bitcast(i32))

        def fwd_gmap(gm):
            bins_of_tiles(gm, NT, TE, 1)
            return ts(gm.bitcast(i32), gm, float(C + 1), ALU.mult)

        s_gm, s_gd = sem("bin_of_tile"), sem("bin_of_tile_dma", True)
        w = [0]

        def wk(n):
            w[0] += n
            return work[:, w[0] - n:w[0]]

        xs, xT, zs, zT = ([wk(C) for _ in range(2)] for _ in range(4))
        mst = wk(770)
        qx = wk(C)
        ist = [sb(f"ist{h}", 8, i32) for h in range(2)]
        pst = [sb(f"pst{h}", 16, i32) for h in range(2)]
        HALF = 8
        s_sc = sems("scatter", 2 * HALF, True)
        s_cp = sem("copied", True)
        sc_base = [0]

        def bin_edges(e, count, table_dram, adr, pay, width, base_):
            def body(i):
                for h in range(2):
                    for u in range(HALF):
                        G.wait(s_sc[HALF * h + u], sc_base[0] + 16 * i)
                    G.settle()
                    c0 = (i * 2 + h) * HALF
                    nc.gpsimd.tensor_copy(ist[h][:, :], adr[:, ds(c0, HALF)]).then_inc(s_cp, 1)
                    nc.gpsimd.tensor_copy(pst[h][:, 0:HALF * width],
                                          pay[:, ds(c0 * width, HALF * width)]).then_inc(s_cp, 1)
                    e.wait_ge(s_cp, base_ + 4 * i + 2 * h + 2)
                    G.settle()
                    for u in range(HALF):
                        e.indirect_dma_start(table_dram, bass.IndirectOffsetOnAxis(ap=ist[h][:, u:u + 1], axis=0),
                                             pst[h][:, u * width:(u + 1) * width],
                                             None).then_inc(s_sc[HALF * h + u], 16)
            turns = count // (2 * HALF)
            G.loop(turns, body)
            sc_base[0] += 16 * turns
            for s_ in s_sc:
                e.wait_ge(s_, sc_base[0])
            return base_ + 4 * turns

        def tiles(eng, step, after=None, job=None):
            def body(i):
                for u in range(2):
                    step(2 * i + u, i, u)
            if job is not None:
                eng.loop(after, body)
                job()
            eng.loop(NT // 2 - 1, body, start=after or 0)
            for u in range(2):
                step(NT - 2 + u, NT // 2 - 1, u)

        def has(t, n):
            return not (isinstance(t, int) and t + n >= NT)

        s_bar = sem("phase")
        sv1, sq1, sv2, sq2 = sem("var"), sem("root"), sem("var"), sem("root")
        s_xn, s_ixb, s_wb = sem("xn_ready"), sem("backward_addresses"), sem("backward_weights")
        pass_sems = [[sem(n) for n in ("tile_ready", "transposed", "transposes_out", "proj_mm", "proj_out",
                                       "tile_done")] for _ in range(2)]
        s_td = [sems("table_dma", 2) for _ in range(2)]
        s_mm, s_mrow, s_mdma, s_q, s_qe = (sem(n) for n in
            ("mix_mm", "mix_row", "mix_dma", "q_minus_max", "q_exp"))

        def evacuate(d, t, c):
            s_pj, s_po = pass_sems[d][3:5]
            if c % 4 == 0:
                A.wait(s_td[d][c // 4], 16 * t)
            A.e.wait_ge(s_pj, 8 * t + c + 1)
            act.activation(ar(STG[d] + c * 512, 512), ps[4 + c % 4][:, :], ACT.Copy).then_inc(s_po, 1)

        def project(d, t, u):
            s_pj, s_po, s_done = pass_sems[d][3:6]
            for c in range(8):
                T.wait(s_po, 8 * t + c - 3)
                for k in range(2):
                    last = pe.matmul(ps[4 + c % 4][:, :], xT[u][:, k * P:(k + 1) * P],
                                     ar(W_off + d * 8192 + k * 4096 + c * 512, 512),
                                     start=(k == 0), stop=(k == 1))
                last.then_inc(s_pj, 1)
            T.e.sem_inc(s_done, 1)

        tv = [tb.rearrange("(n r) c -> n (r c)", r=R) for tb in table]

        def store_rows(d, t):
            s_po = pass_sems[d][4]
            for h in range(2):
                S.e.wait_ge(s_po, 8 * t + 4 * h + 4)
                S.e.dma_start(tv[d][ds(t * P, P), h * 2048:(h + 1) * 2048],
                              ar(STG[d] + h * 2048, 2048)).then_inc(s_td[d][h], 16)

        NB = 4
        kx = [ar(5760 + 258 * j, 258) for j in range(NB)]
        km = [ar(256 * j, C) for j in range(NB)]
        kin = [ar(1024 + 514 * j, 514) for j in range(NB)]
        kmb = ar(4352, C)
        dg = ar(4608, P)
        KX, KXT = ar(4736, C), ar(4992, C)
        M = ar(5248, 512)
        s_k1, s_k2, s_k3, s_k4 = (sem("kmax_step") for _ in range(4))
        s_ki = sems("mix_in", NB)
        s_ks, s_ke, s_kv, s_km, s_kd = (sem(n) for n in
            ("k_minus_max", "k_exp", "xm_masked", "kv_mm", "kv_steps"))
        hall = ar(16384, NT * C)
        qin = [ar(C * j, C) for j in range(NB)]
        qT = [ar(1024 + C * j, C) for j in range(NB)]
        s_qi = sems("q_in", NB)

        def in_fours(eng, step, after=None, job=None):
            def body(i):
                for u in range(NB):
                    step(NB * i + u, i, u)
            if job is not None:
                eng.loop(after, body)
                job()
            eng.loop(NT // NB, body, start=after or 0)
            for u in range(NT % NB):
                step(NT // NB * NB + u, NT // NB, u)
        s_qt, s_qc, s_at, s_h = sem("q_transposed"), sem("qT"), sem("attn_mm"), sem("h_out")
        sv3, sq3, sv4, sq4 = (sem(n) for n in ("var", "root", "var", "root"))
        z2 = [Pm[:, j * C:(j + 1) * C] for j in range(2)]
        z2T = ar(13568, 512)
        hT = ar(14080, 8 * C)
        s_z, s_zt, s_zc, s_m1, s_ge, s_m2, s_ad = (sem(n) for n in
            ("z2", "z2_transposed", "z2T", "mlp1", "gelu", "mlp2", "mlp_added"))
        W = C + 1
        ACC = [6800, 0]
        U = 8
        NG = TE // U
        QUARTERS = 4
        msg = [ar(28672 + j * W, W) for j in range(15)] + [lw[:, 0:W]]
        oh = [work[:, j * P:(j + 1) * P] for j in range(16)]
        slots = [work[:, 2048:2048 + 2 * TE], ar(23040, 2 * TE)]
        gmapi = [ar(23920, TE, 1).bitcast(i32), xn[0:1, 1024:1024 + TE].bitcast(i32)]
        rb = [xn[:, 0:C], xn[:, C:2 * C], xn[:, 2 * C:3 * C + 1]]
        gix = [sb(f"gather_index{j}", U, i32) for j in range(QUARTERS)]
        s_ga = sems("gather", 2 * U)
        s_pm, s_oh, s_sm, s_ac, s_bi, s_st, s_sl, s_scd = (sem(n) for n in
            ("pool_copies", "onehot", "segment_mm", "accumulated", "bias_in", "ones_set", "slots_in",
             "scattered"))
        s_z1, s_nm, s_zm = sem("backward_zero"), sem("minus_mean"), sem("z_centred")
        s_slb, s_bi0 = sem("backward_slots_in"), sem("bias_zero")

        class Group:
            def __init__(self, d, i, per, off):
                self.d, self.i, self.per, self.off = d, i, per, off
                self.n = i * per + off
                self.half, self.ring = off % 2, off % QUARTERS
                self.before = i * (per // 2) + off // 2
                self.tile = (self.n - NG * d) * U

            def next(self, d=None):
                return Group(self.d if d is None else d, self.i, self.per, self.off + 1)

        def zero_sums(d, t):
            to = ar(ACC[d], NT * W)[:, ds(t * W, W)]
            if d == 0:
                V.mark(ts(to, cst[:, 0:W], 0.0, ALU.mult))
            else:
                act.activation(to, cst[:, 0:W], ACT.Copy, scale=0.0).then_inc(s_z1, 1)

        def index_group(e, g):
            if isinstance(g.n, int) and g.n == NG:
                e.wait_ge(s_slb, 32)
                G.settle()
            nc.gpsimd.tensor_copy(gix[g.ring][:, :], slots[g.d][:, ds(g.tile * 2, 2 * U)].bitcast(
                i32).rearrange("p (t two) -> p t two", two=2)[:, :, 0]).then_inc(s_pm, 1)

        def gather_group(e, g, nxt):
            for o in range(0, U, U // 2):
                G.wait(s_sm, (g.n - 2) * U + o + U // 2)
                if o == 0:
                    e.wait_ge(s_pm, g.n + 1)
                G.settle()
                for u in range(o, o + U // 2):
                    b = U * g.half + u
                    e.indirect_dma_start(msg[b][:, 0:C], None, table[g.d], bass.IndirectOffsetOnAxis(
                        ap=gix[g.ring][:, u:u + 1], axis=0)).then_inc(s_ga[b], 16)
                if o == 0 and nxt is not None:
                    index_group(e, nxt)

        def onehots(g):
            A.wait(s_sm, (g.n - 1) * U)
            if isinstance(g.n, int) and g.n == NG:
                A.e.wait_ge(s_slb, 32)
            A.settle()
            for u in range(U):
                A.mark(act.activation(oh[U * g.half + u], iota, ACT.Abs, scale=-1.0,
                                      bias=slots[g.d][:, ds((g.tile + u) * 2 + 1, 1)]))
            A.join()
            half = work[:, U * P * g.half:U * P * (g.half + 1)]
            act.activation(half, half, ACT.Relu, scale=-1.0, bias=ones[:, 0:1]).then_inc(s_oh, 1)

        def add_sums(e, g):
            acc = ar(ACC[g.d], NT * W)
            for u in range(U):
                n = g.n * U + u
                at = e.value_load(gmapi[g.d][0:1, ds(g.tile + u, 1)], min_val=0, max_val=(NT - 1) * W)
                e.wait_ge(s_sm, n + 1)
                V.wait(s_ac, n)
                vec.tensor_tensor(acc[:, ds(at, W)], acc[:, ds(at, W)], ps[4 + u % 4][:, 0:W],
                                  ALU.add).then_inc(s_ac, 1)

        def sum_tile(e, g, u):
            n, b = g.n * U + u, U * g.half + u
            e.wait_ge(s_ga[b], 16 * (g.before + 1))
            if u == 0:
                if isinstance(g.n, int) and g.n == NG:
                    e.wait_ge(s_bi, 48)
                    e.wait_ge(s_bi0, 1)
                e.wait_ge(s_oh, g.n + 1)
            T.wait(s_ac, n - 3)
            bank = ps[4 + u % 4][:, 0:W]
            last = pe.matmul(bank, oh[b], msg[b], start=True, stop=(g.d == 0))
            if g.d == 1:
                last = pe.matmul(bank, oh[b], rb[2], start=False, stop=True)
            last.then_inc(s_sm, 1)

        def sum_group(e, g):
            for u in range(U):
                sum_tile(e, g, u)

        def messages(eng, turn, turn_b, group):
            eng.loop(NT // 2, lambda i: turn(i, [Group(0, i, QUARTERS, o) for o in range(QUARTERS)]), last=True)
            for o in range(NT // 2 * QUARTERS, NG):
                g = Group(0, 0, QUARTERS, o)
                group(g, g.next(1 if o == NG - 1 else 0))
            eng.loop(NT // 2, lambda i: turn_b(i, [Group(1, i, QUARTERS, NG + o) for o in range(QUARTERS)]))
            for o in range(NG + NT // 2 * QUARTERS, 2 * NG):
                g = Group(1, 0, QUARTERS, o)
                group(g, g.next() if o < 2 * NG - 1 else None)

        with nc.Block() as block:
            @block.gpsimd
            def _(e):
                G.e = e
                e.wait_ge(s_ixf, 1)
                e.wait_ge(s_ed, 32)
                n = bin_edges(e, EC, slotd[0], ar(ADR[0], EC).bitcast(i32), ar(PAY[0], 2 * EC).bitcast(i32), 2, 0)
                e.sem_inc(s_scd, 1)
                e.wait_ge(s_ixb, 1)
                bin_edges(e, EC, slotd[1], ar(ADR[1], EC).bitcast(i32), ar(PAY[1], 2 * EC).bitcast(i32), 2, n)
                e.sem_inc(s_scd, 1)
                e.wait_ge(s_sl, 32)
                ones_of_rows = ar(28672, 15 * W).rearrange("p (j w) -> p j w", w=W)[:, :, C]
                nc.gpsimd.memset(ones_of_rows, 1.0).then_inc(s_st, 1)
                nc.gpsimd.memset(msg[15][:, C:W], 1.0).then_inc(s_st, 1)
                e.wait_ge(s_st, 2)
                index_group(e, Group(0, 0, QUARTERS, 0))
                all_four = lambda i, gs: [gather_group(e, g, g.next()) for g in gs]
                messages(G, all_four, all_four, lambda g, nxt: gather_group(e, g, nxt))

            @block.sync
            def _(e):
                S.e = e
                for j, k in enumerate(("src", "dst", "et")):
                    e.dma_start(ei[j], a[k]).then_inc(lde, 16)
                small_loads = ((cst[:, :], a["cst"]), (lncol[:, 0:2], a["ln1w"]), (lncol[:, 2:4], a["ln1b"]),
                               (lncol[:, 4:6], a["ln2w"]), (lncol[:, 6:8], a["ln2b"]), (b1col, a["mb1"]),
                               (bxcol, a["bx"]))
                for o, i in small_loads:
                    e.dma_start(o, i).then_inc(ld, 16)
                for c in range(2):
                    cs = slice(c * P, (c + 1) * P)
                    e.dma_start(WX[:, c * C:(c + 1) * C], a["Wx"][cs, :]).then_inc(ldf, 16)
                    e.dma_start(WOT[:, c * C:(c + 1) * C], a["WoT"][cs, :]).then_inc(ldf, 16)
                    e.dma_start(ar(WM_off + c * 768 + 512, C), a["WxT"][cs, :]).then_inc(ldf, 16)
                e.wait_ge(zbd, 3)
                for j in range(4):
                    o = slice(j * HD, (j + 1) * HD)
                    for m, k in ((BD, "WqT"), (BDk, "WkT"), (BDv, "Wv")):
                        e.dma_start(m[o, o], a[k]).then_inc(ldb, 16)
                e.wait_ge(s_em, 1)
                for d in range(2):
                    e.dma_start(slotd[d].rearrange("(p t) two -> p (t two)", p=P),
                                empty.bitcast(i32)).then_inc(s_ed, 16)
                e.dma_start(X1[:, :].rearrange("p (t c) -> p t c", c=C),
                            a["x"].rearrange("(t p) c -> p t c", p=P)).then_inc(ldx, 16)
                for c in range(2):
                    e.dma_start(ar(W_off + c * 4096, 4096), a["Wf"][c * P:(c + 1) * P, :]).then_inc(ldw, 16)
                e.wait_ge(s_ixf, 1)
                for j, k in enumerate(("bxrow", "bo", "mb2")):
                    e.dma_start(raw_rows[:, 512 + j * C:512 + (j + 1) * C],
                                a[k].broadcast_to([96, C])).then_inc(ldr, 16)
                pair = lambda i: [store_rows(0, i * 2 + u) for u in range(2)]
                S.loop(7, pair)
                e.wait_ge(s_gm, 1)
                e.dma_start(gmapd[0], gmap_s.bitcast(i32)).then_inc(s_gd, 16)
                e.wait_ge(s_gd, 16)
                e.wait_ge(s_ixb, 2)
                e.dma_start(gmapd[1], gmap_row.bitcast(i32)).then_inc(s_gd, 16)
                for c in range(2):
                    e.dma_start(ar(W_off + 8192 + c * 4096, 4096), a["Wb"][c * P:(c + 1) * P, :]).then_inc(s_wb, 16)
                    e.dma_start(ar(W1T_off + c * HID, HID), a["mW1T"][c * P:(c + 1) * P, :]).then_inc(s_wb, 16)
                    e.dma_start(lw[:, c * C:(c + 1) * C], a["lw"][c * P:(c + 1) * P, :]).then_inc(s_wb, 16)
                for j in range(8):
                    e.dma_start(ar(W2T_off + j * C, C), a["mW2T"][j * P:(j + 1) * P, :]).then_inc(s_wb, 16)
                S.loop(NT // 2, pair, start=7)

                def second(i):
                    for u in range(2):
                        t = i * 2 + u
                        store_rows(1, t)
                        e.wait_ge(s_mrow, t + 1)
                        e.dma_start(mixd[ds(t * P, P), :], mst).then_inc(s_mdma, 16)
                S.loop(NT // 2, second)
                e.wait_ge(s_mdma, 16 * NT)
                for d in range(2):
                    for h in range(2):
                        e.wait_ge(s_td[d][h], 16 * NT)
                e.wait_ge(s_gd, 32)
                S.barrier(s_bar, 1)
                e.wait_ge(s_scd, 1)

                def slots_in(d):
                    e.dma_start(slots[d].bitcast(i32),
                                slotd[d].rearrange("(p t) two -> p (t two)", p=P)).then_inc((s_sl, s_slb)[d], 16)
                    e.dma_start(gmapi[d], gmapd[d]).then_inc((s_sl, s_slb)[d], 16)
                slots_in(0)

                def mix_in(t, i, u):
                    S.wait(s_kv, t - NB + 1)
                    e.dma_start(kin[u], mixd[ds(t * P, P), 0:514]).then_inc(s_ki[u], 16)
                in_fours(S, mix_in)
                S.barrier(s_bar, 2)

                def q_in(t, i, u):
                    S.wait(s_qt, t - NB + 1)
                    e.dma_start(qin[u], mixd[ds(t * P, P), 514:770]).then_inc(s_qi[u], 16)
                in_fours(S, q_in)
                S.barrier(s_bar, 3)
                for j, k in enumerate(("self_b", "fwd_b", "bwd_b")):
                    e.dma_start(rb[j][:, 0:C], a[k].broadcast_to([P, C])).then_inc(s_bi, 16)
                e.wait_ge(s_scd, 2)
                slots_in(1)
                e.wait_ge(s_slb, 32)
                e.wait_ge(s_bi, 48)

            @block.vector
            def _(e):
                V.e = e
                for m in (BD, BDk, BDv):
                    vec.memset(m, 0.0).then_inc(zbd, 1)
                V.link(vec.memset(empty, 0.0))
                vec.memset(empty.rearrange("p (t two) -> p t two", two=2)[:, :, 1], 999.0).then_inc(s_em, 1)
                e.wait_ge(ld, 7 * 16)
                e.wait_ge(lde, 48)
                bin_edges_of(0)
                e.sem_inc(s_ixf, 1)
                V.link(vec.tensor_copy(row_sel[:, :], cst[0:96, C_ROW:C_ROW + 1].broadcast_to([96, P])))
                e.wait_ge(folded, 1)
                vec.tensor_copy(Pm[:, :], ps[4][:, :]).then_inc(s_pmo, 1)
                e.wait_ge(ldx, 16)
                norm_stats(X1, mean, rstd, sv1, sq1)

                def normalise(t, i, u):
                    norm_apply(xn[:, ds(t * C, C)], t, X1, mean, rstd).then_inc(s_xn, 1)
                in_fours(V, normalise)
                for c in range(2):
                    V.link(vec.tensor_copy(ar(WM_off + c * 768, 512), ps[1 + c][:, :]))
                e.wait_ge(ldr, 3 * 16)
                V.link(vec.tensor_copy(raw_rows[:, 0:512], ps[3][0:96, :]))
                three_parts([(brow, 0, 768), (rows_o, 768, C), (rows_2, 1024, C)], raw_rows, part_rows)
                e.wait_ge(s_xn, NT)
                fwd_gmap(gmap_s).then_inc(s_gm, 1)
                bin_edges_of(1)
                e.sem_inc(s_ixb, 1)
                V.link(fwd_gmap(gmap_row))
                e.sem_inc(s_ixb, 1)
                norm_stats(xn, mean2, rstd2, sv2, sq2)
                V.link(vec.memset(kmax[:, :], -3.0e38))
                V.link(vec.memset(mst[:, C + P:C + P + 1], 1.0))
                V.link(vec.memset(mst[:, 513:514], 1.0))
                s_xs, s_tp, s_xT, _, _, s_done = pass_sems[1]

                def load_tile(t, u):
                    V.wait(s_tp, t - 1)
                    V.link(norm_apply(zs[u], t, xn, mean2, rstd2))
                    ts(xs[u], xn[:, ds(t * C, C)], 1.0, ALU.mult).then_inc(s_xs, 1)

                def transposes_out(t, u):
                    e.wait_ge(s_tp, t + 1)
                    V.wait(s_done, t - 1)
                    V.link(vec.tensor_copy(xT[u], ps[0][:, 0:C]))
                    for k in range(2):
                        V.link(ts(zT[u][:, k * P:(k + 1) * P], ps[0][:, C + k * P:C + (k + 1) * P],
                                  lncol[:, k:k + 1], ALU.mult, lncol[:, 2 + k:3 + k], ALU.add))
                    e.sem_inc(s_xT, 1)

                def mix_rows(t):
                    e.wait_ge(s_mm, t + 1)
                    V.link(vec.scalar_tensor_tensor(X1[:, ds(t * C, C)], ps[3][:, 0:C], 2.0,
                                                    X1[:, ds(t * C, C)], ALU.mult, ALU.add))
                    V.wait(s_mdma, 16 * t)
                    V.link(vec.tensor_tensor(kmax[:, :], kmax[:, :], ps[1][:, 0:C], ALU.max))
                    V.link(vec.tensor_copy(mst[:, 0:C], ps[1][:, 0:C]))
                    V.link(vec.tensor_copy(mst[:, C:514].rearrange("p (k c) -> p k c", k=2)[:, :, 0:P],
                                           ps[2][:, 0:C].rearrange("p (k c) -> p k c", k=2)))
                    qv = ps[1][:, C:2 * C].rearrange("p (h s) -> p h s", s=HD)
                    qxv = qx.rearrange("p (h s) -> p h s", s=HD)
                    V.link(vec.tensor_reduce(rmax, qv, AX.X, ALU.max))
                    vec.tensor_tensor(qxv, qv, rmax.unsqueeze(2).broadcast_to([P, HEADS, HD]),
                                      ALU.subtract).then_inc(s_q, 1)
                    e.wait_ge(s_qe, t + 1)
                    V.link(vec.tensor_reduce(rsum, qxv, AX.X, ALU.add))
                    V.link(vec.reciprocal(rsum, rsum))
                    vec.tensor_tensor(mst[:, 514:770].rearrange("p (h s) -> p h s", s=HD), qxv,
                                      rsum.unsqueeze(2).broadcast_to([P, HEADS, HD]),
                                      ALU.mult).then_inc(s_mrow, 1)

                e.wait_ge(pass_sems[0][5], NT)
                load_tile(0, 0)
                load_tile(1, 1)
                transposes_out(0, 0)

                def second(t, i, u):
                    if has(t, 1):
                        transposes_out(t + 1, 1 - u)
                    if has(t, 2):
                        load_tile(t + 2, u)
                    mix_rows(t)
                tiles(V, second)
                V.barrier(s_bar, 1)

                e.wait_ge(s_k1, 1)
                V.link(vec.tensor_reduce(kmT, ps[0][:, 0:C].rearrange("p (c n) -> p c n", c=2), AX.X, ALU.max))
                for c in range(2):
                    ts(dg, ident, kmT[:, c:c + 1], ALU.mult).then_inc(s_k2, 1)
                    e.wait_ge(s_k3, c + 1)
                V.link(vec.tensor_copy(kmb, ps[1][:, 0:C]))

                def keys(t, i, u):
                    V.wait(s_km, t - NB + 1)
                    e.wait_ge(s_ki[u], 16 * (i + 1))
                    vec.tensor_tensor(km[u], kin[u][:, 0:C], kmb, ALU.subtract).then_inc(s_ks, 1)
                    ts(kx[u], kin[u][:, C:514], cst[:, ds(C_VALID + t, 1)], ALU.mult).then_inc(s_kv, 1)
                    zero_sums(0, t)
                in_fours(V, keys)
                e.wait_ge(s_km, NT)
                V.link(vec.memset(KX, 0.0))
                for c in range(2):
                    V.link(vec.reciprocal(den[:, c:c + 1], ps[2 + c][:, P:P + 1]))
                    for j in range(4):
                        o = slice(j * HD, (j + 1) * HD)
                        V.link(vec.tensor_scalar(KX[o, c * P + j * HD:c * P + (j + 1) * HD], ps[2 + c][o, o],
                                                 den[o, c:c + 1], None, ALU.mult))
                e.sem_inc(s_kd, 1)
                e.wait_ge(s_k4, 1)
                vec.tensor_copy(KXT, ps[4][:, 0:C]).then_inc(s_kd, 1)
                e.wait_ge(s_k4, 2)
                V.link(vec.tensor_copy(M, ps[5][:, :]))
                V.barrier(s_bar, 2)

                def attn(t, i, u):
                    e.wait_ge(s_at, t + 1)
                    vec.tensor_tensor(hall[:, ds(t * C, C)], ps[4 + u][:, 0:C], xn[:, ds(t * C, C)],
                                      ALU.add).then_inc(s_h, 1)
                    e.wait_ge(s_h, t + 1)
                    V.settle()
                    tile_stats(hall, t)
                in_fours(V, attn)
                V.barrier(s_bar, 3)
                norm_stats(None, mean, rstd, sv3, sq3)
                ts(mean2, mean, -1.0, ALU.mult).then_inc(s_nm, 1)
                vec.memset(rb[2][:, C:C + 1], 0.0).then_inc(s_bi0, 1)
                e.wait_ge(s_sl, 32)

                def turn(i, gs):
                    for g in gs[:2]:
                        add_sums(e, g)
                    for g in gs[2:]:
                        add_sums(e, g)
                    e.wait_ge(s_m2, 2 * i + 2)
                    pair = X1[:, ds(i * 2 * C, 2 * C)]
                    V.link(vec.tensor_tensor(pair, pair, ps[3][:, :], ALU.add))
                    vec.tensor_tensor(pair, pair, hall[:, ds(i * 2 * C, 2 * C)], ALU.add).then_inc(s_ad, 1)
                def group(g, nxt):
                    add_sums(e, g)

                def degrees(d):
                    deg = ar(ACC[d], NT * W).rearrange("p (t c) -> p t c", c=W)[:, :, C]
                    V.link(ts(winv, deg, 1.0, ALU.max))
                    V.link(vec.reciprocal(winv, winv))
                    if d == 0:
                        V.link(ts(whas, deg, 1.0, ALU.min))

                def finish(d, ts_):
                    for t in ts_:
                        xt = X1[:, ds(t * C, C)]
                        V.mark(vec.scalar_tensor_tensor(xt, ar(ACC[d], NT * W)[:, ds(t * W, C)],
                                                        winv[:, ds(t, 1)], xt, ALU.mult, ALU.add))
                    V.join()
                    if d == 0:
                        for t in ts_:
                            xt = X1[:, ds(t * C, C)]
                            V.mark(vec.scalar_tensor_tensor(xt, rb[1], whas[:, ds(t, 1)], xt, ALU.mult, ALU.add))
                        V.join()
                        for t in ts_:
                            xt = X1[:, ds(t * C, C)]
                            V.mark(vec.tensor_tensor(xt, xt, rb[0], ALU.add))
                        V.join()

                def turn_b(i, gs):
                    for g in gs:
                        group(g, g.next())
                    finish(0, (2 * i, 2 * i + 1))

                def last_forward(g, nxt):
                    group(g, nxt)
                    if nxt is not None and nxt.d != g.d:
                        e.wait_ge(s_z1, NT)
                        e.wait_ge(s_slb, 32)
                        e.wait_ge(s_ac, TE)
                        e.wait_ge(s_ad, NT // 2)
                        e.wait_ge(s_bi, 48)
                        degrees(0)
                messages(V, turn, turn_b, last_forward)
                e.wait_ge(s_ac, 2 * TE)
                degrees(1)
                norm_stats(X1, mean, rstd, sv4, sq4, before=lambda pair: finish(1, pair))

            @block.scalar
            def _(e):
                A.e = e
                norm_root(sv1, sq1)
                s_xs, s_tp, s_xT, _, _, s_done = pass_sems[0]

                def load_tile(t, u):
                    e.wait_ge(s_xn, t + 1)
                    A.wait(s_tp, t - 1)
                    A.settle()
                    act.activation(xs[u], xn[:, ds(t * C, C)], ACT.Copy).then_inc(s_xs, 1)

                def transposes_out(t, u):
                    e.wait_ge(s_tp, t + 1)
                    A.wait(s_done, t - 1)
                    act.activation(xT[u], ps[0][:, 0:C], ACT.Copy).then_inc(s_xT, 1)

                e.wait_ge(s_ed, 32)
                load_tile(0, 0)
                load_tile(1, 1)
                transposes_out(0, 0)

                def first(t, i, u):
                    for c in range(8):
                        evacuate(0, t, c)
                        if c == 3:
                            if has(t, 1):
                                transposes_out(t + 1, 1 - u)
                            if has(t, 2):
                                load_tile(t + 2, u)
                tiles(A, first)
                norm_root(sv2, sq2)

                def second(t, i, u):
                    for c in range(8):
                        evacuate(1, t, c)
                        if c == 3:
                            e.wait_ge(s_q, t + 1)
                            act.activation(qx, qx, ACT.Exp).then_inc(s_qe, 1)
                tiles(A, second)
                A.barrier(s_bar, 1)

                def keys(t, i, u):
                    e.wait_ge(s_ks, t + 1)
                    act.activation(km[u], km[u], ACT.Exp).then_inc(s_ke, 1)
                in_fours(A, keys)
                A.barrier(s_bar, 2)

                def attn(t, i, u):
                    e.wait_ge(s_qt, t + 1)
                    A.wait(s_at, t - NB + 1)
                    act.activation(qT[u], ps[u][:, 0:C], ACT.Copy).then_inc(s_qc, 1)
                in_fours(A, attn)
                A.barrier(s_bar, 3)
                norm_root(sv3, sq3)

                def normalise_pair(i):
                    A.wait(s_zt, i)
                    A.settle()
                    for u in range(2):
                        t = i * 2 + u
                        act.activation(z2[u], hall[:, ds(t * C, C)], ACT.Identity,
                                       bias=mean2[:, ds(t, 1)]).then_inc(s_zm, 1)
                    e.wait_ge(s_zm, 2 * i + 2)
                    A.settle()
                    for u in range(2):
                        t = i * 2 + u
                        act.activation(z2[u], z2[u], ACT.Copy, scale=rstd[:, ds(t, 1)]).then_inc(s_z, 1)

                def z_out(i):
                    e.wait_ge(s_zt, i + 1)
                    A.wait(s_m1, 8 * i)
                    for k in range(2):
                        last = act.activation(z2T[:, k * C:(k + 1) * C], ps[0][:, k * C:(k + 1) * C], ACT.Identity,
                                              scale=lncol[:, 4 + k:5 + k], bias=lncol[:, 6 + k:7 + k])
                        A.mark(last)
                    A.join()
                    e.sem_inc(s_zc, 1)

                def gelu(i, js):
                    for j in js:
                        e.wait_ge(s_m1, 8 * i + j + 1)
                        act.activation(hT[:, j * C:(j + 1) * C], ps[1 + j % 2][:, 0:C], ACT.Gelu,
                                       bias=b1col[:, j:j + 1]).then_inc(s_ge, 1)

                def turn(i, gs):
                    onehots(gs[1])
                    A.wait(s_m2, 2 * i)
                    gelu(i, range(4))
                    onehots(gs[2])
                    gelu(i, range(4, 8))
                    if has(2 * i, 2):
                        normalise_pair(i + 1)
                    onehots(gs[3])
                    for u in range(2):
                        zero_sums(1, 2 * i + u)
                    onehots(gs[3].next())
                    if has(2 * i, 2):
                        z_out(i + 1)
                e.wait_ge(s_sl, 32)
                onehots(Group(0, 0, QUARTERS, 0))
                e.wait_ge(s_nm, 1)
                normalise_pair(0)
                z_out(0)
                messages(A, turn, lambda i, gs: [onehots(g.next()) for g in gs],
                         lambda g, nxt: nxt is not None and onehots(nxt))
                norm_root(sv4, sq4)

            @block.tensor
            def _(e):
                T.e = e
                e.wait_ge(ld, 7 * 16)
                e.wait_ge(ldf, 6 * 16)
                e.wait_ge(ldb, 12 * 16)
                for i in range(2):
                    for m, bd in enumerate((BDk, BD)):
                        for c in range(2):
                            pe.matmul(ps[1 + i][:, m * C + c * P:m * C + (c + 1) * P],
                                      WX[:, c * C + i * P:c * C + (i + 1) * P], bd, start=True, stop=True)
                for m, bd in enumerate((BDk, BD)):
                    for c in range(2):
                        pe.matmul(ps[3][0:96, m * C + c * P:m * C + (c + 1) * P],
                                  bxcol[:, c:c + 1].broadcast_to([P, 96]), bd, start=True, stop=True)
                for c in range(2):
                    last = pe.matmul(ps[4][:, c * C:(c + 1) * C], BDv, WOT[:, c * C:(c + 1) * C],
                                     start=True, stop=True)
                last.then_inc(folded, 1)
                bin_counts(NT, sc[0], stt[0], ps[0])

                def transpose_tile(d, t, u):
                    s_xs, s_tp, s_xT = pass_sems[d][0:3]
                    e.wait_ge(s_xs, t + 1)
                    T.wait(s_xT, t)
                    for k in range(2):
                        last = pe.transpose(ps[0][:, k * P:(k + 1) * P], xs[u][:, k * P:(k + 1) * P], ident)
                    if d == 1:
                        for k in range(2):
                            last = pe.transpose(ps[0][:, C + k * P:C + (k + 1) * P],
                                                zs[u][:, k * P:(k + 1) * P], ident)
                    last.then_inc(s_tp, 1)

                def first(t, i, u):
                    if has(t, 1):
                        transpose_tile(0, t + 1, 1 - u)
                    e.wait_ge(pass_sems[0][2], t + 1)
                    project(0, t, u)

                e.wait_ge(ldw, 32)
                e.wait_ge(s_pmo, 1)
                transpose_tile(0, 0, 0)
                tiles(T, first, 4, lambda: bin_counts(NT, sc[1], stt[1], ps[3]))
                e.wait_ge(s_wb, 14 * 16)
                transpose_tile(1, 0, 0)

                def second(t, i, u):
                    e.wait_ge(pass_sems[1][2], t + 1)
                    T.wait(s_mrow, t)
                    for k in range(2):
                        lz = zT[u][:, k * P:(k + 1) * P]
                        wm = WM_off + k * 768
                        pe.matmul(ps[1][:, :], lz, ar(wm, 512), start=(k == 0), stop=False)
                        pe.matmul(ps[2][:, 0:C], lz, ar(wm + 512, C), start=(k == 0), stop=False)
                        pe.matmul(ps[3][:, 0:C], xT[u][:, k * P:(k + 1) * P], lw[:, k * C:(k + 1) * C],
                                  start=(k == 0), stop=(k == 1))
                    pe.matmul(ps[1][:, :], row_sel[:, :], brow[:, 0:512], start=False, stop=True)
                    pe.matmul(ps[2][:, 0:C], row_sel[:, :], brow[:, 512:768], start=False,
                              stop=True).then_inc(s_mm, 1)
                    if has(t, 1):
                        transpose_tile(1, t + 1, 1 - u)
                    project(1, t, u)
                tiles(T, second)
                T.barrier(s_bar, 1)

                for c in range(2):
                    last = pe.transpose(ps[0][:, c * P:(c + 1) * P], kmax[:, c * P:(c + 1) * P], ident)
                last.then_inc(s_k1, 1)
                for c in range(2):
                    e.wait_ge(s_k2, c + 1)
                    pe.matmul(ps[1][:, c * P:(c + 1) * P], ones, dg, start=True, stop=True).then_inc(s_k3, 1)

                def keys(t, i, u):
                    e.wait_ge(s_ke, t + 1)
                    e.wait_ge(s_kv, t + 1)
                    for c in range(2):
                        last = pe.matmul(ps[2 + c][:, 0:P + 1], km[u][:, c * P:(c + 1) * P],
                                         kx[u][:, c * 129:(c + 1) * 129],
                                         start=isinstance(t, int) and t == 0,
                                         stop=isinstance(t, int) and t == NT - 1)
                    last.then_inc(s_km, 1)
                in_fours(T, keys)
                e.wait_ge(s_kd, 1)
                for c in range(2):
                    last = pe.transpose(ps[4][:, c * P:(c + 1) * P], KX[:, c * P:(c + 1) * P], ident)
                last.then_inc(s_k4, 1)
                e.wait_ge(s_kd, 2)
                for c in range(2):
                    last = pe.matmul(ps[5][:, c * C:(c + 1) * C], KXT[:, c * P:(c + 1) * P],
                                     Pm[:, c * C:(c + 1) * C], start=True, stop=True)
                last.then_inc(s_k4, 1)
                T.barrier(s_bar, 2)

                def transpose_q(t, i, u):
                    e.wait_ge(s_qi[u], 16 * (i + 1))
                    T.wait(s_qc, t - NB + 1)
                    for c in range(2):
                        last = pe.transpose(ps[u][:, c * P:(c + 1) * P], qin[u][:, c * P:(c + 1) * P], ident)
                    last.then_inc(s_qt, 1)

                def attn(t, i, u):
                    if has(t, 2):
                        transpose_q(t + 2, i + (u + 2) // NB, (u + 2) % NB)
                    e.wait_ge(s_qc, t + 1)
                    T.wait(s_h, t - NB + 1)
                    for c in range(2):
                        pe.matmul(ps[4 + u][:, 0:C], qT[u][:, c * P:(c + 1) * P], M[:, c * C:(c + 1) * C],
                                  start=(c == 0), stop=False)
                    pe.matmul(ps[4 + u][:, 0:C], row_sel[:, :], rows_o[:, :], start=False,
                              stop=True).then_inc(s_at, 1)
                for t in range(2):
                    transpose_q(t, 0, t)
                in_fours(T, attn)
                T.barrier(s_bar, 3)

                def z_transpose(i):
                    e.wait_ge(s_z, 2 * i + 2)
                    T.wait(s_zc, i)
                    for k in range(2):
                        for u in range(2):
                            last = pe.transpose(ps[0][:, k * C + u * P:k * C + (u + 1) * P],
                                                z2[u][:, k * P:(k + 1) * P], ident)
                    last.then_inc(s_zt, 1)

                def turn(i, gs):
                    for n in range(2 * U):
                        sum_tile(e, gs[n // U], n % U)
                        if n % 2 == 0:
                            continue
                        j = n // 2
                        if j == 0:
                            e.wait_ge(s_zc, i + 1)
                        T.wait(s_ge, 8 * i + j - 1)
                        for k in range(2):
                            w1 = ar(W1T_off + k * HID + j * P, P)
                            last = pe.matmul(ps[1 + j % 2][:, 0:C], w1, z2T[:, k * C:(k + 1) * C],
                                             start=(k == 0), stop=(k == 1))
                        last.then_inc(s_m1, 1)
                    for n in range(2 * U):
                        sum_tile(e, gs[2 + n // U], n % U)
                        if n == 0:
                            e.wait_ge(s_ge, 8 * i + 8)
                            T.wait(s_ad, i)
                        u, j = n // 8, n % 8
                        bank = ps[3][:, u * C:(u + 1) * C]
                        pe.matmul(bank, hT[:, j * C + u * P:j * C + (u + 1) * P], ar(W2T_off + j * C, C),
                                  start=(j == 0), stop=False)
                        if j == 7:
                            pe.matmul(bank, row_sel[:, :], rows_2[:, :], start=False, stop=True).then_inc(s_m2, 1)
                        if n == U and has(2 * i, 2):
                            z_transpose(i + 1)
                z_transpose(0)
                messages(T, turn, lambda i, gs: [sum_group(e, g) for g in gs], lambda g, nxt: sum_group(e, g))

        end_of_block()
        WE1, WE2 = 0, 16384
        lgt = work[:, 2640:2640 + NT * NX]
        xk = [work[:, j * 512:j * 512 + C] for j in range(NB)]
        xkT = [work[:, j * 512 + C:(j + 1) * 512] for j in range(NB)]
        so[0] = 0
        st, mean, rstd, mean2, rstd2, v1, v2, v3 = (sm(n) for n in (NT * 6,) + (NT,) * 7)
        cnt, tot, til, base, incl, ends = (sm(NT) for _ in range(6))
        wgt = sm(2 * NT)
        gsel = sm(2 * NX * 2)
        key52, pos52, place52, tile52 = (sm(2 * NT) for _ in range(4))
        wr = sm(2 * NX)
        br = sm(NX)
        L = NT * NX
        lg2, eq, oh1 = work[:, 1536:1536 + L], work[:, 1744:1744 + L], work[:, 1952:1952 + L]
        gx, gxi = work[:, 2160:2160 + TX], sm(TX, 1).bitcast(i32)
        tA = work[:, 2324:2376].bitcast(i32)
        pos_i = work[:, 2428:2480].bitcast(i32)
        xsl = work[:, 2480:2480 + TX].bitcast(i32)
        sv5, sq5 = sem("var"), sem("root")
        s_w, s_wx, s_xk, s_xt, s_xc, s_lg, s_le = (sem(n) for n in
            ("small_in", "experts_in", "token_tile", "token_T", "token_T_out", "logits", "logits_out"))
        s_xo, s_xf, s_xr = sem("token_rows"), sem("token_norm"), sem("x_norm")
        s_c5, s_t5, s_d, s_dw = sem("counts"), sem("totals"), sem("difference"), sem("ratio")
        s_o5, s_q5, s_m5 = sem("place_onehots"), sem("tile_onehots"), sem("slot_mm")
        ohr = [xn[:, 2048 + j * P:2048 + (j + 1) * P] for j in range(NB)]
        ohq = [work[:, 0:NT * TX], xn[:, 2560:2560 + NT * TX]]
        b1e, b2e = xn[0:96, 4608:5120].bitcast(bf16), xn[0:96, 5120:5248].bitcast(bf16)
        braw, bpart = xn[0:96, 0:1280], xn[0:96, 1280:1920].bitcast(bf16)
        s_be, s_bz = sem("expert_biases"), sem("zeroed")
        hit5, run5 = xk[0].bitcast(bf16), work[:, 768:768 + 2 * NT * NX]
        with nc.Block() as block:
            @block.sync
            def _(e):
                S.e = e
                for c in range(2):
                    e.dma_start(wr[:, c * NX:(c + 1) * NX], a["Wr"][c * P:(c + 1) * P, :]).then_inc(s_w, 16)
                e.dma_start(br, a["br"].broadcast_to([P, NX])).then_inc(s_w, 16)
                e.dma_start(gsel[:, 0:2 * NX], a["lng"]).then_inc(s_w, 16)
                e.dma_start(gsel[:, 2 * NX:4 * NX], a["lnb"]).then_inc(s_w, 16)
                for x in range(NX):
                    for k in range(2):
                        e.dma_start(ar(WE1 + k * 8192 + x * HID, HID),
                                    a["W1"][x * C + k * P:x * C + (k + 1) * P, :]).then_inc(s_wx, 16)
                    e.dma_start(ar(WE2 + x * 2048, 2048).rearrange("p (j c) -> p j c", c=C),
                                a["W2"][x * HID:(x + 1) * HID, :].rearrange("(j p) c -> p j c", p=P)
                                ).then_inc(s_wx, 16)


                def token_rows(t, i, u):
                    e.wait_ge(s_xf, t + 1)
                    e.dma_start(xtok[ds(t * P, P), :], xn[:, ds(t * C, C)]).then_inc(s_xo, 16)
                in_fours(S, token_rows)
                e.wait_ge(s_bz, 1)
                for j in range(3):
                    o = slice(32 * j, 32 * j + NX)
                    e.dma_start(xn[o, 0:HID], a["b1"]).then_inc(s_be, 16)
                    e.dma_start(xn[o, HID:HID + C], a["b2"]).then_inc(s_be, 16)
                e.wait_ge(s_be, 96)
                e.wait_ge(s_w, 5 * 16)
                e.wait_ge(s_wx, 24 * 16)

            @block.vector
            def _(e):
                V.e = e
                def normalise(t, i, u):
                    norm_apply(xn[:, ds(t * C, C)], t, X1, mean, rstd).then_inc(s_xr, 1)
                in_fours(V, normalise)
                e.wait_ge(s_xr, NT)
                norm_stats(xn, mean2, rstd2, sv5, sq5)

                def tokens(t, i, u):
                    e.wait_ge(s_xk, t + 1)
                    norm_apply(xn[:, ds(t * C, C)], t, xn, mean2, rstd2).then_inc(s_xf, 1)
                in_fours(V, tokens)
                e.wait_ge(s_le, NT)
                lg3 = lgt.rearrange("p (t e) -> p t e", e=NX)
                l23, e3, o3 = (x.rearrange("p (t e) -> p t e", e=NX) for x in (lg2, eq, oh1))
                io = iota[:, 0:NX].unsqueeze(1).broadcast_to([P, NT, NX])

                def spread(v):
                    return v.unsqueeze(2).broadcast_to([P, NT, NX])
                e.wait_ge(s_w, 5 * 16)
                V.link(vec.tensor_tensor(lg3, lg3, br.unsqueeze(1).broadcast_to([P, NT, NX]), ALU.add))

                def first_max(src, top, idx):
                    V.link(vec.tensor_reduce(top, src, AX.X, ALU.max))
                    V.link(vec.tensor_tensor(e3, src, spread(top), ALU.not_equal))
                    V.link(vec.scalar_tensor_tensor(e3, e3, 100.0, io, ALU.mult, ALU.add))
                    V.link(vec.tensor_reduce(idx, e3, AX.X, ALU.min))
                first_max(lg3, v1, key52[:, 0:NT])
                V.link(vec.tensor_tensor(o3, io, spread(key52[:, 0:NT]), ALU.is_equal))
                V.link(vec.scalar_tensor_tensor(l23, o3, -1.0e30, lg3, ALU.mult, ALU.add))
                first_max(l23, v2, key52[:, NT:2 * NT])
                vec.tensor_tensor(v2, v2, v1, ALU.subtract).then_inc(s_d, 1)
                e.wait_ge(s_dw, 1)
                V.link(ts(v1, v3, 1.0, ALU.add))
                V.link(vec.reciprocal(wgt[:, 0:NT], v1))
                V.link(vec.tensor_tensor(wgt[:, NT:2 * NT], wgt[:, 0:NT], v3, ALU.mult))
                vd = cst[:, C_VALID:C_VALID + NT]
                for j in range(2):
                    k_ = key52[:, j * NT:(j + 1) * NT]
                    V.link(ts(k_, k_, -float(NX), ALU.add))
                    V.link(vec.tensor_tensor(k_, k_, vd, ALU.mult))
                    V.link(ts(k_, k_, float(NX), ALU.add))
                bin_positions(key52, 2 * NT, NX, pos52, [(0, NX, hit5, run5)], s_c5, s_t5, ps[0])
                V.link(vec.tensor_copy(pos_i, pos52))
                V.link(vec.tensor_single_scalar(tA, pos_i, P - 1, op=ALU.bitwise_and))
                V.link(vec.tensor_copy(place52, tA))
                V.link(vec.tensor_single_scalar(tA, pos_i, 7, op=ALU.arith_shift_right))
                V.link(vec.tensor_copy(tile52, tA))
                for j in range(2):
                    q_ = tile52[:, j * NT:(j + 1) * NT]
                    V.link(ts(q_, q_, 1.0, ALU.add))
                    V.link(vec.tensor_tensor(q_, q_, vd, ALU.mult))
                    V.link(ts(q_, q_, -1.0, ALU.add))
                e.wait_ge(s_xo, 16 * NT)
                vec.memset(braw, 0.0).then_inc(s_bz, 1)

                for j in range(2):
                    o3 = ohq[j].rearrange("p (t q) -> p t q", q=TX)
                    V.link(vec.tensor_tensor(o3, iota[:, 0:TX].unsqueeze(1).broadcast_to([P, NT, TX]),
                                             tile52[:, j * NT:(j + 1) * NT].unsqueeze(2).broadcast_to(
                                                 [P, NT, TX]), ALU.is_equal))
                    V.link(vec.tensor_tensor(o3, o3, cst[:, C_TOK:C_TOK + NT].unsqueeze(2).broadcast_to(
                        [P, NT, TX]), ALU.mult))
                e.sem_inc(s_q5, 1)

                def place(t, i, u):
                    for j in range(2):
                        b = 2 * (u % 2) + j
                        V.wait(s_m5, 2 * t + j - 3)
                        c = t + j * NT
                        ts(ohr[b], iota, place52[:, ds(c, 1)], ALU.is_equal).then_inc(s_o5, 1)
                in_fours(V, place)
                bins_of_tiles(gx, NX, TX, P)
                V.link(vec.tensor_copy(gxi[0:1, :], gx[0:1, :]))
                e.wait_ge(s_m5, 2 * NT)
                V.link(vec.tensor_copy(xsl, ps[1][:, 0:TX]))
                e.wait_ge(s_be, 96)
                three_parts([(xn[0:96, 4608:5248].bitcast(bf16), 0, HID + C)], braw, bpart)

            @block.scalar
            def _(e):
                A.e = e
                def copy_tile(t, u):
                    e.wait_ge(s_xr, t + 1)
                    A.wait(s_xt, t - NB + 1)
                    A.settle()
                    act.activation(xk[u], xn[:, ds(t * C, C)], ACT.Copy).then_inc(s_xk, 1)

                def tokens(t, i, u):
                    if has(t, 2):
                        copy_tile(t + 2, (u + 2) % NB)
                    e.wait_ge(s_xt, t + 1)
                    A.wait(s_lg, t - NB + 1)
                    act.activation(xkT[u], ps[u][:, 0:C], ACT.Copy).then_inc(s_xc, 1)
                    if not (isinstance(t, int) and t == 0):
                        logits_out(t - 1, (u - 1) % NB)

                def logits_out(t, u):
                    e.wait_ge(s_lg, t + 1)
                    A.settle()
                    act.activation(lgt[:, ds(t * NX, NX)], ps[4 + u][:, 0:NX], ACT.Copy).then_inc(s_le, 1)
                for t in range(2):
                    copy_tile(t, t)
                in_fours(A, tokens, 3, lambda: norm_root(sv5, sq5))
                logits_out(NT - 1, (NT - 1) % NB)
                e.wait_ge(s_d, 1)
                act.activation(v3, v2, ACT.Exp).then_inc(s_dw, 1)

            @block.tensor
            def _(e):
                T.e = e
                e.wait_ge(s_w, 5 * 16)

                def transpose_tile(t, u):
                    e.wait_ge(s_xk, t + 1)
                    T.wait(s_xc, t - NB + 1)
                    for k in range(2):
                        last = pe.transpose(ps[u][:, k * P:(k + 1) * P], xk[u][:, k * P:(k + 1) * P], ident)
                    last.then_inc(s_xt, 1)

                def tokens(t, i, u):
                    if has(t, 1):
                        transpose_tile(t + 1, (u + 1) % NB)
                    e.wait_ge(s_xc, t + 1)
                    T.wait(s_le, t - NB + 1)
                    for k in range(2):
                        last = pe.matmul(ps[4 + u][:, 0:NX], xkT[u][:, k * P:(k + 1) * P],
                                  wr[:, k * NX:(k + 1) * NX], start=(k == 0), stop=(k == 1))
                    last.then_inc(s_lg, 1)
                transpose_tile(0, 0)
                in_fours(T, tokens)
                bin_counts(NX, s_c5, s_t5, ps[0])

                def place(t, i, u):
                    for j in range(2):
                        b = 2 * (u % 2) + j
                        e.wait_ge(s_o5, 2 * t + j + 1)
                        pe.matmul(ps[1][:, 0:TX], ohr[b], ohq[j][:, ds(t * TX, TX)],
                                  start=isinstance(t, int) and t + j == 0,
                                  stop=isinstance(t, int) and t + j == NT).then_inc(s_m5, 1)
                e.wait_ge(s_q5, 1)
                in_fours(T, place)

        end_of_block()
        xk = [work[:, j * 768:j * 768 + C] for j in range(2)]
        xkT = [work[:, j * 768 + C:j * 768 + 2 * C] for j in range(2)]
        xg = [work[:, j * 768 + 2 * C:(j + 1) * 768] for j in range(2)]
        xT7 = xk
        sel1 = [xkT[u][0:96, 0:64].bitcast(bf16) for u in range(2)]
        sel2 = [xkT[u][0:96, 64:128].bitcast(bf16) for u in range(2)]
        XB = xn[:, 0:4608]
        hb = [XB[:, j * HID:(j + 1) * HID] for j in range(2)]
        hTb = [XB[:, 2048 + j * HID:2048 + (j + 1) * HID] for j in range(2)]
        yb = [XB[:, 4096 + j * C:4096 + (j + 1) * C] for j in range(2)]
        ist7 = [sb(f"ist7{u}", 1, i32) for u in range(2)]
        s_g7 = sems("token_gather", 2)
        s_i7, s_t7, s_x7, s_h7, s_e7, s_r7, s_c7, s_y7, s_o7 = (sem(n) for n in
            ("index", "x_T", "x_T_out", "layer1", "gelu", "hidden_T", "hidden_T_out", "layer2", "y_out"))
        s_yd = sems("y_dma", 2)

        def in_pairs(eng, step):
            def body(i):
                for c in (1, 2):
                    step(2 * i + c, i, c)
            eng.loop(TX // 2 - 1, body)
            step(TX - 1, TX // 2 - 1, 1)

        with nc.Block() as block:
            @block.gpsimd
            def _(e):
                G.e = e

                def body(i):
                    for u in range(2):
                        t = i * 2 + u
                        G.wait(s_t7, t - 1)
                        G.settle()
                        nc.gpsimd.tensor_copy(ist7[u][:, :], xsl[:, ds(t, 1)]).then_inc(s_i7, 1)
                        e.wait_ge(s_i7, t + 1)
                        G.settle()
                        e.indirect_dma_start(xg[u], None, xtok, bass.IndirectOffsetOnAxis(
                            ap=ist7[u][:, 0:1], axis=0)).then_inc(s_g7[u], 16)
                G.loop(TX // 2, body)

            @block.vector
            def _(e):
                V.e = e

                def pick(dst, t):
                    return ts(dst, gx[0:96, ds(t, 1)].broadcast_to([96, P]), cst[0:96, C_PID:C_PID + 1],
                              ALU.is_equal)

                def x_out(t, u):
                    V.settle()
                    x = e.value_load(gxi[0:1, ds(t, 1)], min_val=0, max_val=NX - 1)
                    V.wait(s_h7, 2 * t - 2)
                    V.link(pick(sel1[u], t))
                    e.wait_ge(s_t7, t + 1)
                    for k in range(2):
                        last = ts(xT7[u][:, k * P:(k + 1) * P], ps[0][:, k * P:(k + 1) * P],
                                  gsel[:, ds(x + k * NX, 1)], ALU.mult, gsel[:, ds(x + (2 + k) * NX, 1)], ALU.add)
                        if k == 0:
                            V.link(last)
                    last.then_inc(s_x7, 1)

                def h_out(t, u):
                    V.wait(s_y7, t - 1)
                    V.link(pick(sel2[u], t))
                    e.wait_ge(s_r7, t + 1)
                    for k in range(2):
                        vec.tensor_copy(hTb[u][:, k * 512:(k + 1) * 512], ps[3 + k][:, :]).then_inc(s_c7, 1)

                def y_out(t, i, u):
                    e.wait_ge(s_y7, t + 1)
                    V.wait(s_yd[u], 16 * i)
                    vec.tensor_copy(yb[u], ps[5 + u][:, 0:C]).then_inc(s_o7, 1)

                x_out(0, 0)
                x_out(1, 1)

                def step(t, i, c):
                    h_out(t - 1, (c - 1) % 2)
                    if not (isinstance(t, int) and t == TX - 1):
                        x_out(t + 1, (c + 1) % 2)
                    y_out(t - 1, i, (c - 1) % 2)
                in_pairs(V, step)
                h_out(TX - 1, 1)
                y_out(TX - 1, TX // 2 - 1, 1)

            @block.scalar
            def _(e):
                A.e = e

                def body(i):
                    for u in range(2):
                        t = i * 2 + u
                        A.wait(s_r7, t - 1)
                        for c in range(2):
                            e.wait_ge(s_h7, 2 * t + c + 1)
                            act.activation(hb[u][:, c * 512:(c + 1) * 512], ps[1 + c][:, :],
                                           ACT.Gelu).then_inc(s_e7, 1)
                A.loop(TX // 2, body)

            @block.tensor
            def _(e):
                T.e = e

                def expert(t):
                    T.settle()
                    return e.value_load(gxi[0:1, ds(t, 1)], min_val=0, max_val=NX - 1)

                def x_transpose(t, i, u):
                    T.wait(s_x7, t)
                    e.wait_ge(s_g7[u], 16 * (i + 1))
                    for k in range(2):
                        last = pe.transpose(ps[0][:, k * P:(k + 1) * P], xg[u][:, k * P:(k + 1) * P], ident)
                    last.then_inc(s_t7, 1)

                def layer1(t, u):
                    x = expert(t)
                    e.wait_ge(s_x7, t + 1)
                    T.wait(s_e7, 2 * t)
                    for c in range(2):
                        for k in range(2):
                            pe.matmul(ps[1 + c][:, :], xT7[u][:, k * P:(k + 1) * P],
                                      arena[:, ds(x * HID + (WE1 + k * 8192 + c * 512), 512)],
                                      start=(k == 0), stop=False)
                        pe.matmul(ps[1 + c][:, :], sel1[u], b1e[:, c * 512:(c + 1) * 512],
                                  start=False, stop=True).then_inc(s_h7, 1)

                def h_transpose(t, u):
                    e.wait_ge(s_e7, 2 * t + 2)
                    T.wait(s_c7, 2 * t)
                    for j in range(8):
                        last = pe.transpose(ps[3 + j // 4][:, (j % 4) * P:(j % 4 + 1) * P],
                                            hb[u][:, j * P:(j + 1) * P], ident)
                    last.then_inc(s_r7, 1)

                def layer2(t, u):
                    x = expert(t)
                    e.wait_ge(s_c7, 2 * t + 2)
                    T.wait(s_o7, t - 1)
                    for j in range(8):
                        pe.matmul(ps[5 + u][:, 0:C], hTb[u][:, j * P:(j + 1) * P],
                                  arena[:, ds(x * 2048 + (WE2 + j * C), C)], start=(j == 0), stop=False)
                    pe.matmul(ps[5 + u][:, 0:C], sel2[u], b2e, start=False, stop=True).then_inc(s_y7, 1)

                x_transpose(0, 0, 0)
                x_transpose(1, 0, 1)
                layer1(0, 0)

                def step(t, i, c):
                    h_transpose(t - 1, (c - 1) % 2)
                    if not (isinstance(t, int) and t == TX - 1):
                        x_transpose(t + 1, i + (c + 1) // 2, (c + 1) % 2)
                    layer1(t, c % 2)
                    layer2(t - 1, (c - 1) % 2)
                in_pairs(T, step)
                h_transpose(TX - 1, 1)
                layer2(TX - 1, 1)

            @block.sync
            def _(e):
                S.e = e

                def body(i):
                    for u in range(2):
                        t = i * 2 + u
                        e.wait_ge(s_o7, t + 1)
                        e.dma_start(yslot[ds(t * P, P), :], yb[u]).then_inc(s_yd[u], 16)
                S.loop(TX // 2, body)
                for u in range(2):
                    e.wait_ge(s_yd[u], 16 * TX // 2)

        end_of_block()
        pk = [[[XB[:, (4 * h + 2 * j + u) * C:(4 * h + 2 * j + u + 1) * C] for u in range(2)]
               for j in range(2)] for h in range(2)]
        s_i8, s_w8 = sem("index"), sem("pair_added")
        s_g8 = [sems(f"pick{h}", 4) for h in range(2)]
        ist8 = [sb(f"ist8{h}", 4, i32) for h in range(2)]
        s_od = sems("out", 2)

        def pairs(eng, step):
            def body(i):
                for h in range(2):
                    step(2 * i + h, i, h)
            eng.loop(NT // 4, body)
            step(NT // 2 - 1, NT // 4, 0)

        with nc.Block() as block:
            @block.gpsimd
            def _(e):
                G.e = e

                def pick(n, i, h):
                    G.wait(s_w8, n - 1)
                    G.settle()
                    both = "p (j t) -> p j t"
                    nc.gpsimd.tensor_copy(ist8[h].rearrange(both, j=2),
                                          pos_i.rearrange(both, j=2)[:, :, ds(2 * n, 2)]).then_inc(s_i8, 1)
                    e.wait_ge(s_i8, n + 1)
                    G.settle()
                    for j in range(2):
                        for u in range(2):
                            e.indirect_dma_start(pk[h][j][u], None, yslot, bass.IndirectOffsetOnAxis(
                                ap=ist8[h][:, 2 * j + u:2 * j + u + 1], axis=0)).then_inc(s_g8[h][2 * j + u], 16)
                pairs(G, pick)

            @block.vector
            def _(e):
                V.e = e

                def combine(n, i, h):
                    for j in range(2):
                        for u in range(2):
                            t = 2 * n + u
                            xt_ = X1[:, ds(t * C, C)]
                            e.wait_ge(s_g8[h][2 * j + u], 16 * (i + 1))
                            V.mark(vec.scalar_tensor_tensor(xt_, pk[h][j][u], wgt[:, ds(t + j * NT, 1)], xt_,
                                                            ALU.mult, ALU.add))
                        V.join()
                    e.sem_inc(s_w8, 1)
                pairs(V, combine)

            @block.sync
            def _(e):
                S.e = e

                def rows(n, i, h):
                    e.wait_ge(s_w8, n + 1)
                    e.dma_start(out[ds(n * 2 * P, 2 * P), :].rearrange("(t p) c -> p t c", p=P),
                                X1[:, ds(n * 2 * C, 2 * C)].rearrange("p (t c) -> p t c", c=C)
                                ).then_inc(s_od[h], 16)
                pairs(S, rows)
                e.wait_ge(s_od[0], 16 * (NT // 4 + 1))
                e.wait_ge(s_od[1], 16 * (NT // 4))


def kernel(**inputs):
    import numpy as np
    import concourse.bacc as bacc
    from concourse.bass_utils import run_bass_kernel_spmd as run

    g = {k: np.asarray(v) for k, v in inputs.items()}
    cols = lambda v: np.ascontiguousarray(v.reshape(-1, P).T)
    row = lambda v: v.reshape(1, -1)
    edge = lambda v, fill: np.concatenate([v, np.full(P * EC - E, fill, v.dtype)]).reshape(P, EC)
    x = g["x"]
    arrays = {
        "cst": constants(np),
        "x": np.concatenate([x, x[:NP - N]]),
        "src": edge(g["src"], N + P - 1), "dst": edge(g["dst"], N + P - 1), "et": edge(g["edge_type_16"], 0),
        "Wf": g["L0_gnn_Wf"].transpose(1, 0, 2).reshape(C, R * C),
        "Wb": g["L0_gnn_Wb"].transpose(1, 0, 2).reshape(C, R * C),
        "lw": g["L0_gnn_loop_weight"], "fwd_b": row(g["L0_gnn_forward_bias"]),
        "bwd_b": row(g["L0_gnn_backward_bias"]), "self_b": row(g["L0_gnn_self_bias"]),
        "ln1w": cols(g["L0_mix_ln1_w"]), "ln1b": cols(g["L0_mix_ln1_b"]),
        "ln2w": cols(g["L0_mix_ln2_w"]), "ln2b": cols(g["L0_mix_ln2_b"]),
        "Wx": g["L0_mix_Wx"], "WxT": g["L0_mix_Wx"].T, "bx": cols(g["L0_mix_bx"]), "bxrow": row(g["L0_mix_bx"]),
        "WqT": g["L0_mix_Wq"].T, "WkT": g["L0_mix_Wk"].T, "Wv": g["L0_mix_Wv"], "WoT": g["L0_mix_Wo"].T,
        "bo": row(g["L0_mix_bo"]), "mW1T": g["L0_mix_W1"].T, "mb1": cols(g["L0_mix_b1"]),
        "mW2T": g["L0_mix_W2"].T, "mb2": row(g["L0_mix_b2"]),
        "Wr": g["L0_ffn_Wr"], "br": row(g["L0_ffn_br"]),
        "lng": g["L0_ffn_ln_g"].reshape(NX, 2, P).transpose(2, 1, 0).reshape(P, 2 * NX),
        "lnb": g["L0_ffn_ln_b"].reshape(NX, 2, P).transpose(2, 1, 0).reshape(P, 2 * NX),
        "W1": g["L0_ffn_W1"].reshape(NX * C, HID), "b1": g["L0_ffn_b1"],
        "W2": g["L0_ffn_W2"].reshape(NX * HID, C), "b2": g["L0_ffn_b2"],
    }
    arrays = {f"in_{k}": np.ascontiguousarray(v) for k, v in arrays.items()}
    nc = bacc.Bacc("TRN2", target_bir_lowering=False, num_devices=1)
    a = {k[3:]: nc.dram_tensor(k, v.shape, mybir.dt.from_np(v.dtype), kind="ExternalInput").ap()
         for k, v in arrays.items()}
    out = nc.dram_tensor("out", (NP, C), f32, kind="ExternalOutput").ap()
    build(nc, a, out)
    return run(nc, [arrays], core_ids=[0]).results[0]["out"][:N]
```
